# Optimizing a Trainium2 kernel written in Bass

```python
import numpy as np
import jax
import jax.numpy as jnp

def _softmax(x, axis=-1):
    return jax.nn.softmax(x, axis=axis)

def _gelu(x):
    return jax.nn.gelu(x, approximate=True)

def _silu(x):
    return jax.nn.silu(x)

def _sigmoid(x):
    return jax.nn.sigmoid(x)

def _layernorm(x, axis=-1, eps=1e-05):
    m = jnp.mean(x, axis=axis, keepdims=True)
    v = jnp.var(x, axis=axis, keepdims=True)
    return (x - m) / jnp.sqrt(v + eps)

def _scatter_add(tgt, idx, src, axis=0):
    return tgt.at[idx].add(src)

def _segment_sum(src, seg, n):
    return jax.ops.segment_sum(src, seg, n)
kernel_name = 'mk_seq_postln_d2_jaxref_r8_2ad373'

def setup_inputs(seed: int=0):
    np.random.seed(seed)
    _w = jnp.asarray

    def _L0_attn_setup():
        import jax, jax.numpy as jnp
        import numpy as np
        D_MODEL = 256
        N_HEADS = 16
        HEAD_DIM = D_MODEL // N_HEADS
        B, T = (2, 256)
        key = jax.random.key(seed)
        ks = jax.random.split(key, 9)
        s = 0.02
        x = jax.random.normal(ks[0], (B, T, D_MODEL), dtype=jnp.float32)
        Wq = jax.random.normal(ks[1], (N_HEADS, D_MODEL, HEAD_DIM), dtype=jnp.float32) * s
        bq = jax.random.normal(ks[2], (N_HEADS, HEAD_DIM), dtype=jnp.float32) * s
        Wk = jax.random.normal(ks[3], (N_HEADS, D_MODEL, HEAD_DIM), dtype=jnp.float32) * s
        bk = jax.random.normal(ks[4], (N_HEADS, HEAD_DIM), dtype=jnp.float32) * s
        Wv = jax.random.normal(ks[5], (N_HEADS, D_MODEL, HEAD_DIM), dtype=jnp.float32) * s
        bv = jax.random.normal(ks[6], (N_HEADS, HEAD_DIM), dtype=jnp.float32) * s
        Wo = jax.random.normal(ks[7], (D_MODEL, D_MODEL), dtype=jnp.float32) * s
        bo = jax.random.normal(ks[8], (D_MODEL,), dtype=jnp.float32) * s
        return {'x': x, 'Wq': Wq, 'bq': bq, 'Wk': Wk, 'bk': bk, 'Wv': Wv, 'bv': bv, 'Wo': Wo, 'bo': bo}
    _L0_attn_in = _L0_attn_setup()

    def _L0_ffn_setup():
        import jax, jax.numpy as jnp
        import numpy as np
        H = 256
        I = 128
        E = 8
        TOP_K = 2
        IS = 512
        B, S = (2, 256)

        def _moe_forward(hidden_states, w_router, wg, wu, wd, sw_gate, sw_up, sw_down, gate_w):
            b, s, h = hidden_states.shape
            x = hidden_states.reshape(-1, h)
            t = x.shape[0]
            shared = jax.nn.silu(x @ sw_gate.T) * (x @ sw_up.T) @ sw_down.T
            logits = x @ w_router.T
            probs = jax.nn.softmax(logits.astype(jnp.float32), axis=-1)
            top_v, top_i = jax.lax.top_k(probs, TOP_K)
            top_v = top_v / jnp.sum(top_v, axis=-1, keepdims=True)
            top_v = top_v.astype(probs.dtype)
            combine = jnp.zeros((t, probs.shape[-1]), x.dtype).at[jnp.arange(t)[:, None], top_i].add(top_v)
            g = jax.nn.silu(jnp.einsum('th,eih->tei', x, wg))
            u = jnp.einsum('th,eih->tei', x, wu)
            y = jnp.einsum('tei,ehi->teh', g * u, wd)
            expert_out = jnp.einsum('teh,te->th', y, combine)
            shared = jax.nn.sigmoid(x @ gate_w.T) * shared
            out = expert_out + shared
            return out.reshape(b, s, h)
        key = jax.random.key(seed)
        ks = jax.random.split(key, 10)
        sc_h = 1.0 / np.sqrt(H)
        sc_i = 1.0 / np.sqrt(I)
        sc_is = 1.0 / np.sqrt(IS)
        return {'hidden_states': jax.random.normal(ks[0], (B, S, H), jnp.float32), 'w_router': jax.random.normal(ks[1], (E, H), jnp.float32) * sc_h, 'wg': jax.random.normal(ks[2], (E, I, H), jnp.float32) * sc_h, 'wu': jax.random.normal(ks[3], (E, I, H), jnp.float32) * sc_h, 'wd': jax.random.normal(ks[4], (E, H, I), jnp.float32) * sc_i, 'sw_gate': jax.random.normal(ks[5], (IS, H), jnp.float32) * sc_h, 'sw_up': jax.random.normal(ks[6], (IS, H), jnp.float32) * sc_h, 'sw_down': jax.random.normal(ks[7], (H, IS), jnp.float32) * sc_is, 'gate_w': jax.random.normal(ks[8], (1, H), jnp.float32) * sc_h}
    _L0_ffn_in = _L0_ffn_setup()

    def _L1_attn_setup():
        import jax, jax.numpy as jnp
        import numpy as np
        import math
        B, T, DIM, NH = (2, 256, 256, 16)
        HD = DIM // NH

        def rotate_half(x):
            h = x.shape[-1] // 2
            return jnp.concatenate([-x[..., h:], x[..., :h]], axis=-1)

        def rope_tables(t_len, rot_dim, base=10000.0, dtype=jnp.float32):
            inv_freq = 1.0 / base ** (jnp.arange(0, rot_dim, 2, dtype=dtype) / rot_dim)
            t = jnp.arange(t_len, dtype=dtype)
            ang = jnp.einsum('i,j->ij', t, inv_freq)
            return (jnp.sin(ang), jnp.cos(ang))

        def apply_rope(q, k, sin, cos):
            h = q.shape[-1] // 2
            q1, q2 = (q[..., :h], q[..., h:])
            k1, k2 = (k[..., :h], k[..., h:])
            sin = sin[None, None]
            cos = cos[None, None]
            q1r = q1 * cos + rotate_half(q1) * sin
            k1r = k1 * cos + rotate_half(k1) * sin
            return (jnp.concatenate([q1r, q2], axis=-1), jnp.concatenate([k1r, k2], axis=-1))
        key = jax.random.key(seed)
        ks = jax.random.split(key, 5)
        s = 1.0 / math.sqrt(DIM)
        return {'x': jax.random.normal(ks[0], (B, T, DIM), jnp.float32), 'wq': jax.random.normal(ks[1], (DIM, DIM), jnp.float32) * s, 'wk': jax.random.normal(ks[2], (DIM, DIM), jnp.float32) * s, 'wv': jax.random.normal(ks[3], (DIM, DIM), jnp.float32) * s, 'wo': jax.random.normal(ks[4], (DIM, DIM), jnp.float32) * s}
    _L1_attn_in = _L1_attn_setup()

    def _L1_ffn_setup():
        import jax, jax.numpy as jnp
        import numpy as np
        B, T, D, E, H = (4, 256, 256, 4, 1024)
        TOPK = 2
        CAPACITY_FACTOR = 1
        key = jax.random.key(seed)
        k0, k1, k2, k3 = jax.random.split(key, 4)
        x = jax.random.normal(k0, (B, T, D), dtype=jnp.float32)
        Wg = jax.random.normal(k1, (D, E), dtype=jnp.float32) * 0.02
        bg = jnp.zeros((E,), dtype=jnp.float32)
        W1 = jax.random.normal(k2, (E, D, H), dtype=jnp.float32) * (1.0 / np.sqrt(D))
        W2 = jax.random.normal(k3, (E, H, D), dtype=jnp.float32) * (1.0 / np.sqrt(H))
        return {'x': x, 'Wg': Wg, 'bg': bg, 'W1': W1, 'W2': W2}
    _L1_ffn_in = _L1_ffn_setup()
    _d = {'L0_attn_x': _L0_attn_in['x'], 'L0_attn_Wq': _L0_attn_in['Wq'], 'L0_attn_bq': _L0_attn_in['bq'], 'L0_attn_Wk': _L0_attn_in['Wk'], 'L0_attn_bk': _L0_attn_in['bk'], 'L0_attn_Wv': _L0_attn_in['Wv'], 'L0_attn_bv': _L0_attn_in['bv'], 'L0_attn_Wo': _L0_attn_in['Wo'], 'L0_attn_bo': _L0_attn_in['bo'], 'L0_ffn_w_router': _L0_ffn_in['w_router'], 'L0_ffn_wg': _L0_ffn_in['wg'], 'L0_ffn_wu': _L0_ffn_in['wu'], 'L0_ffn_wd': _L0_ffn_in['wd'], 'L0_ffn_sw_gate': _L0_ffn_in['sw_gate'], 'L0_ffn_sw_up': _L0_ffn_in['sw_up'], 'L0_ffn_sw_down': _L0_ffn_in['sw_down'], 'L0_ffn_gate_w': _L0_ffn_in['gate_w'], 'L1_attn_wq': _L1_attn_in['wq'], 'L1_attn_wk': _L1_attn_in['wk'], 'L1_attn_wv': _L1_attn_in['wv'], 'L1_attn_wo': _L1_attn_in['wo'], 'L1_ffn_Wg': _L1_ffn_in['Wg'], 'L1_ffn_bg': _L1_ffn_in['bg'], 'L1_ffn_W1': _L1_ffn_in['W1'], 'L1_ffn_W2': _L1_ffn_in['W2']}
    _x0 = _d['L0_attn_x']
    _d['L0_attn_x'] = jax.random.normal(jax.random.fold_in(jax.random.key(seed), 1), (1, 1024, 256), dtype=_x0.dtype)
    del _x0
    return _d

def reference(L0_attn_x, L0_attn_Wq, L0_attn_bq, L0_attn_Wk, L0_attn_bk, L0_attn_Wv, L0_attn_bv, L0_attn_Wo, L0_attn_bo, L0_ffn_w_router, L0_ffn_wg, L0_ffn_wu, L0_ffn_wd, L0_ffn_sw_gate, L0_ffn_sw_up, L0_ffn_sw_down, L0_ffn_gate_w, L1_attn_wq, L1_attn_wk, L1_attn_wv, L1_attn_wo, L1_ffn_Wg, L1_ffn_bg, L1_ffn_W1, L1_ffn_W2):

    def _L0_attn_ref(x, Wq, bq, Wk, bk, Wv, bv, Wo, bo):
        import jax, jax.numpy as jnp
        import numpy as np
        D_MODEL = 256
        N_HEADS = 16
        HEAD_DIM = D_MODEL // N_HEADS
        B, T = (2, 256)
        Bn, Tn, C = x.shape
        H, _, D = Wq.shape
        scale = D ** (-0.5)
        q = jnp.einsum('btc,hcd->bhtd', x, Wq) + bq[None, :, None, :]
        k = jnp.einsum('btc,hcd->bhtd', x, Wk) + bk[None, :, None, :]
        v = jnp.einsum('btc,hcd->bhtd', x, Wv) + bv[None, :, None, :]
        scores = jnp.einsum('bhtd,bhsd->bhts', q, k) * scale
        neg = jnp.finfo(scores.dtype).min
        causal = jnp.triu(jnp.full((Tn, Tn), neg, dtype=scores.dtype), k=1)
        probs = jax.nn.softmax(scores + causal, axis=-1)
        y = jnp.einsum('bhts,bhsd->bhtd', probs, v)
        y = y.transpose(0, 2, 1, 3).reshape(Bn, Tn, H * D)
        return y @ Wo + bo

    def _L0_ffn_ref(hidden_states, w_router, wg, wu, wd, sw_gate, sw_up, sw_down, gate_w):
        import jax, jax.numpy as jnp
        import numpy as np
        H = 256
        I = 128
        E = 8
        TOP_K = 2
        IS = 512
        B, S = (2, 256)

        def _moe_forward(hidden_states, w_router, wg, wu, wd, sw_gate, sw_up, sw_down, gate_w):
            b, s, h = hidden_states.shape
            x = hidden_states.reshape(-1, h)
            t = x.shape[0]
            shared = jax.nn.silu(x @ sw_gate.T) * (x @ sw_up.T) @ sw_down.T
            logits = x @ w_router.T
            probs = jax.nn.softmax(logits.astype(jnp.float32), axis=-1)
            top_v, top_i = jax.lax.top_k(probs, TOP_K)
            top_v = top_v / jnp.sum(top_v, axis=-1, keepdims=True)
            top_v = top_v.astype(probs.dtype)
            combine = jnp.zeros((t, probs.shape[-1]), x.dtype).at[jnp.arange(t)[:, None], top_i].add(top_v)
            g = jax.nn.silu(jnp.einsum('th,eih->tei', x, wg))
            u = jnp.einsum('th,eih->tei', x, wu)
            y = jnp.einsum('tei,ehi->teh', g * u, wd)
            expert_out = jnp.einsum('teh,te->th', y, combine)
            shared = jax.nn.sigmoid(x @ gate_w.T) * shared
            out = expert_out + shared
            return out.reshape(b, s, h)
        return _moe_forward(hidden_states, w_router, wg, wu, wd, sw_gate, sw_up, sw_down, gate_w)

    def _L1_attn_ref(x, wq, wk, wv, wo):
        import jax, jax.numpy as jnp
        import numpy as np
        import math
        B, T, DIM, NH = (2, 256, 256, 16)
        HD = DIM // NH

        def rotate_half(x):
            h = x.shape[-1] // 2
            return jnp.concatenate([-x[..., h:], x[..., :h]], axis=-1)

        def rope_tables(t_len, rot_dim, base=10000.0, dtype=jnp.float32):
            inv_freq = 1.0 / base ** (jnp.arange(0, rot_dim, 2, dtype=dtype) / rot_dim)
            t = jnp.arange(t_len, dtype=dtype)
            ang = jnp.einsum('i,j->ij', t, inv_freq)
            return (jnp.sin(ang), jnp.cos(ang))

        def apply_rope(q, k, sin, cos):
            h = q.shape[-1] // 2
            q1, q2 = (q[..., :h], q[..., h:])
            k1, k2 = (k[..., :h], k[..., h:])
            sin = sin[None, None]
            cos = cos[None, None]
            q1r = q1 * cos + rotate_half(q1) * sin
            k1r = k1 * cos + rotate_half(k1) * sin
            return (jnp.concatenate([q1r, q2], axis=-1), jnp.concatenate([k1r, k2], axis=-1))
        b, t, c = x.shape

        def proj(w):
            return (x @ w.T).reshape(b, t, NH, HD).transpose(0, 2, 1, 3)
        q, k, v = (proj(wq), proj(wk), proj(wv))
        sin, cos = rope_tables(t, HD, dtype=x.dtype)
        q, k = apply_rope(q, k, sin, cos)
        att = jnp.einsum('bhqd,bhkd->bhqk', q, k) * (1.0 / math.sqrt(HD))
        att = jax.nn.softmax(att, axis=-1)
        y = jnp.einsum('bhqk,bhkd->bhqd', att, v)
        y = y.transpose(0, 2, 1, 3).reshape(b, t, c)
        return y @ wo.T

    def _L1_ffn_ref(x, Wg, bg, W1, W2):
        import jax, jax.numpy as jnp
        import numpy as np
        B, T, D, E, H = (4, 256, 256, 4, 1024)
        TOPK = 2
        CAPACITY_FACTOR = 1
        Bq, Tq, Dq = x.shape
        N = Bq * Tq
        capacity = int(N * CAPACITY_FACTOR / E)
        flat_x = x.reshape(N, Dq)
        logits = flat_x @ Wg + bg
        top_vals, top_idx = jax.lax.top_k(logits, TOPK)
        sparse = jnp.full_like(logits, -jnp.inf)
        sparse = sparse.at[jnp.arange(N)[:, None], top_idx].set(top_vals)
        probs = jax.nn.softmax(sparse, axis=-1)
        out = jnp.zeros_like(flat_x)
        for i in range(E):
            assigned = (top_idx == i).any(axis=-1)
            score = jnp.where(assigned, probs[:, i], -jnp.inf)
            sel_p, sel_idx = jax.lax.top_k(score, capacity)
            p = jnp.where(jnp.isfinite(sel_p), sel_p, 0.0)[:, None]
            tok = flat_x[sel_idx]
            h = jax.nn.gelu(tok @ W1[i], approximate=False)
            y = h @ W2[i] * p
            out = out.at[sel_idx].add(y)
        return out.reshape(Bq, Tq, Dq)
    x = L0_attn_x
    x = _layernorm(x + _L0_attn_ref(x, L0_attn_Wq, L0_attn_bq, L0_attn_Wk, L0_attn_bk, L0_attn_Wv, L0_attn_bv, L0_attn_Wo, L0_attn_bo), axis=-1)
    x = _layernorm(x + _L0_ffn_ref(x, L0_ffn_w_router, L0_ffn_wg, L0_ffn_wu, L0_ffn_wd, L0_ffn_sw_gate, L0_ffn_sw_up, L0_ffn_sw_down, L0_ffn_gate_w), axis=-1)
    x = _layernorm(x + _L1_attn_ref(x, L1_attn_wq, L1_attn_wk, L1_attn_wv, L1_attn_wo), axis=-1)
    x = _layernorm(x + _L1_ffn_ref(x, L1_ffn_Wg, L1_ffn_bg, L1_ffn_W1, L1_ffn_W2), axis=-1)
    return x

_drawn_inputs = setup_inputs


def setup_inputs(seed=0):
    import zlib

    import numpy as np

    out = dict(_drawn_inputs(seed))
    spreads = {'L1_ffn_bg': (0.0, 0.1)}
    factors = {'L0_attn_Wq': 4.817, 'L0_attn_bq': 8.0, 'L0_attn_Wk': 3.512, 'L0_attn_bk': 8.0}
    for name, (base, spread) in spreads.items():
        noise = np.random.default_rng([zlib.crc32(name.encode()), seed]).standard_normal(out[name].shape)
        drawn = base * np.exp(spread * noise) if base else spread * noise
        out[name] = jnp.asarray(drawn.astype(out[name].dtype))
    for name, factor in factors.items():
        out[name] = (out[name] * factor).astype(out[name].dtype)
    return out
```

```python
from contextlib import ExitStack

import numpy as np

import concourse.bass as bass
from concourse import mybir

F32 = mybir.dt.float32
F32R = mybir.dt.float32r
BF16 = mybir.dt.bfloat16
ALU = mybir.AluOpType
ACT = mybir.ActivationFunctionType
AX = mybir.AxisListType

P = 128
T = 1024
D = 256
H = 16
HD = D // H
NT = T // P
KD = D // P
HALF = 512
EPS = 1e-5
MASKED = -3.0e38

E0 = 8
I0 = 128
CH = E0 + 512 // I0
NR0 = E0 + 2
E1 = 4
H1 = 1024
CAP = T // E1
MT1 = H1 // P

C_ID, C_CM, C_CMT, C_T8, C_T4, C_IOTA, C_SLOT, C_TRI, C_END = 0, 128, 256, 384, 448, 464, 720, 722, 850

ROWS = 2 * 2 * HD
STACK = ROWS + 2


class Stage(ExitStack):

    def __init__(self, nc):
        super().__init__()
        self.nc, self.numbers = nc, []

    def semaphore(self, name):
        sem = self.enter_context(self.nc.semaphore(name))
        self.numbers.append(sem.num)
        return sem

    def __exit__(self, *exc):
        super().__exit__(*exc)
        if exc[0] is None:
            numbers = sorted(self.numbers)
            starts = [n for n in numbers if n - 1 not in numbers]
            ends = [n + 1 for n in numbers if n + 1 not in numbers]
            with self.nc.Block() as block:

                @block.sync
                def _(sp):
                    for start, end in zip(starts, ends):
                        sp.sem_clear(range(start, end))


def product(pe, out, lhs, rhs, first, last):
    (lh, ll), (rh, rl) = lhs, rhs
    pe.matmul(out, lh, rl, start=first, stop=False, skip_group_check=True)
    pe.matmul(out, ll, rh, start=False, stop=False, skip_group_check=True)
    return pe.matmul(out, lh, rh, start=False, stop=last, skip_group_check=True)


def load_and_split(nc, mem, dram):
    with Stage(nc) as ctx:
        sem = lambda name: ctx.semaphore(name)
        x_raw = ctx.enter_context(nc.sbuf_tensor("x_raw", [P, KD, T], F32))
        w_raw = ctx.enter_context(nc.sbuf_tensor("w_raw", [P, 10, KD * D], F32))
        consts_in, x_in, w_in = sem("consts_in"), sem("x_in"), [sem("w0_in"), sem("w1_in")]
        rest_in = sem("rest_in")
        x_high, w_high, low_done, preset = sem("x_high"), sem("w_high"), sem("low_done"), sem("preset")
        block = ctx.enter_context(nc.Block())

        @block.sync
        def _(sp):
            sp.dma_start(x_raw[:, :, :], dram["x_t"]).then_inc(x_in, 16)
            sp.dma_start(w_raw[:, 0:4, :], dram["w_attn"][:, 0:4, :]).then_inc(w_in[0], 16)
            sp.dma_start(mem["consts"][:, :], dram["consts"]).then_inc(consts_in, 16)
            sp.dma_start(mem["bias_qk"][:, :], dram["bias_qk"]).then_inc(rest_in, 16)
            sp.dma_start(mem["bias_v"][:, :], dram["bias_v"].broadcast_to([P, D])).then_inc(rest_in, 16)
            sp.dma_start(mem["bias_o"][:, :], dram["bias_o"].broadcast_to([P, D])).then_inc(rest_in, 16)
            sp.dma_start(mem["bias_g"][:, :], dram["bias_g"].broadcast_to([P, E1])).then_inc(rest_in, 16)
            sp.dma_start(w_raw[:, 4:10, :], dram["w_attn"][:, 4:10, :]).then_inc(w_in[1], 16)
            sp.dma_start(mem["x"][:, :, :], dram["x_tok"]).then_inc(rest_in, 16)
            sp.dma_start(mem["rope"][:, :, :], dram["rope"]).then_inc(rest_in, 16)
            sp.wait_ge(rest_in, 16 * 6)

        @block.scalar
        def _(act):
            act.wait_ge(x_in, 16)
            act.activation(mem["xt_h"][:, :, :], x_raw[:, :, :], ACT.Copy).then_inc(x_high, 1)
            for n, (a, b) in enumerate(((0, 4), (4, 10))):
                act.wait_ge(w_in[n], 16)
                act.activation(mem["wa_h"][:, a:b, :], w_raw[:, a:b, :], ACT.Copy).then_inc(w_high, 1)

        @block.vector
        def _(dve):
            dve.memset(mem["v_ring"][:, :, :, :], 1.0).then_inc(preset, 1)
            dve.memset(mem["zeros"][:, :], 0.0).then_inc(preset, 1)
            dve.memset(mem["eps"][:, :], EPS).then_inc(preset, 1)
            dve.memset(mem["row_max"][:, :, :], MASKED).then_inc(preset, 1)
            dve.memset(mem["max_parts"][:, :].bitcast(F32), 0.0).then_inc(preset, 1)
            for j in range(4):
                dve.memset(mem["k_stack"][ROWS:STACK, j, :].bitcast(F32), 1.0).then_inc(preset, 1)
            dve.wait_ge(x_high, 1)
            dve.tensor_tensor(mem["xt_l"][:, :, :], x_raw[:, :, :], mem["xt_h"][:, :, :].bitcast(F32),
                              ALU.subtract).then_inc(low_done, 1)
            for n, (a, b) in enumerate(((0, 4), (4, 10))):
                dve.wait_ge(w_high, n + 1)
                dve.tensor_tensor(mem["wa_l"][:, a:b, :], w_raw[:, a:b, :], mem["wa_h"][:, a:b, :].bitcast(F32),
                                  ALU.subtract).then_inc(low_done, 1)
            dve.wait_ge(consts_in, 16)
            dve.tensor_copy(mem["masks"][:, :], mem["consts"][:, C_ID:C_T8]).then_inc(low_done, 1)


def attention(nc, mem, dram, layer):
    causal, rope = layer == 0, layer == 1
    ps, y = mem["ps"], mem["y"]
    qs, ks, vr = mem["q_stack"], mem["k_stack"], mem["v_ring"]
    scratch = {"q": dram["q_parts"], "k": dram["k_parts"]}
    units = [(t, m, n) for m in range(KD) for t in "qk" for n in range(2)]
    w_at = {"q": 4, "qp": 5, "k": 6, "kp": 7, "v": 8} if rope else {"q": 0, "k": 1, "v": 2}

    def pieces(qt):
        end = (qt + 1) * P if causal else T
        return [(a, min(a + HALF, end)) for a in range(0, end, HALF)]

    def piece_number(qt):
        return sum(len(pieces(t)) for t in range(qt))

    PIECES = piece_number(NT)

    with Stage(nc) as ctx:
        sem = lambda name: ctx.semaphore(f"{name}_{layer}")
        sb = lambda name, shape, dt=F32: ctx.enter_context(nc.sbuf_tensor(f"{name}_{layer}", shape, dt))
        flat = sb("flat", [P, 2, HALF])
        turned = sb("turned", [P, 2, HALF])
        parts = sb("parts", [P, 2, 2, T], F32R)
        v_all = sb("v_all", [P, NT, D])
        probs = sb("probs", [P, 2, T])
        max_rows = sb("max_rows", [P, 2, 32])
        negmax = sb("negmax", [P, NT])
        recip = sb("recip", [P, NT])

        unit_ready, unit_out, high_ready, low_ready = sem("unit_ready"), sem("unit_out"), sem("high_ready"), sem("low_ready")
        rope_step = sem("rope_step")
        v_ready, v_out = sem("v_ready"), sem("v_out")
        written = [sem(f"written{m}") for m in range(2 * KD)]
        loaded = [sem(f"loaded{j}") for j in range(4)]
        max_loaded = [sem(f"max_loaded{j}") for j in range(4)]
        scores_ready, scores_free, fin, max_ready = sem("scores_ready"), sem("scores_free"), sem("fin"), sem("max_ready")
        st_ready, exp_done = sem("st_ready"), sem("exp_done")
        pv_ready, pv_free, recip_ready = sem("pv_ready"), sem("pv_free"), sem("recip_ready")
        v_copied = sem("v_copied")
        block = ctx.enter_context(nc.Block())

        def bank(b, a=0, n=HALF):
            return ps[:, b * HALF + a:b * HALF + a + n]

        def pv(h2):
            return bank(6 + h2, 0, NT * (HD + 1)).rearrange("p (t c) -> p t c", c=HD + 1)

        @block.sync
        def _(sp):
            def write_parts(g):
                t, m, _ = units[2 * g]
                sp.wait_ge(low_ready, 2 * g + 2)
                sp.dma_start(scratch[t][m * P:(m + 1) * P, :, :], parts[:, g % 2, :, :].bitcast(F32)).then_inc(written[g], 16)

            def load_stacks(h, j):
                q = scratch["q"][bass.ds(h * HD, HD), :, :]
                k = scratch["k"][bass.ds(h * HD, HD), :, :].rearrange("d l t -> (d l) t")
                for part in range(2):
                    rows = slice(part * 2 * HD, (part + 1) * 2 * HD)
                    sp.dma_start(qs[rows, j, :].bitcast(F32), q[:, part:part + 1, :].broadcast_to([HD, 2, T])
                                 ).then_inc(loaded[j], 16)
                    sp.dma_start(ks[rows, j, :].bitcast(F32), k).then_inc(loaded[j], 16)
                sp.dma_start(qs[ROWS:STACK, j, :].bitcast(F32), mem["zeros"][0:2, :]).then_inc(loaded[j], 16)

            def load_max(h, j, count):
                sp.wait_ge(max_ready, count)
                for i in range(4):
                    dst = qs[ROWS:STACK, j, :].bitcast(F32).rearrange("l (t i c) -> l t i c", i=4, c=32)[:, :, i, :]
                    sp.dma_start(dst, max_rows[32 * i:32 * i + 2 * NT, j % 2, :]).then_inc(max_loaded[j], 16)

            write_parts(0)
            write_parts(1)
            sp.wait_ge(written[0], 16)
            sp.wait_ge(written[1], 16)
            for h in range(4):
                load_stacks(h, h)
            write_parts(2)
            write_parts(3)
            load_max(0, 0, 1)
            load_max(1, 1, 2)
            sp.wait_ge(written[2], 16)
            sp.wait_ge(written[3], 16)
            with sp.Fori(0, H // 4 - 1) as i:
                for j in range(4):
                    load_max(i * 4 + (j + 2), (j + 2) % 4, i * 4 + (j + 3))
                    sp.wait_ge(pv_ready, i * 4 + (j + 1))
                    load_stacks(i * 4 + (j + 4), j)
            load_max(H - 2, 2, H - 1)
            load_max(H - 1, 3, H)

        @block.tensor
        def _(pe):
            def unit(u):
                t, m, n = units[u]
                if u >= 2:
                    pe.wait_ge(unit_out, u - 1)
                cols = slice(n * HALF, (n + 1) * HALF)
                for r, name in enumerate([t, t + "p"][:1 + rope]):
                    for k in range(KD):
                        w = slice(k * D + m * P, k * D + (m + 1) * P)
                        mm = product(pe, bank(2 * (u % 2) + r),
                                     (mem["wa_h"][:, w_at[name], w], mem["wa_l"][:, w_at[name], w]),
                                     (mem["xt_h"][:, k, cols], mem["xt_l"][:, k, cols]), k == 0, k == KD - 1)
                mm.then_inc(unit_ready, 1)

            def project_v(t):
                if t >= 2:
                    pe.wait_ge(v_out, t - 1)
                for k in range(KD):
                    toks, w = slice(t * P, (t + 1) * P), slice(k * D, (k + 1) * D)
                    mm = product(pe, bank(4 + t % 2, 0, D), (mem["xt_h"][:, k, toks], mem["xt_l"][:, k, toks]),
                                 (mem["wa_h"][:, w_at["v"], w], mem["wa_l"][:, w_at["v"], w]), k == 0, k == KD - 1)
                mm.then_inc(v_ready, 1)

            def score_tile(h, j, qt, loads):
                if qt == 0:
                    pe.wait_ge(loaded[j], 80 * loads)
                for n, (a, b) in enumerate(pieces(qt)):
                    at = piece_number(qt) + n
                    pe.wait_ge(scores_free, h * PIECES + (at + 1))
                    diagonal = causal and b == (qt + 1) * P
                    mm = pe.matmul(bank(4 + at % 2, 0, b - a), qs[0:STACK, j, qt * P:(qt + 1) * P], ks[0:STACK, j, a:b],
                                   start=True, stop=True)
                    if diagonal:
                        mm = pe.matmul(bank(4 + at % 2, b - a - P, P), mem["masks"][:, C_ID:C_ID + P],
                                       mem["masks"][:, C_CM:C_CM + P], start=False, stop=True, skip_group_check=True)
                    mm.then_inc(scores_ready, 1)

            def transposed_scores(j, kt, loads):
                if kt == 0:
                    pe.wait_ge(max_loaded[j], 64 * loads)
                first = kt * P if causal else 0
                base = 2 * (kt % 2) * HALF
                for a, b in ((first, HALF), (max(first, HALF), T)):
                    if a >= b:
                        continue
                    diagonal = causal and a == first
                    mm = pe.matmul(ps[:, base + a:base + b], ks[0:STACK, j, kt * P:(kt + 1) * P], qs[0:STACK, j, a:b],
                                   start=True, stop=True)
                    if diagonal:
                        mm = pe.matmul(ps[:, base + a:base + a + P], mem["masks"][:, C_ID:C_ID + P],
                                       mem["masks"][:, C_CMT:C_CMT + P], start=False, stop=True, skip_group_check=True)
                mm.then_inc(st_ready, 1)

            def head(h, j, loads, max_next, ahead, next_head):
                for kt in range(NT):
                    pe.wait_ge(exp_done, h * NT + (kt + 1))
                    if kt == 0:
                        pe.wait_ge(pv_free, h + 1)
                        pe.wait_ge(v_copied, h + 1)
                    for qt in range(kt if causal else 0, NT):
                        mm = pe.matmul(pv(j % 2)[:, qt, :], probs[:, kt % 2, qt * P:(qt + 1) * P], vr[:, j, kt, :],
                                       start=(kt == 0 and qt == 0), stop=(kt == (qt if causal else NT - 1)),
                                       skip_group_check=True)
                    if kt == NT - 1:
                        mm.then_inc(pv_ready, 1)
                    if kt < NT - 2:
                        transposed_scores(j, kt + 2, loads)
                    elif next_head:
                        transposed_scores((j + 1) % 4, kt + 2 - NT, max_next)
                    if ahead is not None:
                        score_tile(h + 2, (j + 2) % 4, kt, ahead)

            for u in range(4):
                unit(u)
            for t in range(NT):
                project_v(t)
            for u in range(4, 8):
                unit(u)
            pe.wait_ge(v_out, NT)
            for h in range(2):
                for qt in range(NT):
                    score_tile(h, h, qt, 1)
            pe.wait_ge(unit_out, 8)
            transposed_scores(0, 0, 1)
            transposed_scores(0, 1, 1)
            with pe.Fori(0, H // 4 - 1) as i:
                for j in range(4):
                    head(i * 4 + j, j, i + 1, i + (1 + (j == 3)), i + (1 + (j >= 2)), True)
            for j in range(4):
                head(H - 4 + j, j, H // 4, H // 4, H // 4 if j < 2 else None, j < 3)

        @block.scalar
        def _(act):
            for u, (t, m, n) in enumerate(units):
                g = u // 2
                act.wait_ge(unit_out, u + 1)
                if g >= 2 and n == 0:
                    act.wait_ge(written[g - 2], 16)
                act.activation(parts[:, g % 2, 0, n * HALF:(n + 1) * HALF], flat[:, u % 2, :], ACT.Copy
                               ).then_inc(high_ready, 1)
            with act.Fori(0, H) as h:
                for kt in range(NT):
                    first = kt * P if causal else 0
                    base = 2 * (kt % 2) * HALF
                    act.wait_ge(st_ready, h * NT + (kt + 1))
                    act.activation(probs[:, kt % 2, first:T], ps[:, base + first:base + T], ACT.Exp
                                   ).then_inc(exp_done, 1)

        @block.gpsimd
        def _(pool):
            def copy_v(h, j):
                pool.tensor_copy(vr[:, j, :, 0:HD], v_all[:, :, bass.ds(h * HD, HD)]).then_inc(v_copied, 1)

            pool.wait_ge(v_out, NT)
            for h in range(4):
                copy_v(h, h)
            with pool.Fori(0, H // 4 - 1) as i:
                for j in range(4):
                    pool.wait_ge(pv_ready, i * 4 + (j + 1))
                    copy_v(i * 4 + (j + 4), j)

        @block.vector
        def _(dve):
            def unit_to_flat(u):
                t, m, n = units[u]
                dve.wait_ge(unit_ready, u + 1)
                src, dst = bank(2 * (u % 2)), flat[:, u % 2, :]
                scale = HD ** -0.5 if t == "q" else 1.0
                if not rope:
                    bias = mem["bias_qk"][:, 2 * (t == "k") + m:2 * (t == "k") + m + 1]
                    dve.tensor_scalar(dst, src, bias, scale, ALU.add, ALU.mult).then_inc(unit_out, 1)
                else:
                    cols = slice(n * HALF, (n + 1) * HALF)
                    dve.scalar_tensor_tensor(out=dst, in0=src, scalar=scale, in1=mem["rope"][:, 0, cols],
                                             op0=ALU.mult, op1=ALU.mult).then_inc(rope_step, 1)
                    dve.scalar_tensor_tensor(out=turned[:, u % 2, :], in0=bank(2 * (u % 2) + 1), scalar=scale,
                                             in1=mem["rope"][:, 1, cols], op0=ALU.mult, op1=ALU.mult
                                             ).then_inc(rope_step, 1)
                    dve.wait_ge(rope_step, 2 * u + 2)
                    dve.tensor_tensor(dst, dst, turned[:, u % 2, :], ALU.add).then_inc(unit_out, 1)
                dve.wait_ge(high_ready, u + 1)
                high = parts[:, (u // 2) % 2, 0, n * HALF:(n + 1) * HALF]
                dve.tensor_tensor(parts[:, (u // 2) % 2, 1, n * HALF:(n + 1) * HALF], dst, high.bitcast(F32),
                                  ALU.subtract).then_inc(low_ready, 1)

            def v_to_sbuf(t):
                dve.wait_ge(v_ready, t + 1)
                if rope:
                    ins = dve.tensor_copy(v_all[:, t, :], bank(4 + t % 2, 0, D))
                else:
                    ins = dve.tensor_tensor(v_all[:, t, :], bank(4 + t % 2, 0, D), mem["bias_v"][:, :], ALU.add)
                ins.then_inc(v_out, 1)

            def tile_max(h, qt):
                for n, (a, b) in enumerate(pieces(qt)):
                    at = piece_number(qt) + n
                    dve.wait_ge(scores_ready, h * PIECES + (at + 1))
                    dve.tensor_reduce(mem["row_max"][:, qt, n:n + 1], bank(4 + at % 2, 0, b - a), AX.X, ALU.max
                                      ).then_inc(scores_free, 1)

            def finish_max(h, j, loads):
                dve.wait_ge(scores_free, h * PIECES + (2 + PIECES))
                dve.tensor_reduce(negmax[:, :], mem["row_max"][:, :, :], AX.X, ALU.max, negate=True).then_inc(fin, 1)
                dve.wait_ge(fin, h * 3 + 1)
                dve.tensor_copy(mem["max_parts"][:, 0:NT], negmax[:, :]).then_inc(fin, 1)
                dve.wait_ge(fin, h * 3 + 2)
                dve.tensor_tensor(mem["max_parts"][:, NT:2 * NT], negmax[:, :], mem["max_parts"][:, 0:NT].bitcast(F32),
                                  ALU.subtract).then_inc(fin, 1)
                dve.wait_ge(fin, h * 3 + 3)
                if loads is not None:
                    dve.wait_ge(max_loaded[(j + 2) % 4], loads)
                dve.transpose(max_rows[:, j % 2, :], mem["max_parts"][:, :].bitcast(F32)).then_inc(max_ready, 1)

            def head_out(h, j):
                dve.wait_ge(pv_ready, h + 1)
                acc = pv(j % 2)
                dve.wait_ge(pv_free, h + 2)
                dve.reciprocal(recip[:, :], acc[:, :, HD]).then_inc(recip_ready, 1)
                dve.wait_ge(recip_ready, h + 1)
                dve.tensor_tensor(y[:, :, bass.ds(h * HD, HD)], acc[:, :, 0:HD],
                                  recip[:, :].unsqueeze(2).broadcast_to([P, NT, HD]), ALU.mult).then_inc(pv_free, 1)

            for u in range(4):
                unit_to_flat(u)
            for t in range(NT):
                v_to_sbuf(t)
            for u in range(4, 8):
                unit_to_flat(u)
            dve.memset(recip[:, :], 1.0).then_inc(scores_free, 2)
            dve.memset(negmax[:, :], 0.0).then_inc(pv_free, 2)
            for h in range(2):
                for qt in range(NT):
                    tile_max(h, qt)
                finish_max(h, h, None)
            with dve.Fori(0, H // 4 - 1) as i:
                for j in range(4):
                    for qt in range(NT):
                        tile_max(i * 4 + (j + 2), qt)
                    finish_max(i * 4 + (j + 2), (j + 2) % 4, i * 64 + 64)
                    head_out(i * 4 + j, j)
            for j in range(4):
                if j < 2:
                    for qt in range(NT):
                        tile_max(H - 2 + j, qt)
                    finish_max(H - 2 + j, j + 2, 64 * (H // 4))
                head_out(H - 4 + j, j)


def norm_statistics(dve, stats, mv, rows, t, step, count):
    dve.bn_stats(stats[:, t % 2, :], rows).then_inc(step, 1)
    dve.wait_ge(step, count + 1)
    dve.bn_aggr(mv[:, t, :], stats[:, t % 2, :]).then_inc(step, 1)
    return count + 2


def output_projection(nc, mem, layer):
    ps, x, y = mem["ps"], mem["x"], mem["y"]
    w_o = 3 if layer == 0 else 9
    with Stage(nc) as ctx:
        sem = lambda name: ctx.semaphore(f"{name}_{layer}")
        sb = lambda name, shape, dt=F32: ctx.enter_context(nc.sbuf_tensor(f"{name}_{layer}", shape, dt))
        yt_h, yt_l = sb("yt_h", [P, KD, T], F32R), sb("yt_l", [P, KD, T], F32R)
        turned, high_ready, low_ready = sem("y_turned"), sem("y_high"), sem("y_low")
        o_ready, o_out, biased = sem("o_ready"), sem("o_out"), sem("x_biased")
        block_sems = (turned, high_ready, low_ready)
        norm = NormStage(nc, ctx, mem, f"a{layer}")
        block = ctx.enter_context(nc.Block())

        def turned_bank(n):
            return ps[:, (n % 2) * HALF:(n % 2 + 1) * HALF]

        def out_bank(t):
            return ps[:, (2 + t % 2) * HALF:(2 + t % 2) * HALF + D]

        @block.tensor
        def _(pe):
            for n in range(4):
                if n >= 2:
                    pe.wait_ge(low_ready, n - 1)
                    pe.wait_ge(high_ready, n - 1)
                k, g = n % 2, n // 2
                for t in range(4):
                    mm = pe.transpose(turned_bank(n)[:, t * P:(t + 1) * P], y[:, 4 * g + t, k * P:(k + 1) * P],
                                      mem["consts"][:, C_ID:C_ID + P])
                mm.then_inc(turned, 1)
            for t in range(NT):
                if t % 4 == 0:
                    pe.wait_ge(low_ready, 2 + 2 * (t // 4))
                if t >= 2:
                    pe.wait_ge(o_out, t - 1)
                toks = slice(t * P, (t + 1) * P)
                for k in range(KD):
                    w = slice(k * D, (k + 1) * D)
                    mm = product(pe, out_bank(t), (yt_h[:, k, toks], yt_l[:, k, toks]),
                                 (mem["wa_h"][:, w_o, w], mem["wa_l"][:, w_o, w]), k == 0, k == KD - 1)
                mm.then_inc(o_ready, 1)
            norm.tensor(pe)

        @block.scalar
        def _(act):
            for n in range(4):
                k, g = n % 2, n // 2
                act.wait_ge(turned, n + 1)
                act.activation(yt_h[:, k, g * HALF:(g + 1) * HALF], turned_bank(n), ACT.Copy).then_inc(high_ready, 1)
            norm.scalar(act)

        if layer == 0:
            @block.gpsimd
            def _(pool):
                for t in range(NT):
                    pool.tensor_tensor(x[:, t, :], x[:, t, :], mem["bias_o"][:, :], ALU.add).then_inc(biased, 1)

        @block.vector
        def _(dve):
            for n in range(4):
                k, g = n % 2, n // 2
                dve.wait_ge(high_ready, n + 1)
                dve.tensor_tensor(yt_l[:, k, g * HALF:(g + 1) * HALF], turned_bank(n),
                                  yt_h[:, k, g * HALF:(g + 1) * HALF].bitcast(F32), ALU.subtract).then_inc(low_ready, 1)
            for t in range(NT):
                dve.wait_ge(o_ready, t + 1)
                if layer == 0:
                    dve.wait_ge(biased, t + 1)
                dve.tensor_tensor(x[:, t, :], out_bank(t), x[:, t, :], ALU.add).then_inc(o_out, 1)
                dve.wait_ge(o_out, t + 1)
                norm.statistics(dve, t)
            norm.vector(dve)


class NormStage:

    def __init__(self, nc, ctx, mem, name, last=False):
        self.mem, self.last, self.count = mem, last, 0
        sb = lambda n, shape: ctx.enter_context(nc.sbuf_tensor(f"{n}_{name}", shape, F32))
        sem = lambda n: ctx.semaphore(f"{n}_{name}")
        self.stats, self.mv = sb("stats", [P, 2, 6]), sb("mv", [P, NT, 2])
        self.std, self.rstd = sb("std", [P, NT]), sb("rstd", [P, NT])
        self.step, self.std_ready, self.rstd_ready = sem("stat_step"), sem("std_ready"), sem("rstd_ready")
        self.normed, self.turned, self.high, self.low = sem("normed"), sem("x_turned"), sem("xt_high"), sem("xt_low")

    def bank(self, n):
        return self.mem["ps"][:, (4 + n) * HALF:(5 + n) * HALF]

    def statistics(self, dve, t):
        self.count = norm_statistics(dve, self.stats, self.mv, self.mem["x"][:, t, :], t, self.step, self.count)

    def scalar(self, act):
        act.wait_ge(self.step, 2 * NT)
        act.activation(self.std[:, :], self.mv[:, :, 1], ACT.Sqrt, bias=self.mem["eps"][:, :]).then_inc(self.std_ready, 1)
        if not self.last:
            for n in range(4):
                k, g = n % 2, n // 2
                act.wait_ge(self.turned, n + 1)
                act.activation(self.mem["xt_h"][:, k, g * HALF:(g + 1) * HALF], self.bank(n), ACT.Copy).then_inc(self.high, 1)

    def tensor(self, pe):
        for n in range(4):
            k, g = n % 2, n // 2
            pe.wait_ge(self.normed, 4 * (g + 1))
            for t in range(4):
                mm = pe.transpose(self.bank(n)[:, t * P:(t + 1) * P], self.mem["x"][:, 4 * g + t, k * P:(k + 1) * P],
                                  self.mem["consts"][:, C_ID:C_ID + P])
            mm.then_inc(self.turned, 1)

    def vector(self, dve):
        x = self.mem["x"]
        dve.wait_ge(self.std_ready, 1)
        dve.reciprocal(self.rstd[:, :], self.std[:, :]).then_inc(self.rstd_ready, 1)
        dve.wait_ge(self.rstd_ready, 1)
        for t in range(NT):
            dve.tensor_scalar(x[:, t, :], x[:, t, :], self.mv[:, t, 0:1], self.rstd[:, t:t + 1],
                              ALU.subtract, ALU.mult).then_inc(self.normed, 1)
        if not self.last:
            for n in range(4):
                k, g = n % 2, n // 2
                dve.wait_ge(self.high, n + 1)
                xh = self.mem["xt_h"][:, k, g * HALF:(g + 1) * HALF]
                dve.tensor_tensor(self.mem["xt_l"][:, k, g * HALF:(g + 1) * HALF], self.bank(n), xh.bitcast(F32),
                                  ALU.subtract).then_inc(self.low, 1)


class TopTwo:

    def __init__(self, nc, ctx, mem, name, experts, tri):
        self.mem, self.e, self.tri = mem, experts, tri
        sb = lambda n, shape: ctx.enter_context(nc.sbuf_tensor(f"{n}_{name}", shape, F32))
        sem = lambda n: ctx.semaphore(f"{n}_{name}")
        e = experts
        self.logits = sb("logits", [P, NT, e])
        self.above, self.equal = sb("above", [P, NT, e * e]), sb("equal", [P, NT, e * e])
        self.chosen, self.shifted, self.expd = sb("chosen", [P, NT, e]), sb("shifted", [P, NT, e]), sb("expd", [P, NT, e])
        self.top, self.total, self.inv = sb("top", [P, NT]), sb("total", [P, NT]), sb("inv", [P, NT])
        self.weights = sb("weights", [P, NT, e])
        self.step, self.shift_ready, self.exp_ready, self.done = sem("route_step"), sem("shift_ready"), sem("rexp_ready"), sem("routed")

    def scalar(self, act):
        act.wait_ge(self.shift_ready, 1)
        act.activation(self.expd[:, :, :], self.shifted[:, :, :], ACT.Exp).then_inc(self.exp_ready, 1)

    def vector(self, dve):
        e, step = self.e, self.step
        flat = lambda a: a[:, :, :].rearrange("p t (e j) -> p t e j", j=e)
        mine = self.logits[:, :, :].unsqueeze(3).broadcast_to([P, NT, e, e])
        other = self.logits[:, :, :].unsqueeze(2).broadcast_to([P, NT, e, e])
        tri = self.mem["consts"][:, self.tri:self.tri + e * e].unsqueeze(1).broadcast_to([P, NT, e * e])
        wide = lambda a: a[:, :].unsqueeze(2).broadcast_to([P, NT, e])
        dve.tensor_reduce(self.top[:, :], self.logits[:, :, :], AX.X, ALU.max).then_inc(step, 1)
        dve.tensor_tensor(flat(self.above), other, mine, ALU.is_gt).then_inc(step, 1)
        dve.tensor_tensor(flat(self.equal), other, mine, ALU.is_equal).then_inc(step, 1)
        dve.wait_ge(step, 1)
        dve.tensor_tensor(self.shifted[:, :, :], self.logits[:, :, :], wide(self.top), ALU.subtract).then_inc(self.shift_ready, 1)
        dve.wait_ge(step, 3)
        dve.tensor_tensor(self.equal[:, :, :], self.equal[:, :, :], tri, ALU.mult).then_inc(step, 1)
        dve.wait_ge(step, 4)
        dve.tensor_tensor(self.above[:, :, :], self.above[:, :, :], self.equal[:, :, :], ALU.add).then_inc(step, 1)
        dve.wait_ge(step, 5)
        dve.tensor_reduce(self.chosen[:, :, :], flat(self.above), AX.X, ALU.add).then_inc(step, 1)
        dve.wait_ge(step, 6)
        dve.tensor_scalar(self.chosen[:, :, :], self.chosen[:, :, :], 2.0, None, ALU.is_lt).then_inc(step, 1)
        dve.wait_ge(step, 7)
        dve.wait_ge(self.exp_ready, 1)
        dve.tensor_tensor(self.expd[:, :, :], self.expd[:, :, :], self.chosen[:, :, :], ALU.mult).then_inc(step, 1)
        dve.wait_ge(step, 8)
        dve.tensor_reduce(self.total[:, :], self.expd[:, :, :], AX.X, ALU.add).then_inc(step, 1)
        dve.wait_ge(step, 9)
        dve.reciprocal(self.inv[:, :], self.total[:, :]).then_inc(step, 1)
        dve.wait_ge(step, 10)
        dve.tensor_tensor(self.weights[:, :, :], self.expd[:, :, :], wide(self.inv), ALU.mult).then_inc(self.done, 1)


def mixture_0(nc, mem, dram):
    ps, x, xt = mem["ps"], mem["x"], (mem["xt_h"], mem["xt_l"])
    CW = 2 * KD * I0 + D
    with Stage(nc) as ctx:
        sem = lambda name: ctx.semaphore(f"{name}_m0")
        sb = lambda name, shape, dt=F32: ctx.enter_context(nc.sbuf_tensor(f"{name}_m0", shape, dt))
        raw = sb("w_chunk", [P, 2, CW])
        w_h, w_l = sb("w_chunk_h", [P, 2, CW], F32R), sb("w_chunk_l", [P, 2, CW], F32R)
        r_raw = sb("r_raw", [P, KD * NR0])
        r_h, r_l = sb("r_h", [P, KD * NR0], F32R), sb("r_l", [P, KD * NR0], F32R)
        gated = sb("gated", [P, 2, HALF])
        hidden = sb("hidden", [P, 2, HALF])
        h_h, h_l = sb("h_h", [P, 2, T], F32R), sb("h_l", [P, 2, T], F32R)
        share = sb("share", [P, NT, CH])
        gate = sb("gate", [P, NT])
        loaded = [sem("chunk_loaded0"), sem("chunk_loaded1")]
        r_loaded, r_high, r_low = sem("r_loaded"), sem("r_high"), sem("r_low")
        up_high, up_low, dn_high, dn_low = sem("up_high"), sem("up_low"), sem("dn_high"), sem("dn_low")
        UPW, DNW = slice(0, 2 * KD * I0), slice(2 * KD * I0, CW)
        logits_ready, copied, gate_exp, gate_step, shared_ready = sem("logits_ready"), sem("copied"), sem("gate_exp"), sem("gate_step"), sem("shared_ready")
        up_ready, silu_ready, hidden_ready, hh_ready, hl_ready = sem("up_ready"), sem("silu_ready"), sem("hidden_ready"), sem("hh_ready"), sem("hl_ready")
        down_ready, added = sem("down_ready"), sem("added")
        top = TopTwo(nc, ctx, mem, "m0", E0, C_T8)
        norm = NormStage(nc, ctx, mem, "m0")
        block = ctx.enter_context(nc.Block())

        G, U = 0, 2

        def bank(b):
            return ps[:, b * HALF:(b + 1) * HALF]

        def down_bank(t):
            return ps[:, (4 + t // 2) * HALF + (t % 2) * D:(4 + t // 2) * HALF + (t % 2 + 1) * D]

        @block.sync
        def _(sp):
            sp.dma_start(r_raw[:, :], dram["w_router0"]).then_inc(r_loaded, 16)
            for c in range(2):
                sp.dma_start(raw[:, c, :], dram["w_chunks0"][c]).then_inc(loaded[c], 16)
            with sp.Fori(0, CH // 2 - 1) as i:
                for b in range(2):
                    sp.wait_ge(dn_low, i * 2 + (b + 1))
                    sp.dma_start(raw[:, b, :], dram["w_chunks0"][bass.ds(i * 2 + (b + 2), 1), :, :]
                                 .rearrange("c p n -> (c p) n")).then_inc(loaded[b], 16)

        @block.gpsimd
        def _(pool):
            def low(c, b, w, high, done):
                pool.wait_ge(high, c + 1)
                pool.tensor_tensor(w_l[:, b, w], raw[:, b, w], w_h[:, b, w].bitcast(F32), ALU.subtract).then_inc(done, 1)

            low(0, 0, UPW, up_high, up_low)
            with pool.Fori(0, CH // 2 - 1) as i:
                for b in range(2):
                    low(i * 2 + (b + 1), 1 - b, UPW, up_high, up_low)
                    low(i * 2 + b, b, DNW, dn_high, dn_low)
            low(CH - 1, 1, UPW, up_high, up_low)
            low(CH - 2, 0, DNW, dn_high, dn_low)
            low(CH - 1, 1, DNW, dn_high, dn_low)

        @block.tensor
        def _(pe):
            pe.wait_ge(r_low, 1)
            for t in range(NT):
                toks = slice(t * P, (t + 1) * P)
                for k in range(KD):
                    r = slice(k * NR0, (k + 1) * NR0)
                    mm = product(pe, ps[:, 4 * HALF + t * NR0:4 * HALF + (t + 1) * NR0],
                                 (xt[0][:, k, toks], xt[1][:, k, toks]), (r_h[:, r], r_l[:, r]), k == 0, k == KD - 1)
            mm.then_inc(logits_ready, 1)

            def up(c, b):
                pe.wait_ge(up_low, c + 1)
                for n in range(2):
                    pe.wait_ge(hidden_ready, c * 2 + (n + 1))
                    cols = slice(n * HALF, (n + 1) * HALF)
                    for base, off in ((G, 0), (U, KD * I0)):
                        for k in range(KD):
                            w = slice(off + k * I0, off + (k + 1) * I0)
                            mm = product(pe, bank(base + n), (w_h[:, b, w], w_l[:, b, w]),
                                         (xt[0][:, k, cols], xt[1][:, k, cols]), k == 0, k == KD - 1)
                    mm.then_inc(up_ready, 1)

            def down(c, b):
                pe.wait_ge(hl_ready, c * 2 + 2)
                pe.wait_ge(dn_low, c + 1)
                pe.wait_ge(added, c * NT + NT)
                w = slice(2 * KD * I0, CW)
                for t in range(NT):
                    toks = slice(t * P, (t + 1) * P)
                    mm = product(pe, down_bank(t), (h_h[:, b, toks], h_l[:, b, toks]), (w_h[:, b, w], w_l[:, b, w]),
                                 True, True)
                    mm.then_inc(down_ready, 1)

            up(0, 0)
            with pe.Fori(0, CH // 2 - 1) as i:
                for b in range(2):
                    up(i * 2 + (b + 1), 1 - b)
                    down(i * 2 + b, b)
            up(CH - 1, 1)
            down(CH - 2, 0)
            down(CH - 1, 1)
            norm.tensor(pe)

        @block.scalar
        def _(act):
            def split_up(c, b, loads):
                act.wait_ge(loaded[b], 16 * loads)
                act.activation(w_h[:, b, UPW], raw[:, b, UPW], ACT.Copy).then_inc(up_high, 1)

            def split_down(c, b):
                act.activation(w_h[:, b, DNW], raw[:, b, DNW], ACT.Copy).then_inc(dn_high, 1)

            def silu(c, b):
                for n in range(2):
                    act.wait_ge(up_ready, c * 2 + (n + 1))
                    act.wait_ge(hidden_ready, c * 2 + (n + 1))
                    act.activation(gated[:, n, :], bank(G + n), ACT.Silu).then_inc(silu_ready, 1)
                    act.wait_ge(hidden_ready, c * 2 + (n + 3))
                    act.activation(h_h[:, b, n * HALF:(n + 1) * HALF], hidden[:, n, :], ACT.Copy).then_inc(hh_ready, 1)

            act.wait_ge(r_loaded, 16)
            act.activation(r_h[:, :], r_raw[:, :], ACT.Copy).then_inc(r_high, 1)
            split_up(0, 0, 1)
            top.scalar(act)
            act.wait_ge(copied, 2)
            act.activation(gate[:, :], gate[:, :], ACT.Exp, scale=-1.0).then_inc(gate_exp, 1)
            split_up(1, 1, 1)
            split_down(0, 0)
            silu(0, 0)
            act.wait_ge(up_ready, 2)
            split_up(2, 0, 2)
            split_down(1, 1)
            silu(1, 1)
            with act.Fori(1, CH // 2 - 1) as i:
                for b in range(2):
                    act.wait_ge(up_ready, i * 4 + 2 * b)
                    split_up(i * 2 + (b + 1), 1 - b, i + (1 + b))
                    act.wait_ge(down_ready, i * (2 * NT) + (b - 1) * NT)
                    split_down(i * 2 + b, b)
                    silu(i * 2 + b, b)
            act.wait_ge(up_ready, 2 * CH - 4)
            split_up(CH - 1, 1, CH // 2)
            act.wait_ge(down_ready, (CH - 3) * NT)
            split_down(CH - 2, 0)
            silu(CH - 2, 0)
            act.wait_ge(down_ready, (CH - 2) * NT)
            split_down(CH - 1, 1)
            silu(CH - 1, 1)
            norm.scalar(act)

        @block.vector
        def _(dve):
            def multiply(c, b):
                for n in range(2):
                    dve.wait_ge(silu_ready, c * 2 + (n + 1))
                    dve.tensor_tensor(hidden[:, n, :], gated[:, n, :], bank(U + n), ALU.mult).then_inc(hidden_ready, 1)
                    dve.wait_ge(hh_ready, c * 2 + (n + 1))
                    cols = slice(n * HALF, (n + 1) * HALF)
                    dve.tensor_tensor(h_l[:, b, cols], hidden[:, n, :], h_h[:, b, cols].bitcast(F32), ALU.subtract
                                      ).then_inc(hl_ready, 1)

            def add_up(c, b):
                for t in range(NT):
                    dve.wait_ge(down_ready, c * NT + (t // 2 * 2 + 2))
                    dve.wait_ge(added, c * NT + (t + 1))
                    dve.scalar_tensor_tensor(out=x[:, t, :], in0=down_bank(t), scalar=share[:, t, bass.ds(c, 1)],
                                             in1=x[:, t, :], op0=ALU.mult, op1=ALU.add).then_inc(added, 1)

            dve.wait_ge(r_high, 1)
            dve.tensor_tensor(r_l[:, :], r_raw[:, :], r_h[:, :].bitcast(F32), ALU.subtract).then_inc(r_low, 1)
            dve.memset(hidden[:, 0, 0:1], 0.0).then_inc(hidden_ready, 2)
            dve.memset(hidden[:, 1, 0:1], 0.0).then_inc(copied, 1)
            dve.wait_ge(logits_ready, 1)
            logits = ps[:, 4 * HALF:4 * HALF + NT * NR0].rearrange("p (t e) -> p t e", e=NR0)
            dve.tensor_copy(gate[:, :], logits[:, :, E0]).then_inc(copied, 1)
            dve.tensor_copy(top.logits[:, :, :], logits[:, :, 0:E0]).then_inc(copied, 1)
            dve.wait_ge(copied, 3)
            dve.memset(share[:, :, :], 0.0).then_inc(added, NT)
            top.vector(dve)
            dve.wait_ge(gate_exp, 1)
            dve.tensor_scalar(gate[:, :], gate[:, :], 1.0, None, ALU.add).then_inc(gate_step, 1)
            dve.wait_ge(gate_step, 1)
            dve.reciprocal(gate[:, :], gate[:, :]).then_inc(gate_step, 1)
            dve.wait_ge(gate_step, 2)
            dve.wait_ge(added, NT)
            dve.wait_ge(top.done, 1)
            dve.tensor_copy(share[:, :, 0:E0], top.weights[:, :, :]).then_inc(shared_ready, 1)
            dve.tensor_copy(share[:, :, E0:CH], gate[:, :].unsqueeze(2).broadcast_to([P, NT, CH - E0])).then_inc(shared_ready, 1)
            dve.wait_ge(shared_ready, 2)
            dve.wait_ge(hidden_ready, 2)
            multiply(0, 0)
            with dve.Fori(0, CH // 2 - 1) as i:
                for b in range(2):
                    multiply(i * 2 + (b + 1), 1 - b)
                    add_up(i * 2 + b, b)
            multiply(CH - 1, 1)
            add_up(CH - 2, 0)
            add_up(CH - 1, 1)
            dve.wait_ge(added, NT * (CH + 1))
            for t in range(NT):
                norm.statistics(dve, t)
            norm.vector(dve)


def mixture_1(nc, mem, dram):
    ps, x, consts = mem["ps"], mem["x"], mem["consts"]
    xt = (mem["xt_h"], mem["xt_l"])
    ST = CAP // P
    with Stage(nc) as ctx:
        sem = lambda name: ctx.semaphore(f"{name}_m1")
        sb = lambda name, shape, dt=F32: ctx.enter_context(nc.sbuf_tensor(f"{name}_m1", shape, dt))
        raw = sb("w_raw", [P, 2, KD * H1])
        w_h, w_l = sb("w_h", [P, 3, KD * H1], F32R), sb("w_l", [P, 3, KD * H1], F32R)
        r_raw, r_h, r_l = sb("r_raw", [P, KD * E1]), sb("r_h", [P, KD * E1], F32R), sb("r_l", [P, KD * E1], F32R)
        x_h, x_l = sb("x_h", [P, NT, D], F32R), sb("x_l", [P, NT, D], F32R)
        score = sb("score", [P, NT, E1])
        s_h, s_l = sb("s_h", [P, NT, E1], F32R), sb("s_l", [P, NT, E1], F32R)
        w_parts = sb("w_parts", [P, NT, E1, 2], F32R)
        ident = sb("ident", [P, P], F32R)
        score_row = sb("score_row", [P, T])
        ties = sb("ties", [P, P])
        before = sb("before", [P, NT, T], BF16)
        ones = sb("ones", [P, P], BF16)
        rank = sb("rank", [P, NT])
        rank_row = sb("rank_row", [P, T])
        one_hot = sb("one_hot", [P, NT, CAP], F32R)
        one_hot_t = sb("one_hot_t", [P, E1, ST, T], F32R)
        xg_h, xg_l = sb("xg_h", [P, KD, CAP], F32R), sb("xg_l", [P, KD, CAP], F32R)
        gelu = sb("gelu", [P, 2, 2 * CAP])
        g_h, g_l = sb("g_h", [P, MT1 * CAP], F32R), sb("g_l", [P, MT1 * CAP], F32R)
        p_parts, p_slot = sb("p_parts", [P, ST, 2]), sb("p_slot", [P, ST])
        scaled = sb("scaled", [P, ST, D])
        y_parts = [mem[n][:, :, :].rearrange("p k (a s d) -> p (k a) s d", s=ST, d=D) for n in ("xt_h", "xt_l")]

        r_in, w1_in, w2_in = sem("r_in"), sem("w1_in"), sem("w2_in")
        r_high, r_low, xh_ready, xl_ready = sem("r_high"), sem("r_low"), sem("xh_ready"), sem("xl_ready")
        preset, logits_ready, logits_out = sem("preset"), sem("logits_ready"), sem("logits_out")
        score_step, parts_ready = sem("score_step"), sem("parts_ready")
        row_ready, row_out, tie_step, before_ready = sem("row_ready"), sem("row_out"), sem("tie_step"), sem("before_ready")
        rank_ready, rank_out, rank_row_out = sem("rank_ready"), sem("rank_out"), sem("rank_row_out")
        hot_ready, hot_t_ready = sem("hot_ready"), sem("hot_t_ready")
        gathered, xgh_ready, xgl_ready = sem("gathered"), sem("xgh_ready"), sem("xgl_ready")
        p_ready, p_out, p_step = sem("p_ready"), sem("p_out"), sem("p_step")
        w_high, w_low = sem("w_high"), sem("w_low")
        up_ready, gelu_ready, gh_ready, gl_ready = sem("up_ready"), sem("gelu_ready"), sem("gh_ready"), sem("gl_ready")
        down_ready, scaled_ready, yh_ready, yl_ready = sem("down_ready"), sem("scaled_ready"), sem("yh_ready"), sem("yl_ready")
        back_ready, added = sem("back_ready"), sem("added")
        top = TopTwo(nc, ctx, mem, "m1", E1, C_T4)
        norm = NormStage(nc, ctx, mem, "m1", last=True)
        block = ctx.enter_context(nc.Block())

        def bank(b, a=0, n=HALF):
            return ps[:, b * HALF + a:b * HALF + a + n]

        LOGITS, ROW, DOWN, RANKS, XG, SMALL, UP = 0, 0, 1, 2, 4, 5, 6
        NQ = MT1 // 2

        @block.sync
        def _(sp):
            sp.dma_start(r_raw[:, :], dram["w_router1"]).then_inc(r_in, 16)
            for e in range(E1):
                for n, done in ((0, w1_in), (1, w2_in)):
                    if e:
                        sp.wait_ge(w_low, 2 * (e - 1) + n + 1)
                    sp.dma_start(raw[:, n, :], dram["w_experts1"][e, n]).then_inc(done, 16)

        @block.gpsimd
        def _(pool):
            for e in range(E1):
                for n in range(2):
                    pool.wait_ge(w_high, 2 * e + n + 1)
                    at = 2 if n else e % 2
                    pool.tensor_tensor(w_l[:, at, :], raw[:, n, :], w_h[:, at, :].bitcast(F32), ALU.subtract
                                       ).then_inc(w_low, 1)

        @block.scalar
        def _(act):
            def split_weights(e, n):
                act.wait_ge((w1_in, w2_in)[n], 16 * (e + 1))
                act.activation(w_h[:, 2 if n else e % 2, :], raw[:, n, :], ACT.Copy).then_inc(w_high, 1)

            def copy_row(e):
                for n in range(2):
                    act.wait_ge(row_ready, 2 * e + n + 1)
                    act.wait_ge(before_ready, NT * e)
                    act.activation(score_row[:, n * HALF:(n + 1) * HALF], bank(ROW), ACT.Copy).then_inc(row_out, 1)

            act.wait_ge(r_in, 16)
            act.activation(r_h[:, :], r_raw[:, :], ACT.Copy).then_inc(r_high, 1)
            act.activation(x_h[:, :, :], x[:, :, :], ACT.Copy).then_inc(xh_ready, 1)
            act.activation(ident[:, :], consts[:, C_ID:C_ID + P], ACT.Copy).then_inc(preset, 1)
            top.scalar(act)
            copy_row(0)
            split_weights(0, 0)
            split_weights(0, 1)
            for e in range(E1):
                for n in range(2):
                    act.wait_ge(rank_ready, 2 * e + 2)
                    if e:
                        act.wait_ge(hot_t_ready, 2 * e)
                    act.activation(rank_row[:, n * HALF:(n + 1) * HALF], bank(RANKS + n), ACT.Copy).then_inc(rank_row_out, 1)
                if e + 1 < E1:
                    copy_row(e + 1)
                act.wait_ge(gathered, e + 1)
                if e:
                    act.wait_ge(up_ready, NQ * e)
                act.activation(xg_h[:, :, :], bank(XG).rearrange("p (k s) -> p k s", k=KD), ACT.Copy).then_inc(xgh_ready, 1)
                for q in range(NQ):
                    n = NQ * e + q
                    act.wait_ge(up_ready, n + 1)
                    if n >= 2:
                        act.wait_ge(gl_ready, n - 1)
                    act.activation(gelu[:, q % 2, :], bank(UP + q % 2), ACT.Gelu).then_inc(gelu_ready, 1)
                    act.wait_ge(gelu_ready, n + 1)
                    if e:
                        act.wait_ge(down_ready, e)
                    act.activation(g_h[:, q * HALF:(q + 1) * HALF], gelu[:, q % 2, :], ACT.Copy).then_inc(gh_ready, 1)
                if e + 1 < E1:
                    split_weights(e + 1, 0)
                act.wait_ge(scaled_ready, e + 1)
                act.activation(y_parts[0][:, e, :, :], scaled[:, :, :], ACT.Copy).then_inc(yh_ready, 1)
                if e + 1 < E1:
                    split_weights(e + 1, 1)
            norm.scalar(act)

        @block.tensor
        def _(pe):
            pe.wait_ge(r_low, 1)
            for t in range(NT):
                toks = slice(t * P, (t + 1) * P)
                for k in range(KD):
                    r = slice(k * E1, (k + 1) * E1)
                    mm = product(pe, bank(LOGITS, t * E1, E1), (xt[0][:, k, toks], xt[1][:, k, toks]),
                                 (r_h[:, r], r_l[:, r]), k == 0, k == KD - 1)
            mm.then_inc(logits_ready, 1)

            def row(e):
                for n in range(2):
                    if e or n:
                        pe.wait_ge(row_out, 2 * e + n)
                    for t in range(4 * n, 4 * n + 4):
                        for part, s in enumerate((s_h, s_l)):
                            mm = pe.matmul(bank(ROW, (t % 4) * P, P), s[:, t, e:e + 1].broadcast_to([P, P]), ident[:, :],
                                           start=part == 0, stop=part == 1, skip_group_check=True)
                    mm.then_inc(row_ready, 1)

            pe.wait_ge(parts_ready, 3)
            pe.wait_ge(preset, 2)
            row(0)
            for e in range(E1):
                for a in range(NT):
                    pe.wait_ge(before_ready, NT * e + a + 1)
                    if a == 0 and e:
                        pe.wait_ge(rank_row_out, 2 * e)
                        pe.wait_ge(p_out, e)
                    for t in range(NT):
                        mm = pe.matmul(bank(SMALL, t, 1), before[:, a, t * P:(t + 1) * P], ones[:, 0:1],
                                       start=(a == 0 and t == 0), stop=a == NT - 1, skip_group_check=True)
                    if a == NT - 1:
                        mm.then_inc(rank_ready, 1)
                    for n in range(2):
                        mm = pe.matmul(bank(RANKS + n), ones[:, :], before[:, a, n * HALF:(n + 1) * HALF],
                                       start=a == 0, stop=a == NT - 1)
                mm.then_inc(rank_ready, 1)
                if e + 1 < E1:
                    row(e + 1)
                if e:
                    pe.wait_ge(xgl_ready, e)
                for k in range(KD):
                    for t in range(NT):
                        if k == 0:
                            pe.wait_ge(hot_ready, NT * e + t + 1)
                        for part, xp in enumerate((x_h, x_l)):
                            mm = pe.matmul(bank(XG, k * CAP, CAP), xp[:, t, k * P:(k + 1) * P], one_hot[:, t, :],
                                           start=(t == 0 and part == 0), stop=(t == NT - 1 and part == 1),
                                           skip_group_check=True)
                mm.then_inc(gathered, 1)
                for s in range(ST):
                    for t in range(NT):
                        mm = pe.matmul(bank(SMALL, 16 + 2 * s, 2), one_hot[:, t, s * P:(s + 1) * P],
                                       w_parts[:, t, e, :], start=t == 0, stop=t == NT - 1, skip_group_check=True)
                mm.then_inc(p_ready, 1)
                pe.wait_ge(xgl_ready, e + 1)
                pe.wait_ge(w_low, 2 * e + 1)
                for q in range(NQ):
                    n = NQ * e + q
                    if n >= 2:
                        pe.wait_ge(gelu_ready, n - 1)
                    for half in range(2):
                        for k in range(KD):
                            w = slice(k * H1 + (2 * q + half) * P, k * H1 + (2 * q + half + 1) * P)
                            mm = product(pe, bank(UP + q % 2, half * CAP, CAP), (w_h[:, e % 2, w], w_l[:, e % 2, w]),
                                         (xg_h[:, k, :], xg_l[:, k, :]), k == 0, k == KD - 1)
                    mm.then_inc(up_ready, 1)
                pe.wait_ge(w_low, 2 * e + 2)
                if e:
                    pe.wait_ge(scaled_ready, e)
                for s in range(ST):
                    for m in range(MT1):
                        if s == 0 and m % 2 == 0:
                            pe.wait_ge(gl_ready, NQ * e + m // 2 + 1)
                        g, w = slice(m * CAP + s * P, m * CAP + (s + 1) * P), slice(m * D, (m + 1) * D)
                        mm = product(pe, bank(DOWN, s * D, D), (g_h[:, g], g_l[:, g]),
                                     (w_h[:, 2, w], w_l[:, 2, w]), m == 0, m == MT1 - 1)
                mm.then_inc(down_ready, 1)
            pe.wait_ge(yl_ready, E1)
            pe.wait_ge(hot_t_ready, 2 * E1)
            for t in range(NT):
                if t >= 2:
                    pe.wait_ge(added, t - 1)
                n = 0
                for e in range(E1):
                    for s in range(ST):
                        for y in y_parts:
                            mm = pe.matmul(bank(RANKS + t % 2, 0, D), one_hot_t[:, e, s, t * P:(t + 1) * P], y[:, e, s, :],
                                           start=n == 0, stop=n == 2 * ST * E1 - 1)
                            n += 1
                mm.then_inc(back_ready, 1)

        @block.vector
        def _(dve):
            steps = [0]

            def link(ins):
                steps[0] += 1
                ins.then_inc(score_step, 1)
                dve.wait_ge(score_step, steps[0])

            dve.memset(ones[:, :], 1.0).then_inc(preset, 1)
            dve.wait_ge(r_high, 1)
            dve.tensor_tensor(r_l[:, :], r_raw[:, :], r_h[:, :].bitcast(F32), ALU.subtract).then_inc(r_low, 1)
            dve.wait_ge(xh_ready, 1)
            dve.tensor_tensor(x_l[:, :, :], x[:, :, :], x_h[:, :, :].bitcast(F32), ALU.subtract).then_inc(xl_ready, 1)
            dve.wait_ge(logits_ready, 1)
            dve.tensor_tensor(top.logits[:, :, :], bank(LOGITS, 0, NT * E1).rearrange("p (t e) -> p t e", e=E1),
                              mem["bias_g"][:, :].unsqueeze(1).broadcast_to([P, NT, E1]), ALU.add).then_inc(logits_out, 1)
            dve.wait_ge(logits_out, 1)
            top.vector(dve)
            dve.wait_ge(top.done, 1)
            link(dve.scalar_tensor_tensor(out=score[:, :, :], in0=top.chosen[:, :, :], scalar=-1.0,
                                          in1=top.weights[:, :, :], op0=ALU.add, op1=ALU.add))
            link(dve.tensor_copy(s_h[:, :, :], score[:, :, :]))
            dve.tensor_tensor(s_l[:, :, :], score[:, :, :], s_h[:, :, :].bitcast(F32), ALU.subtract).then_inc(parts_ready, 1)
            link(dve.tensor_copy(w_parts[:, :, :, 0], top.weights[:, :, :]))
            dve.tensor_tensor(w_parts[:, :, :, 1], top.weights[:, :, :], w_parts[:, :, :, 0].bitcast(F32), ALU.subtract
                              ).then_inc(parts_ready, 1)
            dve.wait_ge(parts_ready, 1)
            dve.tensor_tensor(score[:, :, :], s_h[:, :, :].bitcast(F32), s_l[:, :, :].bitcast(F32), ALU.add
                              ).then_inc(parts_ready, 1)
            dve.wait_ge(parts_ready, 3)

            def compare(e, a):
                if a == 0:
                    dve.wait_ge(row_out, 2 * e + 2)
                if e:
                    dve.wait_ge(rank_ready, 2 * e)
                own, mine = slice(a * P, (a + 1) * P), score[:, a, e:e + 1]
                n = NT * e + a
                dve.wait_ge(before_ready, n)
                dve.scalar_tensor_tensor(out=ties[:, :], in0=score_row[:, own], scalar=mine, in1=consts[:, C_TRI:C_TRI + P],
                                         op0=ALU.is_equal, op1=ALU.mult).then_inc(tie_step, 1)
                if a:
                    dve.tensor_scalar(before[:, a, 0:a * P], score_row[:, 0:a * P], mine, None, ALU.is_lt)
                if a < NT - 1:
                    dve.tensor_scalar(before[:, a, (a + 1) * P:T], score_row[:, (a + 1) * P:T], mine, None, ALU.is_le)
                dve.wait_ge(tie_step, n + 1)
                dve.scalar_tensor_tensor(out=before[:, a, own], in0=score_row[:, own], scalar=mine, in1=ties[:, :],
                                         op0=ALU.is_lt, op1=ALU.add).then_inc(before_ready, 1)

            for a in range(NT):
                compare(0, a)
            for e in range(E1):
                dve.wait_ge(rank_ready, 2 * e + 1)
                dve.tensor_copy(rank[:, :], bank(SMALL, 0, NT)).then_inc(rank_out, 1)
                dve.wait_ge(rank_out, e + 1)
                if e:
                    dve.wait_ge(p_ready, e)
                for t in range(NT):
                    dve.tensor_scalar(one_hot[:, t, :], consts[:, C_IOTA:C_IOTA + CAP], rank[:, t:t + 1], None,
                                      ALU.is_equal).then_inc(hot_ready, 1)
                dve.wait_ge(rank_row_out, 2 * e + 2)
                for s in range(ST):
                    dve.tensor_scalar(one_hot_t[:, e, s, :], rank_row[:, :], consts[:, C_SLOT + s:C_SLOT + s + 1], None,
                                      ALU.is_equal).then_inc(hot_t_ready, 1)
                dve.wait_ge(xgh_ready, e + 1)
                dve.tensor_tensor(xg_l[:, :, :], bank(XG).rearrange("p (k s) -> p k s", k=KD), xg_h[:, :, :].bitcast(F32),
                                  ALU.subtract).then_inc(xgl_ready, 1)
                dve.wait_ge(p_ready, e + 1)
                dve.tensor_copy(p_parts[:, :, :], bank(SMALL, 16, 2 * ST).rearrange("p (s l) -> p s l", l=2)).then_inc(p_out, 1)
                dve.wait_ge(p_out, e + 1)
                dve.tensor_reduce(p_slot[:, :], p_parts[:, :, :], AX.X, ALU.add).then_inc(p_step, 1)
                for q in range(NQ):
                    if e + 1 < E1:
                        compare(e + 1, 2 * q)
                        compare(e + 1, 2 * q + 1)
                    n = NQ * e + q
                    dve.wait_ge(gh_ready, n + 1)
                    cols = slice(q * HALF, (q + 1) * HALF)
                    dve.tensor_tensor(g_l[:, cols], gelu[:, q % 2, :], g_h[:, cols].bitcast(F32), ALU.subtract
                                      ).then_inc(gl_ready, 1)
                dve.wait_ge(down_ready, e + 1)
                dve.wait_ge(p_step, e + 1)
                dve.tensor_tensor(scaled[:, :, :], bank(DOWN).rearrange("p (s d) -> p s d", s=ST),
                                  p_slot[:, :].unsqueeze(2).broadcast_to([P, ST, D]), ALU.mult).then_inc(scaled_ready, 1)
                dve.wait_ge(yh_ready, e + 1)
                dve.tensor_tensor(y_parts[1][:, e, :, :], scaled[:, :, :], y_parts[0][:, e, :, :].bitcast(F32), ALU.subtract
                                  ).then_inc(yl_ready, 1)
            for t in range(NT):
                dve.wait_ge(back_ready, t + 1)
                dve.tensor_tensor(x[:, t, :], bank(RANKS + t % 2, 0, D), x[:, t, :], ALU.add).then_inc(added, 1)
                dve.wait_ge(added, t + 1)
                norm.statistics(dve, t)
            norm.vector(dve)


def store(nc, mem, dram):
    with Stage(nc) as ctx:
        stored = ctx.semaphore("stored")
        block = ctx.enter_context(nc.Block())

        @block.sync
        def _(sp):
            sp.dma_start(dram["out"].rearrange("(t p) d -> p t d", p=P), mem["x"][:, :, :]).then_inc(stored, 16)
            sp.wait_ge(stored, 16)


def program(nc, dram):
    dram = dict(dram)
    for t in "qk":
        dram[f"{t}_parts"] = nc.dram_tensor(f"{t}_parts", (D, 2, T), F32, kind="Internal").ap()
    with ExitStack() as ctx:
        def sb(c, name, shape, dt=F32):
            return c.enter_context(nc.sbuf_tensor(name, shape, dt))

        mem = {
            "ps": ctx.enter_context(nc.psum_tensor("ps", [P, 8 * HALF], F32)),
            "x": sb(ctx, "x", [P, NT, D]),
            "xt_h": sb(ctx, "xt_h", [P, KD, T], F32R),
            "xt_l": sb(ctx, "xt_l", [P, KD, T], F32R),
            "consts": sb(ctx, "consts", [P, C_END]),
            "eps": sb(ctx, "eps", [P, 1]),
            "bias_g": sb(ctx, "bias_g", [P, E1]),
        }
        with ExitStack() as heads:
            mem |= {
                "masks": sb(heads, "masks", [P, C_T8], BF16),
                "bias_qk": sb(heads, "bias_qk", [P, 4]),
                "bias_v": sb(heads, "bias_v", [P, D]),
                "bias_o": sb(heads, "bias_o", [P, D]),
                "rope": sb(heads, "rope", [P, 2, T]),
                "zeros": sb(heads, "zeros", [2, T]),
                "wa_h": sb(heads, "wa_h", [P, 10, KD * D], F32R),
                "wa_l": sb(heads, "wa_l", [P, 10, KD * D], F32R),
                "q_stack": sb(heads, "q_stack", [STACK, 4, T], F32R),
                "k_stack": sb(heads, "k_stack", [STACK, 4, T], F32R),
                "v_ring": sb(heads, "v_ring", [P, 4, NT, HD + 1]),
                "row_max": sb(heads, "row_max", [P, NT, 2]),
                "max_parts": sb(heads, "max_parts", [P, 32], F32R),
            }
            load_and_split(nc, mem, dram)
            for layer in range(2):
                with ExitStack() as out:
                    mem["y"] = sb(out, f"y_{layer}", [P, NT, D])
                    attention(nc, mem, dram, layer)
                    output_projection(nc, mem, layer)
                if layer == 0:
                    mixture_0(nc, mem, dram)
        mixture_1(nc, mem, dram)
        store(nc, mem, dram)


def contraction_first(w):
    k, n = w.shape
    return w.reshape(k // P, P, n).transpose(1, 0, 2).reshape(P, -1)


def shape_constants():
    c = np.zeros((P, C_END), np.float32)
    i = np.arange(P)
    c[:, C_ID:C_ID + P] = np.eye(P)
    c[:, C_CM:C_CM + P] = np.where(i[None, :] > i[:, None], MASKED, 0)
    c[:, C_CMT:C_CMT + P] = np.where(i[:, None] > i[None, :], MASKED, 0)
    for at, e in ((C_T8, E0), (C_T4, E1)):
        c[:, at:at + e * e] = np.tril(np.ones((e, e)), -1).reshape(-1)
    c[:, C_IOTA:C_IOTA + CAP] = np.arange(CAP)
    for s in range(CAP // P):
        c[:, C_SLOT + s] = i + s * P
    c[:, C_TRI:C_TRI + P] = i[:, None] < i[None, :]
    return c


def rope_tables():
    rot = HD // 2
    freq = (1.0 / np.float32(10000.0) ** (np.arange(0, HD, 2, dtype=np.float32) / np.float32(HD))).astype(np.float32)
    ang = (np.arange(T, dtype=np.float32)[:, None] * freq[None, :]).astype(np.float64)
    cos, sin = np.ones((HD, T)), np.zeros((HD, T))
    cos[:rot] = np.cos(ang).T
    sin[:rot] = np.sin(ang).T * np.where(np.arange(rot) < rot // 2, -1, 1)[:, None]
    return np.stack([np.tile(a, (P // HD, 1)) for a in (cos, sin)], 1).astype(np.float32)


def kernel(**inputs):
    import concourse.bacc as _bacc
    from concourse.bass_utils import run_bass_kernel_spmd as _run

    a = {k: np.asarray(v) for k, v in inputs.items()}
    cf = contraction_first
    by_head = lambda w: w.transpose(1, 0, 2).reshape(D, D)
    swap = np.arange(D).reshape(H, HD)
    swap = np.concatenate([swap[:, HD // 4:HD // 2], swap[:, :HD // 4], swap[:, HD // 2:]], 1).reshape(-1)
    x = a["L0_attn_x"].reshape(T, D)
    wq, wk = a["L1_attn_wq"], a["L1_attn_wk"]
    attn = [by_head(a["L0_attn_Wq"]), by_head(a["L0_attn_Wk"]), by_head(a["L0_attn_Wv"]), a["L0_attn_Wo"],
            wq.T, wq[swap].T, wk.T, wk[swap].T, a["L1_attn_wv"].T, a["L1_attn_wo"].T]
    router0 = np.concatenate([a["L0_ffn_w_router"], a["L0_ffn_gate_w"], np.zeros((1, D), np.float32)]).T
    gates = [*a["L0_ffn_wg"], *a["L0_ffn_sw_gate"].reshape(-1, I0, D)]
    ups = [*a["L0_ffn_wu"], *a["L0_ffn_sw_up"].reshape(-1, I0, D)]
    downs = [*a["L0_ffn_wd"], *a["L0_ffn_sw_down"].reshape(D, -1, I0).transpose(1, 0, 2)]
    arrays = {
        "x_t": x.T.reshape(KD, P, T).transpose(1, 0, 2),
        "x_tok": x.reshape(NT, P, D).transpose(1, 0, 2),
        "w_attn": np.stack([cf(w) for w in attn], 1),
        "bias_qk": np.concatenate([a["L0_attn_bq"].reshape(KD, P), a["L0_attn_bk"].reshape(KD, P)]).T,
        "bias_v": a["L0_attn_bv"].reshape(1, D),
        "bias_o": a["L0_attn_bo"].reshape(1, D),
        "bias_g": a["L1_ffn_bg"].reshape(1, E1),
        "w_router0": cf(router0),
        "w_chunks0": np.stack([np.concatenate([cf(g.T), cf(u.T), cf(d.T)], 1) for g, u, d in zip(gates, ups, downs)]),
        "w_router1": cf(a["L1_ffn_Wg"]),
        "w_experts1": np.stack([np.stack([cf(w1), cf(w2)]) for w1, w2 in zip(a["L1_ffn_W1"], a["L1_ffn_W2"])]),
        "consts": shape_constants(),
        "rope": rope_tables(),
    }
    arrays = {k: np.ascontiguousarray(v) for k, v in arrays.items()}
    nc = _bacc.Bacc("TRN2", target_bir_lowering=False, num_devices=1)
    dram = {k: nc.dram_tensor(f"in_{k}", v.shape, F32, kind="ExternalInput").ap() for k, v in arrays.items()}
    dram["out"] = nc.dram_tensor("out", (T, D), F32, kind="ExternalOutput").ap()
    program(nc, dram)
    r = _run(nc, [{f"in_{k}": v for k, v in arrays.items()}], core_ids=[0])
    return r.results[0]["out"].reshape(1, T, D)
```

```python
from contextlib import ExitStack

import numpy as np

import concourse.bass as bass
from concourse import mybir

F32 = mybir.dt.float32
F32R = mybir.dt.float32r
BF16 = mybir.dt.bfloat16
ALU = mybir.AluOpType
ACT = mybir.ActivationFunctionType
AX = mybir.AxisListType

P = 128
T = 1024
D = 256
H = 16
HD = D // H
NT = T // P
KD = D // P
HALF = 512
EPS = 1e-5
MASKED = -3.0e38

E0 = 8
I0 = 128
CH = E0 + 512 // I0
NR0 = E0 + 2
E1 = 4
H1 = 1024
CAP = T // E1
MT1 = H1 // P

C_ID, C_CM, C_CMT, C_T8, C_T4, C_IOTA, C_SLOT, C_TRI, C_END = 0, 128, 256, 384, 448, 464, 720, 722, 850

LEAD = 7
ROWS = 2 * 2 * HD
STACK = ROWS + 2


class Stage(ExitStack):

    def __init__(self, nc):
        super().__init__()
        self.nc, self.numbers = nc, []

    def semaphore(self, name):
        sem = self.enter_context(self.nc.semaphore(name))
        self.numbers.append(sem.num)
        return sem

    def __exit__(self, *exc):
        super().__exit__(*exc)
        if exc[0] is None:
            numbers = sorted(self.numbers)
            starts = [n for n in numbers if n - 1 not in numbers]
            ends = [n + 1 for n in numbers if n + 1 not in numbers]
            with self.nc.Block() as block:

                @block.sync
                def _(sp):
                    for start, end in zip(starts, ends):
                        sp.sem_clear(range(start, end))


def product(pe, out, lhs, rhs, first, last):
    (lh, ll), (rh, rl) = lhs, rhs
    pe.matmul(out, lh, rl, start=first, stop=False, skip_group_check=True)
    pe.matmul(out, ll, rh, start=False, stop=False, skip_group_check=True)
    return pe.matmul(out, lh, rh, start=False, stop=last, skip_group_check=True)


def load_and_split(nc, mem, dram):
    with Stage(nc) as ctx:
        sem = lambda name: ctx.semaphore(name)
        x_raw = ctx.enter_context(nc.sbuf_tensor("x_raw", [P, KD, T], F32))
        w_raw = ctx.enter_context(nc.sbuf_tensor("w_raw", [P, 10, KD * D], F32))
        consts_in, x_in, w_in = sem("consts_in"), sem("x_in"), [sem("w0_in"), sem("w1_in")]
        rest_in = sem("rest_in")
        x_high, w_high, low_done, preset = sem("x_high"), sem("w_high"), sem("low_done"), sem("preset")
        block = ctx.enter_context(nc.Block())

        @block.sync
        def _(sp):
            sp.dma_start(x_raw[:, :, :], dram["x_t"]).then_inc(x_in, 16)
            sp.dma_start(w_raw[:, 0:4, :], dram["w_attn"][:, 0:4, :]).then_inc(w_in[0], 16)
            sp.dma_start(mem["consts"][:, :], dram["consts"]).then_inc(consts_in, 16)
            sp.dma_start(mem["bias_qk"][:, :], dram["bias_qk"]).then_inc(rest_in, 16)
            sp.dma_start(mem["bias_v"][:, :], dram["bias_v"].broadcast_to([P, D])).then_inc(rest_in, 16)
            sp.dma_start(mem["bias_o"][:, :], dram["bias_o"].broadcast_to([P, D])).then_inc(rest_in, 16)
            sp.dma_start(mem["bias_g"][:, :], dram["bias_g"].broadcast_to([P, E1])).then_inc(rest_in, 16)
            sp.dma_start(w_raw[:, 4:10, :], dram["w_attn"][:, 4:10, :]).then_inc(w_in[1], 16)
            sp.dma_start(mem["x"][:, :, :], dram["x_tok"]).then_inc(rest_in, 16)
            sp.wait_ge(rest_in, 16 * 5)

        @block.scalar
        def _(act):
            act.wait_ge(x_in, 16)
            act.activation(mem["xt_h"][:, :, :], x_raw[:, :, :], ACT.Copy).then_inc(x_high, 1)
            for n, (a, b) in enumerate(((0, 4), (4, 10))):
                act.wait_ge(w_in[n], 16)
                act.activation(mem["wa_h"][:, a:b, :], w_raw[:, a:b, :], ACT.Copy).then_inc(w_high, 1)

        @block.vector
        def _(dve):
            for name in ("v_full", "v_split"):
                dve.memset(mem[name][:, :, :, 0:2 * HD].bitcast(F32), 0.0).then_inc(preset, 1)
                dve.memset(mem[name][:, :, :, 2 * HD:3 * HD].bitcast(F32), 1.0).then_inc(preset, 1)
            dve.memset(mem["zeros"][:, :], 0.0).then_inc(preset, 1)
            dve.memset(mem["eps"][:, :], EPS).then_inc(preset, 1)
            dve.memset(mem["row_max"][:, :, :], MASKED).then_inc(preset, 1)
            dve.memset(mem["max_parts"][:, :].bitcast(F32), 0.0).then_inc(preset, 1)
            for j in range(4):
                dve.memset(mem["k_stack"][ROWS:STACK, j, :].bitcast(F32), 1.0).then_inc(preset, 1)
            dve.wait_ge(x_high, 1)
            dve.tensor_tensor(mem["xt_l"][:, :, :], x_raw[:, :, :], mem["xt_h"][:, :, :].bitcast(F32),
                              ALU.subtract).then_inc(low_done, 1)
            for n, (a, b) in enumerate(((0, 4), (4, 10))):
                dve.wait_ge(w_high, n + 1)
                dve.tensor_tensor(mem["wa_l"][:, a:b, :], w_raw[:, a:b, :], mem["wa_h"][:, a:b, :].bitcast(F32),
                                  ALU.subtract).then_inc(low_done, 1)
            dve.wait_ge(consts_in, 16)
            dve.tensor_copy(mem["masks"][:, :], mem["consts"][:, C_ID:C_T8]).then_inc(low_done, 1)


def attention(nc, mem, dram, layer):
    causal, rope = layer == 0, layer == 1
    ps = mem["ps"]
    qs, ks = mem["q_stack"], mem["k_stack"]
    low_on = {0: "pool", 1: "dve", 2: "pool", 4: "pool"} if causal else {0: "pool", 1: "dve", 2: "pool", 3: "pool", 4: "dve", 5: "pool", 6: "dve", 7: "pool"}
    split = sorted(low_on)
    on = {e: [kt for kt in split if low_on[kt] == e] for e in ("pool", "dve")}
    scratch = {"q": dram["q_parts"], "k": dram["k_parts"]}
    units = [(t, m, n) for m in range(KD) for t in "qk" for n in range(2)]
    w_at = {"q": 4, "qp": 5, "k": 6, "kp": 7, "v": 8} if rope else {"q": 0, "k": 1, "v": 2}

    def pieces(qt):
        end = (qt + 1) * P if causal else T
        return [(a, min(a + HALF, end)) for a in range(0, end, HALF)]

    def piece_number(qt):
        return sum(len(pieces(t)) for t in range(qt))

    PIECES = piece_number(NT)

    with Stage(nc) as ctx:
        sem = lambda name: ctx.semaphore(f"{name}_{layer}")
        sb = lambda name, shape, dt=F32: ctx.enter_context(nc.sbuf_tensor(f"{name}_{layer}", shape, dt))
        probs = sb("probs", [P, 4, T])
        p_high, p_low = sb("p_high", [P, 4, T], F32R), sb("p_low", [P, 4, T], F32R)
        halves = lambda n: probs[:, n, :].rearrange("p (u c) -> p u c", u=2)
        flat, turned = halves(0), halves(1)
        parts = p_high[:, :, :].rearrange("p (g l) t -> p g l t", l=2)
        tables = probs[:, 2:4, :]
        v_all = sb("v_all", [P, NT, D])
        max_rows = sb("max_rows", [P, 2, 32])
        negmax = sb("negmax", [P, NT])
        sums = sb("sums", [3 * HD, 2, T])

        unit_ready, unit_out, high_ready, low_ready = sem("unit_ready"), sem("unit_out"), sem("high_ready"), sem("low_ready")
        rope_step = sem("rope_step")
        v_ready, v_out = sem("v_ready"), sem("v_out")
        written = [sem(f"written{m}") for m in range(2 * KD)]
        loaded = [sem(f"loaded{j}") for j in range(4)]
        max_loaded = [sem(f"max_loaded{j}") for j in range(4)]
        scores_ready, scores_free, fin, max_ready = sem("scores_ready"), sem("scores_free"), sem("fin"), sem("max_ready")
        st_ready, exp_done = sem("st_ready"), sem("exp_done")
        pv_ready, sums0_out, sums1_out = sem("pv_ready"), sem("sums0_out"), sem("sums1_out")
        p_high_ready = sem("p_high_ready")
        p_low_ready = {"pool": sem("p_low_pool"), "dve": sem("p_low_dve")}
        stored = [sem("sums_stored0"), sem("sums_stored1")]
        tables_in, recip_ready = sem("tables_in"), sem("sums_inverted")
        y_loaded = sem("y_loaded")
        v_step, v_copied = sem("v_step"), sem("v_copied")
        block = ctx.enter_context(nc.Block())

        def bank(b, a=0, n=HALF):
            return ps[:, b * HALF + a:b * HALF + a + n]

        def sums_bank(n, a=0, b=HALF):
            return ps[0:3 * HD, (6 + n) * HALF + a:(6 + n) * HALF + b]

        @block.sync
        def _(sp):
            def write_parts(g):
                t, m, _ = units[2 * g]
                sp.wait_ge(low_ready, 2 * g + 2)
                sp.dma_start(scratch[t][m * P:(m + 1) * P, :, :], parts[:, g % 2, :, :].bitcast(F32)).then_inc(written[g], 16)

            def load_stacks(h, j):
                q = scratch["q"][bass.ds(h * HD, HD), :, :]
                k = scratch["k"][bass.ds(h * HD, HD), :, :].rearrange("d l t -> (d l) t")
                for part in range(2):
                    rows = slice(part * 2 * HD, (part + 1) * 2 * HD)
                    sp.dma_start(qs[rows, j, :].bitcast(F32), q[:, part:part + 1, :].broadcast_to([HD, 2, T])
                                 ).then_inc(loaded[j], 16)
                    sp.dma_start(ks[rows, j, :].bitcast(F32), k).then_inc(loaded[j], 16)
                sp.dma_start(qs[ROWS:STACK, j, :].bitcast(F32), mem["zeros"][0:2, :]).then_inc(loaded[j], 16)

            def load_max(h, j, count):
                sp.wait_ge(max_ready, count)
                for i in range(4):
                    dst = qs[ROWS:STACK, j, :].bitcast(F32).rearrange("l (t i c) -> l t i c", i=4, c=32)[:, :, i, :]
                    sp.dma_start(dst, max_rows[32 * i:32 * i + 2 * NT, j % 2, :]).then_inc(max_loaded[j], 16)

            def store_sums(h, j):
                sp.wait_ge(sums0_out, h + 2)
                sp.wait_ge(sums1_out, h + 2)
                for n in range(3):
                    sp.dma_start(dram["sums"][n][bass.ds(h * HD, HD), :], sums[n * HD:(n + 1) * HD, j % 2, :]
                                 ).then_inc(stored[j % 2], 16)

            def load_sums(k, count):
                for st in stored:
                    sp.wait_ge(st, 48 * count + 48)
                for n in range(3):
                    sp.dma_start(mem["y_sums"][:, n, k, :], dram["sums"][n][k * P:(k + 1) * P, :]).then_inc(y_loaded, 16)

            if rope:
                sp.dma_start(tables, dram["rope"]).then_inc(tables_in, 16)
            write_parts(0)
            write_parts(1)
            sp.wait_ge(written[0], 16)
            sp.wait_ge(written[1], 16)
            for h in range(4):
                load_stacks(h, h)
            write_parts(2)
            write_parts(3)
            load_max(0, 0, 1)
            load_max(1, 1, 2)
            sp.wait_ge(written[2], 16)
            sp.wait_ge(written[3], 16)
            with sp.Fori(0, H // 4 - 1) as i:
                for j in range(4):
                    load_max(i * 4 + (j + 2), (j + 2) % 4, i * 4 + (j + 3))
                    sp.wait_ge(pv_ready, i * 4 + (j + 1))
                    load_stacks(i * 4 + (j + 4), j)
                    store_sums(i * 4 + j, j)
            load_sums(0, 6)
            for j in range(4):
                if j < 2:
                    load_max(H - 2 + j, j + 2, H - 1 + j)
                store_sums(H - 4 + j, j)
            load_sums(1, 8)
            sp.wait_ge(y_loaded, 6 * 16)

        @block.tensor
        def _(pe):
            def unit(u):
                t, m, n = units[u]
                if u >= 2:
                    pe.wait_ge(unit_out, u - 1)
                cols = slice(n * HALF, (n + 1) * HALF)
                for r, name in enumerate([t, t + "p"][:1 + rope]):
                    for k in range(KD):
                        w = slice(k * D + m * P, k * D + (m + 1) * P)
                        mm = product(pe, bank(2 * (u % 2) + r),
                                     (mem["wa_h"][:, w_at[name], w], mem["wa_l"][:, w_at[name], w]),
                                     (mem["xt_h"][:, k, cols], mem["xt_l"][:, k, cols]), k == 0, k == KD - 1)
                mm.then_inc(unit_ready, 1)

            def project_v(t):
                if t >= 2:
                    pe.wait_ge(v_out, t - 1)
                for k in range(KD):
                    toks, w = slice(t * P, (t + 1) * P), slice(k * D, (k + 1) * D)
                    mm = product(pe, bank(4 + t % 2, 0, D), (mem["xt_h"][:, k, toks], mem["xt_l"][:, k, toks]),
                                 (mem["wa_h"][:, w_at["v"], w], mem["wa_l"][:, w_at["v"], w]), k == 0, k == KD - 1)
                mm.then_inc(v_ready, 1)

            def score_tile(h, j, qt, loads, which=(0, 1)):
                if qt == 0 and which[0] == 0:
                    pe.wait_ge(loaded[j], 80 * loads)
                for n, (a, b) in enumerate(pieces(qt)):
                    if n not in which:
                        continue
                    at = piece_number(qt) + n
                    pe.wait_ge(scores_free, h * PIECES + (at + 1))
                    diagonal = causal and b == (qt + 1) * P
                    mm = pe.matmul(bank(4 + at % 2, 0, b - a), qs[0:STACK, j, qt * P:(qt + 1) * P], ks[0:STACK, j, a:b],
                                   start=True, stop=True)
                    if diagonal:
                        mm = pe.matmul(bank(4 + at % 2, b - a - P, P), mem["masks"][:, C_ID:C_ID + P],
                                       mem["masks"][:, C_CM:C_CM + P], start=False, stop=True, skip_group_check=True)
                    mm.then_inc(scores_ready, 1)

            def transposed_scores(j, kt, loads):
                if kt == 0:
                    pe.wait_ge(max_loaded[j], 64 * loads)
                first = kt * P if causal else 0
                base = 2 * (kt % 2) * HALF
                for a, b in ((first, HALF), (max(first, HALF), T)):
                    if a >= b:
                        continue
                    diagonal = causal and a == first
                    mm = pe.matmul(ps[:, base + a:base + b], ks[0:STACK, j, kt * P:(kt + 1) * P], qs[0:STACK, j, a:b],
                                   start=True, stop=True)
                    if diagonal:
                        mm = pe.matmul(ps[:, base + a:base + a + P], mem["masks"][:, C_ID:C_ID + P],
                                       mem["masks"][:, C_CMT:C_CMT + P], start=False, stop=True, skip_group_check=True)
                mm.then_inc(st_ready, 1)

            def times_v(h, j, kt):
                if kt == 0:
                    pe.wait_ge(v_copied, h + 1)
                if kt in on["pool"]:
                    pe.wait_ge(p_low_ready["pool"], h * len(on["pool"]) + (on["pool"].index(kt) + 1))
                v = mem["v_split" if kt in split else "v_full"][:, j, kt, :]
                first = kt * P if causal else 0
                for n in range(first // HALF, 2):
                    if kt == 0:
                        pe.wait_ge((sums0_out, sums1_out)[n], h + 1)
                    if kt in on["dve"]:
                        pe.wait_ge(p_low_ready["dve"], h * (2 * len(on["dve"])) + (2 * on["dve"].index(kt) + n + 1))
                    start = max(first, n * HALF)
                    for i, p in enumerate((p_high, p_low) if kt in split else (probs,)):
                        mm = pe.matmul(sums_bank(n, start - n * HALF), v, p[:, kt % 4, start:(n + 1) * HALF],
                                       start=kt == 0 and i == 0, stop=True, skip_group_check=True)
                if kt == NT - 1:
                    mm.then_inc(pv_ready, 1)

            def head(h, j, loads, max_next, ahead, next_head, last_head=True):
                def others(kt, which):
                    if kt < NT - LEAD and next_head:
                        score_tile(h + 1, (j + 1) % 4, kt + LEAD, None, which)
                    elif kt >= NT - LEAD and ahead is not None:
                        score_tile(h + 2, (j + 2) % 4, kt - (NT - LEAD), ahead, which)

                for kt in range(NT):
                    others(kt, (0,))
                    if kt >= 2:
                        times_v(h, j, kt - 2)
                    elif last_head:
                        times_v(h - 1, (j - 1) % 4, kt - 2 + NT)
                    pe.wait_ge(exp_done, h * NT + (kt + 1))
                    if kt < NT - 2:
                        transposed_scores(j, kt + 2, loads)
                    elif next_head:
                        transposed_scores((j + 1) % 4, kt + 2 - NT, max_next)
                    others(kt, (1,))

            for u in range(4):
                unit(u)
            for t in range(NT):
                project_v(t)
            pe.wait_ge(v_out, NT)
            for n in range(4):
                unit(4 + n)
                score_tile(0, 0, 2 * n, 1)
                score_tile(0, 0, 2 * n + 1, 1)
            for qt in range(LEAD):
                score_tile(1, 1, qt, 1)
            pe.wait_ge(unit_out, 8)
            transposed_scores(0, 0, 1)
            transposed_scores(0, 1, 1)
            for j in range(4):
                head(j, j, 1, 1 + (j == 3), 1 + (j >= 2), True, j > 0)
            with pe.Fori(1, H // 4 - 1) as i:
                for j in range(4):
                    head(i * 4 + j, j, i + 1, i + (1 + (j == 3)), i + (1 + (j >= 2)), True)
            for j in range(4):
                head(H - 4 + j, j, H // 4, H // 4, H // 4 if j < 2 else None, j < 3)
            times_v(H - 1, 3, NT - 2)
            times_v(H - 1, 3, NT - 1)

        @block.scalar
        def _(act):
            for u, (t, m, n) in enumerate(units):
                g = u // 2
                act.wait_ge(unit_out, u + 1)
                if g >= 2 and n == 0:
                    act.wait_ge(written[g - 2], 16)
                act.activation(parts[:, g % 2, 0, n * HALF:(n + 1) * HALF], flat[:, u % 2, :], ACT.Copy
                               ).then_inc(high_ready, 1)
                if rope and u == 3:
                    for tile in range(NT):
                        act.wait_ge(v_ready, tile + 1)
                        act.activation(v_all[:, tile, :], bank(4 + tile % 2, 0, D), ACT.Copy).then_inc(v_out, 1)

            def exps(h, tiles):
                for kt in tiles:
                    first = kt * P if causal else 0
                    base = 2 * (kt % 2) * HALF
                    act.wait_ge(st_ready, h * NT + (kt + 1))
                    act.activation(probs[:, kt % 4, first:T], ps[:, base + first:base + T], ACT.Exp
                                   ).then_inc(exp_done, 1)
                    if kt in split:
                        act.wait_ge(exp_done, h * NT + (kt + 1))
                        act.activation(p_high[:, kt % 4, first:T], probs[:, kt % 4, first:T], ACT.Copy
                                       ).then_inc(p_high_ready, 1)

            def take_sums(h, j, stores):
                act.wait_ge(pv_ready, h + 1)
                act.wait_ge(stored[j % 2], stores)
                act.activation(sums[:, j % 2, 0:HALF], sums_bank(0), ACT.Copy).then_inc(sums0_out, 1)

            def heads(i, first=False):
                for j in range(4):
                    exps(i * 4 + j, range(2))
                    if j or not first:
                        take_sums(i * 4 + (j - 1), (j - 1) % 4, i * 96 + 48 * ((j - 1) // 2 + 1))
                    exps(i * 4 + j, range(2, NT))

            act.wait_ge(low_ready, 8)
            act.wait_ge(written[2], 16)
            act.wait_ge(written[3], 16)
            heads(0, True)
            with act.Fori(1, H // 4) as i:
                heads(i)
            take_sums(H - 1, 3, 48 * (H // 2))

        @block.gpsimd
        def _(pool):
            def copy_v(h, j):
                full = mem["v_full"][:, j, :, 0:HD]
                high, low = mem["v_split"][:, j, :, 0:HD], mem["v_split"][:, j, :, HD:2 * HD]
                pool.tensor_copy(full, v_all[:, :, bass.ds(h * HD, HD)]).then_inc(v_step, 1)
                pool.tensor_copy(high, v_all[:, :, bass.ds(h * HD, HD)]).then_inc(v_step, 1)
                pool.wait_ge(v_step, h * 2 + 2)
                pool.tensor_tensor(low, full, high.bitcast(F32), ALU.subtract).then_inc(v_copied, 1)

            def lows(h, j, prepare):
                for n, kt in enumerate(on["pool"]):
                    first = kt * P if causal else 0
                    pool.wait_ge(p_high_ready, h * len(split) + (split.index(kt) + 1))
                    at = slice(first, T)
                    pool.tensor_tensor(p_low[:, kt % 4, at], probs[:, kt % 4, at], p_high[:, kt % 4, at].bitcast(F32),
                                       ALU.subtract).then_inc(p_low_ready["pool"], 1)
                    if n == len(on["pool"]) - 2 and prepare:
                        pool.wait_ge(pv_ready, h)
                        copy_v(h + 3, (j + 3) % 4)

            def unit_low(u):
                g, n = u // 2, u % 2
                high, low = [parts[:, g % 2, l, n * HALF:(n + 1) * HALF] for l in range(2)]
                pool.wait_ge(high_ready, u + 1)
                pool.tensor_tensor(low, flat[:, u % 2, :], high.bitcast(F32), ALU.subtract).then_inc(low_ready, 1)

            for u in range(4):
                unit_low(u)
            for u in range(4, 8):
                pool.wait_ge(written[u // 2 - 2], 16)
                unit_low(u)
            pool.wait_ge(v_out, NT)
            for h in range(4):
                copy_v(h, h)
            for j in range(4):
                lows(j, j, j > 0)
            with pool.Fori(1, H // 4 - 1) as i:
                for j in range(4):
                    lows(i * 4 + j, j, True)
            for j in range(4):
                lows(H - 4 + j, j, j == 0)

        @block.vector
        def _(dve):
            def unit_to_flat(u):
                t, m, n = units[u]
                dve.wait_ge(unit_ready, u + 1)
                if u >= 2:
                    dve.wait_ge(low_ready, u - 1)
                src, dst = bank(2 * (u % 2)), flat[:, u % 2, :]
                scale = HD ** -0.5 if t == "q" else 1.0
                if not rope:
                    bias = mem["bias_qk"][:, 2 * (t == "k") + m:2 * (t == "k") + m + 1]
                    dve.tensor_scalar(dst, src, bias, scale, ALU.add, ALU.mult).then_inc(unit_out, 1)
                else:
                    cols = slice(n * HALF, (n + 1) * HALF)
                    if u == 0:
                        dve.wait_ge(tables_in, 16)
                    dve.scalar_tensor_tensor(out=dst, in0=src, scalar=scale, in1=tables[:, 0, cols],
                                             op0=ALU.mult, op1=ALU.mult).then_inc(rope_step, 1)
                    dve.scalar_tensor_tensor(out=turned[:, u % 2, :], in0=bank(2 * (u % 2) + 1), scalar=scale,
                                             in1=tables[:, 1, cols], op0=ALU.mult, op1=ALU.mult
                                             ).then_inc(rope_step, 1)
                    dve.wait_ge(rope_step, 2 * u + 2)
                    dve.tensor_tensor(dst, dst, turned[:, u % 2, :], ALU.add).then_inc(unit_out, 1)
            def v_to_sbuf(t):
                dve.wait_ge(v_ready, t + 1)
                dve.tensor_tensor(v_all[:, t, :], bank(4 + t % 2, 0, D), mem["bias_v"][:, :], ALU.add).then_inc(v_out, 1)

            def tile_max(h, qt, which=(0, 1)):
                for n, (a, b) in enumerate(pieces(qt)):
                    if n not in which:
                        continue
                    at = piece_number(qt) + n
                    dve.wait_ge(scores_ready, h * PIECES + (at + 1))
                    dve.tensor_reduce(mem["row_max"][:, qt, n:n + 1], bank(4 + at % 2, 0, b - a), AX.X, ALU.max
                                      ).then_inc(scores_free, 1)

            def finish_max(h, j, loads, buf):
                dve.wait_ge(scores_free, h * PIECES + (2 + PIECES))
                dve.tensor_reduce(negmax[:, :], mem["row_max"][:, :, :], AX.X, ALU.max, negate=True).then_inc(fin, 1)
                dve.wait_ge(fin, h * 3 + 1)
                dve.tensor_copy(mem["max_parts"][:, 0:NT], negmax[:, :]).then_inc(fin, 1)
                dve.wait_ge(fin, h * 3 + 2)
                dve.tensor_tensor(mem["max_parts"][:, NT:2 * NT], negmax[:, :], mem["max_parts"][:, 0:NT].bitcast(F32),
                                  ALU.subtract).then_inc(fin, 1)
                dve.wait_ge(fin, h * 3 + 3)
                if loads is not None:
                    dve.wait_ge(max_loaded[buf], loads)
                dve.transpose(max_rows[:, j % 2, :], mem["max_parts"][:, :].bitcast(F32)).then_inc(max_ready, 1)

            def take_sums(h, j, stores):
                dve.wait_ge(pv_ready, h + 1)
                dve.wait_ge(stored[j % 2], stores)
                dve.tensor_copy(sums[:, j % 2, HALF:T], sums_bank(1)).then_inc(sums1_out, 1)

            def head(i, j, first=False, following=2):
                h = i * 4 + j
                for kt in range(NT):
                    if kt == 1 and (j or not first):
                        take_sums(i * 4 + (j - 1), (j - 1) % 4, i * 96 + 48 * ((j - 1) // 2 + 1))
                    for n in range(2):
                        if kt < NT - LEAD and following >= 1:
                            tile_max(i * 4 + (j + 1), kt + LEAD, (n,))
                        elif kt >= NT - LEAD and following >= 2:
                            tile_max(i * 4 + (j + 2), kt - (NT - LEAD), (n,))
                        if kt in on["dve"]:
                            low(h, kt, n)
                    if kt == NT - LEAD - 1 and following >= 1:
                        finish_max(i * 4 + (j + 1), (j + 1) % 4, None if first and j == 0 else i * 64 + 64 * (j > 0), (j - 1) % 4)

            def low(h, kt, n):
                at = slice(max(n * HALF, kt * P if causal else 0), (n + 1) * HALF)
                if n == 0:
                    dve.wait_ge(p_high_ready, h * len(split) + (split.index(kt) + 1))
                dve.tensor_tensor(p_low[:, kt % 4, at], probs[:, kt % 4, at], p_high[:, kt % 4, at].bitcast(F32),
                                  ALU.subtract).then_inc(p_low_ready["dve"], 1)

            for c, (done, n) in enumerate(((scores_free, 2), (sums0_out, 1), (sums1_out, 1), *((st, 48) for st in stored))):
                dve.memset(negmax[:, c:c + 1], 0.0).then_inc(done, n)
            for u in range(4):
                unit_to_flat(u)
            if not rope:
                for t in range(NT):
                    v_to_sbuf(t)
            for n in range(4):
                unit_to_flat(4 + n)
                tile_max(0, 2 * n)
                tile_max(0, 2 * n + 1)
            finish_max(0, 0, None, 0)
            for qt in range(LEAD):
                tile_max(1, qt)
            for j in range(4):
                head(0, j, True)
            with dve.Fori(1, H // 4 - 1) as i:
                for j in range(4):
                    head(i, j)
            for j in range(4):
                head(H // 4 - 1, j, following=3 - j)
                if j == 2:
                    dve.wait_ge(y_loaded, 3 * 16)
                    dve.reciprocal(mem["y_sums"][:, 2, 0, :], mem["y_sums"][:, 2, 0, :]).then_inc(recip_ready, 1)
            take_sums(H - 1, 3, 48 * (H // 2))


def norm_statistics(dve, stats, mv, rows, t, step, count):
    dve.bn_stats(stats[:, t % 2, :], rows).then_inc(step, 1)
    dve.wait_ge(step, count + 1)
    dve.bn_aggr(mv[:, t, :], stats[:, t % 2, :]).then_inc(step, 1)
    return count + 2


def output_projection(nc, mem, layer):
    ps, x = mem["ps"], mem["x"]
    y_sums, y_low_sums, exp_sums = [mem["y_sums"][:, n, :, :] for n in range(3)]
    w_o = 3 if layer == 0 else 9
    with Stage(nc) as ctx:
        sem = lambda name: ctx.semaphore(f"{name}_{layer}")
        sb = lambda name, shape, dt=F32: ctx.enter_context(nc.sbuf_tensor(f"{name}_{layer}", shape, dt))
        yt_h, yt_l = sb("yt_h", [P, KD, T], F32R), sb("yt_l", [P, KD, T], F32R)
        sums_added, recip_ready = sem("sums_added"), sem("recip_ready")
        y_ready, high_ready, low_ready = sem("y_ready"), sem("y_high"), sem("y_low")
        o_ready, o_out, biased = sem("o_ready"), sem("o_out"), sem("x_biased")
        norm = NormStage(nc, ctx, mem, f"a{layer}")
        block = ctx.enter_context(nc.Block())

        def quarter(a, n):
            k, g = n % 2, n // 2
            return a[:, k, g * HALF:(g + 1) * HALF]

        def out_bank(t):
            return ps[:, (2 + t % 2) * HALF:(2 + t % 2) * HALF + D]

        @block.tensor
        def _(pe):
            for t in range(NT):
                if t % 4 == 0:
                    pe.wait_ge(low_ready, 2 + 2 * (t // 4))
                if t >= 2:
                    pe.wait_ge(o_out, t - 1)
                toks = slice(t * P, (t + 1) * P)
                for k in range(KD):
                    w = slice(k * D, (k + 1) * D)
                    mm = product(pe, out_bank(t), (yt_h[:, k, toks], yt_l[:, k, toks]),
                                 (mem["wa_h"][:, w_o, w], mem["wa_l"][:, w_o, w]), k == 0, k == KD - 1)
                mm.then_inc(o_ready, 1)
            norm.tensor(pe)

        @block.scalar
        def _(act):
            for n in range(4):
                act.wait_ge(y_ready, n + 1)
                act.activation(quarter(yt_h, n), quarter(y_sums, n), ACT.Copy).then_inc(high_ready, 1)
            norm.scalar(act)

        @block.gpsimd
        def _(pool):
            for n in range(4):
                pool.tensor_tensor(quarter(y_sums, n), quarter(y_sums, n), quarter(y_low_sums, n), ALU.add).then_inc(sums_added, 1)
            if layer == 0:
                for t in range(NT):
                    pool.tensor_tensor(x[:, t, :], x[:, t, :], mem["bias_o"][:, :], ALU.add).then_inc(biased, 1)

        @block.vector
        def _(dve):
            for g in range(2):
                dve.reciprocal(quarter(exp_sums, 2 * g + 1), quarter(exp_sums, 2 * g + 1)).then_inc(recip_ready, 1)
                for n in (2 * g, 2 * g + 1):
                    dve.wait_ge(sums_added, n + 1)
                    if n % 2:
                        dve.wait_ge(recip_ready, g + 1)
                    dve.tensor_tensor(quarter(y_sums, n), quarter(y_sums, n), quarter(exp_sums, n), ALU.mult).then_inc(y_ready, 1)
                for n in (2 * g, 2 * g + 1):
                    dve.wait_ge(high_ready, n + 1)
                    dve.tensor_tensor(quarter(yt_l, n), quarter(y_sums, n), quarter(yt_h, n).bitcast(F32), ALU.subtract
                                      ).then_inc(low_ready, 1)
            for t in range(NT):
                dve.wait_ge(o_ready, t + 1)
                if layer == 0:
                    dve.wait_ge(biased, t + 1)
                dve.tensor_tensor(x[:, t, :], out_bank(t), x[:, t, :], ALU.add).then_inc(o_out, 1)
                dve.wait_ge(o_out, t + 1)
                norm.statistics(dve, t)
            norm.vector(dve)


class NormStage:

    def __init__(self, nc, ctx, mem, name, last=False):
        self.mem, self.last, self.count = mem, last, 0
        sb = lambda n, shape: ctx.enter_context(nc.sbuf_tensor(f"{n}_{name}", shape, F32))
        sem = lambda n: ctx.semaphore(f"{n}_{name}")
        self.stats, self.mv = sb("stats", [P, 2, 6]), sb("mv", [P, NT, 2])
        self.std, self.rstd = sb("std", [P, NT]), sb("rstd", [P, NT])
        self.step, self.std_ready, self.rstd_ready = sem("stat_step"), sem("std_ready"), sem("rstd_ready")
        self.normed, self.turned, self.high, self.low = sem("normed"), sem("x_turned"), sem("xt_high"), sem("xt_low")

    def bank(self, n):
        return self.mem["ps"][:, (4 + n) * HALF:(5 + n) * HALF]

    def statistics(self, dve, t):
        self.count = norm_statistics(dve, self.stats, self.mv, self.mem["x"][:, t, :], t, self.step, self.count)

    def scalar(self, act):
        act.wait_ge(self.step, 2 * NT)
        act.activation(self.std[:, :], self.mv[:, :, 1], ACT.Sqrt, bias=self.mem["eps"][:, :]).then_inc(self.std_ready, 1)
        if not self.last:
            for n in range(4):
                k, g = n % 2, n // 2
                act.wait_ge(self.turned, n + 1)
                act.activation(self.mem["xt_h"][:, k, g * HALF:(g + 1) * HALF], self.bank(n), ACT.Copy).then_inc(self.high, 1)

    def tensor(self, pe):
        for n in range(4):
            k, g = n % 2, n // 2
            pe.wait_ge(self.normed, 4 * (g + 1))
            for t in range(4):
                mm = pe.transpose(self.bank(n)[:, t * P:(t + 1) * P], self.mem["x"][:, 4 * g + t, k * P:(k + 1) * P],
                                  self.mem["consts"][:, C_ID:C_ID + P])
            mm.then_inc(self.turned, 1)

    def vector(self, dve):
        x = self.mem["x"]
        dve.wait_ge(self.std_ready, 1)
        dve.reciprocal(self.rstd[:, :], self.std[:, :]).then_inc(self.rstd_ready, 1)
        dve.wait_ge(self.rstd_ready, 1)
        for t in range(NT):
            dve.tensor_scalar(x[:, t, :], x[:, t, :], self.mv[:, t, 0:1], self.rstd[:, t:t + 1],
                              ALU.subtract, ALU.mult).then_inc(self.normed, 1)
        if not self.last:
            for n in range(4):
                k, g = n % 2, n // 2
                dve.wait_ge(self.high, n + 1)
                xh = self.mem["xt_h"][:, k, g * HALF:(g + 1) * HALF]
                dve.tensor_tensor(self.mem["xt_l"][:, k, g * HALF:(g + 1) * HALF], self.bank(n), xh.bitcast(F32),
                                  ALU.subtract).then_inc(self.low, 1)


class TopTwo:

    def __init__(self, nc, ctx, mem, name, experts, tri):
        self.mem, self.e, self.tri = mem, experts, tri
        sb = lambda n, shape: ctx.enter_context(nc.sbuf_tensor(f"{n}_{name}", shape, F32))
        sem = lambda n: ctx.semaphore(f"{n}_{name}")
        e = experts
        self.logits = sb("logits", [P, NT, e])
        self.above, self.equal = sb("above", [P, NT, e * e]), sb("equal", [P, NT, e * e])
        self.chosen, self.shifted, self.expd = sb("chosen", [P, NT, e]), sb("shifted", [P, NT, e]), sb("expd", [P, NT, e])
        self.top, self.total, self.inv = sb("top", [P, NT]), sb("total", [P, NT]), sb("inv", [P, NT])
        self.weights = sb("weights", [P, NT, e])
        self.step, self.shift_ready, self.exp_ready, self.done = sem("route_step"), sem("shift_ready"), sem("rexp_ready"), sem("routed")

    def scalar(self, act):
        act.wait_ge(self.shift_ready, 1)
        act.activation(self.expd[:, :, :], self.shifted[:, :, :], ACT.Exp).then_inc(self.exp_ready, 1)

    def vector(self, dve):
        e, step = self.e, self.step
        flat = lambda a: a[:, :, :].rearrange("p t (e j) -> p t e j", j=e)
        mine = self.logits[:, :, :].unsqueeze(3).broadcast_to([P, NT, e, e])
        other = self.logits[:, :, :].unsqueeze(2).broadcast_to([P, NT, e, e])
        tri = self.mem["consts"][:, self.tri:self.tri + e * e].unsqueeze(1).broadcast_to([P, NT, e * e])
        wide = lambda a: a[:, :].unsqueeze(2).broadcast_to([P, NT, e])
        dve.tensor_reduce(self.top[:, :], self.logits[:, :, :], AX.X, ALU.max).then_inc(step, 1)
        dve.tensor_tensor(flat(self.above), other, mine, ALU.is_gt).then_inc(step, 1)
        dve.tensor_tensor(flat(self.equal), other, mine, ALU.is_equal).then_inc(step, 1)
        dve.wait_ge(step, 1)
        dve.tensor_tensor(self.shifted[:, :, :], self.logits[:, :, :], wide(self.top), ALU.subtract).then_inc(self.shift_ready, 1)
        dve.wait_ge(step, 3)
        dve.tensor_tensor(self.equal[:, :, :], self.equal[:, :, :], tri, ALU.mult).then_inc(step, 1)
        dve.wait_ge(step, 4)
        dve.tensor_tensor(self.above[:, :, :], self.above[:, :, :], self.equal[:, :, :], ALU.add).then_inc(step, 1)
        dve.wait_ge(step, 5)
        dve.tensor_reduce(self.chosen[:, :, :], flat(self.above), AX.X, ALU.add).then_inc(step, 1)
        dve.wait_ge(step, 6)
        dve.tensor_scalar(self.chosen[:, :, :], self.chosen[:, :, :], 2.0, None, ALU.is_lt).then_inc(step, 1)
        dve.wait_ge(step, 7)
        dve.wait_ge(self.exp_ready, 1)
        dve.tensor_tensor(self.expd[:, :, :], self.expd[:, :, :], self.chosen[:, :, :], ALU.mult).then_inc(step, 1)
        dve.wait_ge(step, 8)
        dve.tensor_reduce(self.total[:, :], self.expd[:, :, :], AX.X, ALU.add).then_inc(step, 1)
        dve.wait_ge(step, 9)
        dve.reciprocal(self.inv[:, :], self.total[:, :]).then_inc(step, 1)
        dve.wait_ge(step, 10)
        dve.tensor_tensor(self.weights[:, :, :], self.expd[:, :, :], wide(self.inv), ALU.mult).then_inc(self.done, 1)


def mixture_0(nc, mem, dram):
    ps, x, xt = mem["ps"], mem["x"], (mem["xt_h"], mem["xt_l"])
    CW = 2 * KD * I0 + D
    with Stage(nc) as ctx:
        sem = lambda name: ctx.semaphore(f"{name}_m0")
        sb = lambda name, shape, dt=F32: ctx.enter_context(nc.sbuf_tensor(f"{name}_m0", shape, dt))
        raw = sb("w_chunk", [P, 2, CW])
        w_h, w_l = sb("w_chunk_h", [P, 2, CW], F32R), sb("w_chunk_l", [P, 2, CW], F32R)
        r_raw = sb("r_raw", [P, KD * NR0])
        r_h, r_l = sb("r_h", [P, KD * NR0], F32R), sb("r_l", [P, KD * NR0], F32R)
        gated = sb("gated", [P, 2, HALF])
        hidden = sb("hidden", [P, 2, HALF])
        h_h, h_l = sb("h_h", [P, 2, T], F32R), sb("h_l", [P, 2, T], F32R)
        share = sb("share", [P, NT, CH])
        gate = sb("gate", [P, NT])
        loaded = [sem("chunk_loaded0"), sem("chunk_loaded1")]
        r_loaded, r_high, r_low = sem("r_loaded"), sem("r_high"), sem("r_low")
        up_high, up_low, dn_high, dn_low = sem("up_high"), sem("up_low"), sem("dn_high"), sem("dn_low")
        UPW, DNW = slice(0, 2 * KD * I0), slice(2 * KD * I0, CW)
        logits_ready, copied, gate_exp, gate_step, shared_ready = sem("logits_ready"), sem("copied"), sem("gate_exp"), sem("gate_step"), sem("shared_ready")
        up_ready, silu_ready, hidden_ready, hh_ready, hl_ready = sem("up_ready"), sem("silu_ready"), sem("hidden_ready"), sem("hh_ready"), sem("hl_ready")
        down_ready, added = sem("down_ready"), sem("added")
        top = TopTwo(nc, ctx, mem, "m0", E0, C_T8)
        norm = NormStage(nc, ctx, mem, "m0")
        block = ctx.enter_context(nc.Block())

        G, U = 0, 2

        def bank(b):
            return ps[:, b * HALF:(b + 1) * HALF]

        def down_bank(t):
            return ps[:, (4 + t // 2) * HALF + (t % 2) * D:(4 + t // 2) * HALF + (t % 2 + 1) * D]

        @block.sync
        def _(sp):
            sp.dma_start(r_raw[:, :], dram["w_router0"]).then_inc(r_loaded, 16)
            for c in range(2):
                sp.dma_start(raw[:, c, :], dram["w_chunks0"][c]).then_inc(loaded[c], 16)
            with sp.Fori(0, CH // 2 - 1) as i:
                for b in range(2):
                    sp.wait_ge(dn_low, i * 2 + (b + 1))
                    sp.dma_start(raw[:, b, :], dram["w_chunks0"][bass.ds(i * 2 + (b + 2), 1), :, :]
                                 .rearrange("c p n -> (c p) n")).then_inc(loaded[b], 16)

        @block.gpsimd
        def _(pool):
            def low(c, b, w, high, done):
                pool.wait_ge(high, c + 1)
                pool.tensor_tensor(w_l[:, b, w], raw[:, b, w], w_h[:, b, w].bitcast(F32), ALU.subtract).then_inc(done, 1)

            low(0, 0, UPW, up_high, up_low)
            with pool.Fori(0, CH // 2 - 1) as i:
                for b in range(2):
                    low(i * 2 + (b + 1), 1 - b, UPW, up_high, up_low)
                    low(i * 2 + b, b, DNW, dn_high, dn_low)
            low(CH - 1, 1, UPW, up_high, up_low)
            low(CH - 2, 0, DNW, dn_high, dn_low)
            low(CH - 1, 1, DNW, dn_high, dn_low)

        @block.tensor
        def _(pe):
            pe.wait_ge(r_low, 1)
            for t in range(NT):
                toks = slice(t * P, (t + 1) * P)
                for k in range(KD):
                    r = slice(k * NR0, (k + 1) * NR0)
                    mm = product(pe, ps[:, 4 * HALF + t * NR0:4 * HALF + (t + 1) * NR0],
                                 (xt[0][:, k, toks], xt[1][:, k, toks]), (r_h[:, r], r_l[:, r]), k == 0, k == KD - 1)
            mm.then_inc(logits_ready, 1)

            def up(c, b):
                pe.wait_ge(up_low, c + 1)
                for n in range(2):
                    pe.wait_ge(hidden_ready, c * 2 + (n + 1))
                    cols = slice(n * HALF, (n + 1) * HALF)
                    for base, off in ((G, 0), (U, KD * I0)):
                        for k in range(KD):
                            w = slice(off + k * I0, off + (k + 1) * I0)
                            mm = product(pe, bank(base + n), (w_h[:, b, w], w_l[:, b, w]),
                                         (xt[0][:, k, cols], xt[1][:, k, cols]), k == 0, k == KD - 1)
                    mm.then_inc(up_ready, 1)

            def down(c, b):
                pe.wait_ge(hl_ready, c * 2 + 2)
                pe.wait_ge(dn_low, c + 1)
                pe.wait_ge(added, c * NT + NT)
                w = slice(2 * KD * I0, CW)
                for t in range(NT):
                    toks = slice(t * P, (t + 1) * P)
                    mm = product(pe, down_bank(t), (h_h[:, b, toks], h_l[:, b, toks]), (w_h[:, b, w], w_l[:, b, w]),
                                 True, True)
                    mm.then_inc(down_ready, 1)

            up(0, 0)
            with pe.Fori(0, CH // 2 - 1) as i:
                for b in range(2):
                    up(i * 2 + (b + 1), 1 - b)
                    down(i * 2 + b, b)
            up(CH - 1, 1)
            down(CH - 2, 0)
            down(CH - 1, 1)
            norm.tensor(pe)

        @block.scalar
        def _(act):
            def split_up(c, b, loads):
                act.wait_ge(loaded[b], 16 * loads)
                act.activation(w_h[:, b, UPW], raw[:, b, UPW], ACT.Copy).then_inc(up_high, 1)

            def split_down(c, b):
                act.activation(w_h[:, b, DNW], raw[:, b, DNW], ACT.Copy).then_inc(dn_high, 1)

            def silu(c, b):
                for n in range(2):
                    act.wait_ge(up_ready, c * 2 + (n + 1))
                    act.wait_ge(hidden_ready, c * 2 + (n + 1))
                    act.activation(gated[:, n, :], bank(G + n), ACT.Silu).then_inc(silu_ready, 1)
                    act.wait_ge(hidden_ready, c * 2 + (n + 3))
                    act.activation(h_h[:, b, n * HALF:(n + 1) * HALF], hidden[:, n, :], ACT.Copy).then_inc(hh_ready, 1)

            act.wait_ge(r_loaded, 16)
            act.activation(r_h[:, :], r_raw[:, :], ACT.Copy).then_inc(r_high, 1)
            split_up(0, 0, 1)
            top.scalar(act)
            act.wait_ge(copied, 2)
            act.activation(gate[:, :], gate[:, :], ACT.Exp, scale=-1.0).then_inc(gate_exp, 1)
            split_up(1, 1, 1)
            split_down(0, 0)
            silu(0, 0)
            act.wait_ge(up_ready, 2)
            split_up(2, 0, 2)
            split_down(1, 1)
            silu(1, 1)
            with act.Fori(1, CH // 2 - 1) as i:
                for b in range(2):
                    act.wait_ge(up_ready, i * 4 + 2 * b)
                    split_up(i * 2 + (b + 1), 1 - b, i + (1 + b))
                    act.wait_ge(down_ready, i * (2 * NT) + (b - 1) * NT)
                    split_down(i * 2 + b, b)
                    silu(i * 2 + b, b)
            act.wait_ge(up_ready, 2 * CH - 4)
            split_up(CH - 1, 1, CH // 2)
            act.wait_ge(down_ready, (CH - 3) * NT)
            split_down(CH - 2, 0)
            silu(CH - 2, 0)
            act.wait_ge(down_ready, (CH - 2) * NT)
            split_down(CH - 1, 1)
            silu(CH - 1, 1)
            norm.scalar(act)

        @block.vector
        def _(dve):
            def multiply(c, b):
                for n in range(2):
                    dve.wait_ge(silu_ready, c * 2 + (n + 1))
                    dve.tensor_tensor(hidden[:, n, :], gated[:, n, :], bank(U + n), ALU.mult).then_inc(hidden_ready, 1)
                    dve.wait_ge(hh_ready, c * 2 + (n + 1))
                    cols = slice(n * HALF, (n + 1) * HALF)
                    dve.tensor_tensor(h_l[:, b, cols], hidden[:, n, :], h_h[:, b, cols].bitcast(F32), ALU.subtract
                                      ).then_inc(hl_ready, 1)

            def add_up(c, b):
                for t in range(NT):
                    dve.wait_ge(down_ready, c * NT + (t // 2 * 2 + 2))
                    dve.wait_ge(added, c * NT + (t + 1))
                    dve.scalar_tensor_tensor(out=x[:, t, :], in0=down_bank(t), scalar=share[:, t, bass.ds(c, 1)],
                                             in1=x[:, t, :], op0=ALU.mult, op1=ALU.add).then_inc(added, 1)

            dve.wait_ge(r_high, 1)
            dve.tensor_tensor(r_l[:, :], r_raw[:, :], r_h[:, :].bitcast(F32), ALU.subtract).then_inc(r_low, 1)
            dve.memset(hidden[:, 0, 0:1], 0.0).then_inc(hidden_ready, 2)
            dve.memset(hidden[:, 1, 0:1], 0.0).then_inc(copied, 1)
            dve.wait_ge(logits_ready, 1)
            logits = ps[:, 4 * HALF:4 * HALF + NT * NR0].rearrange("p (t e) -> p t e", e=NR0)
            dve.tensor_copy(gate[:, :], logits[:, :, E0]).then_inc(copied, 1)
            dve.tensor_copy(top.logits[:, :, :], logits[:, :, 0:E0]).then_inc(copied, 1)
            dve.wait_ge(copied, 3)
            dve.memset(share[:, :, :], 0.0).then_inc(added, NT)
            top.vector(dve)
            dve.wait_ge(gate_exp, 1)
            dve.tensor_scalar(gate[:, :], gate[:, :], 1.0, None, ALU.add).then_inc(gate_step, 1)
            dve.wait_ge(gate_step, 1)
            dve.reciprocal(gate[:, :], gate[:, :]).then_inc(gate_step, 1)
            dve.wait_ge(gate_step, 2)
            dve.wait_ge(added, NT)
            dve.wait_ge(top.done, 1)
            dve.tensor_copy(share[:, :, 0:E0], top.weights[:, :, :]).then_inc(shared_ready, 1)
            dve.tensor_copy(share[:, :, E0:CH], gate[:, :].unsqueeze(2).broadcast_to([P, NT, CH - E0])).then_inc(shared_ready, 1)
            dve.wait_ge(shared_ready, 2)
            dve.wait_ge(hidden_ready, 2)
            multiply(0, 0)
            with dve.Fori(0, CH // 2 - 1) as i:
                for b in range(2):
                    multiply(i * 2 + (b + 1), 1 - b)
                    add_up(i * 2 + b, b)
            multiply(CH - 1, 1)
            add_up(CH - 2, 0)
            add_up(CH - 1, 1)
            dve.wait_ge(added, NT * (CH + 1))
            for t in range(NT):
                norm.statistics(dve, t)
            norm.vector(dve)


def mixture_1(nc, mem, dram):
    ps, x, consts = mem["ps"], mem["x"], mem["consts"]
    xt = (mem["xt_h"], mem["xt_l"])
    ST = CAP // P
    C1, C2 = 3, 6
    with Stage(nc) as ctx:
        sem = lambda name: ctx.semaphore(f"{name}_m1")
        sb = lambda name, shape, dt=F32: ctx.enter_context(nc.sbuf_tensor(f"{name}_m1", shape, dt))
        raw = sb("w_raw", [P, 2, KD * H1])
        w_h, w_l = sb("w_h", [P, 3, KD * H1], F32R), sb("w_l", [P, 3, KD * H1], F32R)
        r_raw, r_h, r_l = sb("r_raw", [P, KD * E1]), sb("r_h", [P, KD * E1], F32R), sb("r_l", [P, KD * E1], F32R)
        x_h, x_l = sb("x_h", [P, NT, D], F32R), sb("x_l", [P, NT, D], F32R)
        score = sb("score", [P, NT, E1])
        s_h, s_l = sb("s_h", [P, NT, E1], F32R), sb("s_l", [P, NT, E1], F32R)
        w_parts = sb("w_parts", [P, NT, E1, 2], F32R)
        ident = sb("ident", [P, P], F32R)
        score_row = sb("score_row", [P, T])
        ties = sb("ties", [P, P])
        before = sb("before", [P, NT, T], BF16)
        ones = sb("ones", [P, P], BF16)
        rank = sb("rank", [P, NT])
        rank_row = sb("rank_row", [P, T])
        one_hot = sb("one_hot", [P, NT, CAP], F32R)
        one_hot_t = sb("one_hot_t", [P, E1, ST, T], F32R)
        xg_h, xg_l = sb("xg_h", [P, KD, CAP], F32R), sb("xg_l", [P, KD, CAP], F32R)
        gelu = sb("gelu", [P, 2, 2 * CAP])
        g_h, g_l = sb("g_h", [P, MT1 * CAP], F32R), sb("g_l", [P, MT1 * CAP], F32R)
        p_parts, p_slot = sb("p_parts", [P, ST, 2]), sb("p_slot", [P, 2, ST])
        scaled = sb("scaled", [P, ST, D])
        y_parts = [mem[n][:, :, :].rearrange("p k (a s d) -> p (k a) s d", s=ST, d=D) for n in ("xt_h", "xt_l")]

        r_in, w1_in, w2_in = sem("r_in"), sem("w1_in"), sem("w2_in")
        r_high, r_low, xh_ready, xl_ready = sem("r_high"), sem("r_low"), sem("xh_ready"), sem("xl_ready")
        preset, logits_ready, logits_out = sem("preset"), sem("logits_ready"), sem("logits_out")
        score_step, parts_ready = sem("score_step"), sem("parts_ready")
        row_ready, row_out, tie_step, before_ready = sem("row_ready"), sem("row_out"), sem("tie_step"), sem("before_ready")
        rank_ready, rank_out, rank_row_out = sem("rank_ready"), sem("rank_out"), sem("rank_row_out")
        hot_ready, hot_t_ready = sem("hot_ready"), sem("hot_t_ready")
        gathered, xgh_ready, xgl_ready = sem("gathered"), sem("xgh_ready"), sem("xgl_ready")
        p_ready, p_out, p_step = sem("p_ready"), sem("p_out"), sem("p_step")
        w_high, w_low = sem("w_high"), sem("w_low")
        up_ready, gelu_ready, gh_ready, gl_ready = sem("up_ready"), sem("gelu_ready"), sem("gh_ready"), sem("gl_ready")
        down_ready, scaled_ready, yh_ready, yl_ready = sem("down_ready"), sem("scaled_ready"), sem("yh_ready"), sem("yl_ready")
        back_ready, added = sem("back_ready"), sem("added")
        top = TopTwo(nc, ctx, mem, "m1", E1, C_T4)
        norm = NormStage(nc, ctx, mem, "m1", last=True)
        block = ctx.enter_context(nc.Block())

        def bank(b, a=0, n=HALF):
            return ps[:, b * HALF + a:b * HALF + a + n]

        LOGITS, ROW, DOWN, RANKS, XG, SMALL, UP = 0, 0, 1, 2, 4, 5, 6
        NQ = MT1 // 2

        @block.sync
        def _(sp):
            sp.dma_start(r_raw[:, :], dram["w_router1"]).then_inc(r_in, 16)
            for e in range(E1):
                for n, done in ((0, w1_in), (1, w2_in)):
                    if e:
                        sp.wait_ge(w_low, 2 * (e - 1) + n + 1)
                    sp.dma_start(raw[:, n, :], dram["w_experts1"][e, n]).then_inc(done, 16)

        @block.gpsimd
        def _(pool):
            for e in range(E1):
                for n in range(2):
                    pool.wait_ge(w_high, 2 * e + n + 1)
                    at = 2 if n else e % 2
                    pool.tensor_tensor(w_l[:, at, :], raw[:, n, :], w_h[:, at, :].bitcast(F32), ALU.subtract
                                       ).then_inc(w_low, 1)

        @block.scalar
        def _(act):
            def split_weights(e, n):
                act.wait_ge((w1_in, w2_in)[n], 16 * (e + 1))
                act.activation(w_h[:, 2 if n else e % 2, :], raw[:, n, :], ACT.Copy).then_inc(w_high, 1)

            def copy_row(e):
                for n in range(2):
                    act.wait_ge(row_ready, 2 * e + n + 1)
                    act.wait_ge(before_ready, NT * e)
                    act.activation(score_row[:, n * HALF:(n + 1) * HALF], bank(ROW), ACT.Copy).then_inc(row_out, 1)

            act.wait_ge(r_in, 16)
            act.activation(r_h[:, :], r_raw[:, :], ACT.Copy).then_inc(r_high, 1)
            act.activation(x_h[:, :, :], x[:, :, :], ACT.Copy).then_inc(xh_ready, 1)
            act.activation(ident[:, :], consts[:, C_ID:C_ID + P], ACT.Copy).then_inc(preset, 1)
            top.scalar(act)
            copy_row(0)
            split_weights(0, 0)
            split_weights(0, 1)

            def front(e):
                for n in range(2):
                    act.wait_ge(rank_ready, 2 * e + 2)
                    if e:
                        act.wait_ge(hot_t_ready, 2 * e)
                    act.activation(rank_row[:, n * HALF:(n + 1) * HALF], bank(RANKS + n), ACT.Copy).then_inc(rank_row_out, 1)
                if e + 1 < E1:
                    copy_row(e + 1)
                act.wait_ge(gathered, e + 1)
                act.activation(xg_h[:, :, :], bank(XG).rearrange("p (k s) -> p k s", k=KD), ACT.Copy).then_inc(xgh_ready, 1)

            front(0)
            for e in range(E1):
                for q in range(NQ):
                    n = NQ * e + q
                    act.wait_ge(up_ready, n + 1)
                    if n >= 2:
                        act.wait_ge(gl_ready, n - 1)
                    act.activation(gelu[:, q % 2, :], bank(UP + q % 2), ACT.Gelu).then_inc(gelu_ready, 1)
                    act.wait_ge(gelu_ready, n + 1)
                    if e:
                        act.wait_ge(down_ready, e)
                    act.activation(g_h[:, q * HALF:(q + 1) * HALF], gelu[:, q % 2, :], ACT.Copy).then_inc(gh_ready, 1)
                if e + 1 < E1:
                    split_weights(e + 1, 0)
                    front(e + 1)
                act.wait_ge(scaled_ready, e + 1)
                act.activation(y_parts[0][:, e, :, :], scaled[:, :, :], ACT.Copy).then_inc(yh_ready, 1)
                if e + 1 < E1:
                    split_weights(e + 1, 1)
            norm.scalar(act)

        @block.tensor
        def _(pe):
            pe.wait_ge(r_low, 1)
            for t in range(NT):
                toks = slice(t * P, (t + 1) * P)
                for k in range(KD):
                    r = slice(k * E1, (k + 1) * E1)
                    mm = product(pe, bank(LOGITS, t * E1, E1), (xt[0][:, k, toks], xt[1][:, k, toks]),
                                 (r_h[:, r], r_l[:, r]), k == 0, k == KD - 1)
            mm.then_inc(logits_ready, 1)

            def row(e):
                for n in range(2):
                    if e or n:
                        pe.wait_ge(row_out, 2 * e + n)
                    for t in range(4 * n, 4 * n + 4):
                        for part, s in enumerate((s_h, s_l)):
                            mm = pe.matmul(bank(ROW, (t % 4) * P, P), s[:, t, e:e + 1].broadcast_to([P, P]), ident[:, :],
                                           start=part == 0, stop=part == 1, skip_group_check=True)
                    mm.then_inc(row_ready, 1)

            pe.wait_ge(parts_ready, 3)
            pe.wait_ge(preset, 2)
            def front(e):
                for a in range(NT):
                    pe.wait_ge(before_ready, NT * e + a + 1)
                    if a == 0 and e:
                        pe.wait_ge(rank_row_out, 2 * e)
                        pe.wait_ge(p_out, e)
                    for t in range(NT):
                        mm = pe.matmul(bank(SMALL, t, 1), before[:, a, t * P:(t + 1) * P], ones[:, 0:1],
                                       start=(a == 0 and t == 0), stop=a == NT - 1, skip_group_check=True)
                    if a == NT - 1:
                        mm.then_inc(rank_ready, 1)
                    for n in range(2):
                        mm = pe.matmul(bank(RANKS + n), ones[:, :], before[:, a, n * HALF:(n + 1) * HALF],
                                       start=a == 0, stop=a == NT - 1)
                mm.then_inc(rank_ready, 1)
                if e + 1 < E1:
                    row(e + 1)
                if e:
                    pe.wait_ge(xgl_ready, e)
                for k in range(KD):
                    for t in range(NT):
                        if k == 0:
                            pe.wait_ge(hot_ready, NT * e + t + 1)
                        for part, xp in enumerate((x_h, x_l)):
                            mm = pe.matmul(bank(XG, k * CAP, CAP), xp[:, t, k * P:(k + 1) * P], one_hot[:, t, :],
                                           start=(t == 0 and part == 0), stop=(t == NT - 1 and part == 1),
                                           skip_group_check=True)
                mm.then_inc(gathered, 1)
                for s in range(ST):
                    for t in range(NT):
                        mm = pe.matmul(bank(SMALL, 16 + 2 * s, 2), one_hot[:, t, s * P:(s + 1) * P],
                                       w_parts[:, t, e, :], start=t == 0, stop=t == NT - 1, skip_group_check=True)
                mm.then_inc(p_ready, 1)

            row(0)
            front(0)
            for e in range(E1):
                pe.wait_ge(xgl_ready, e + 1)
                pe.wait_ge(w_low, 2 * e + 1)
                for q in range(NQ):
                    n = NQ * e + q
                    if n >= 2:
                        pe.wait_ge(gelu_ready, n - 1)
                    for half in range(2):
                        for k in range(KD):
                            w = slice(k * H1 + (2 * q + half) * P, k * H1 + (2 * q + half + 1) * P)
                            mm = product(pe, bank(UP + q % 2, half * CAP, CAP), (w_h[:, e % 2, w], w_l[:, e % 2, w]),
                                         (xg_h[:, k, :], xg_l[:, k, :]), k == 0, k == KD - 1)
                    mm.then_inc(up_ready, 1)
                if e + 1 < E1:
                    front(e + 1)
                pe.wait_ge(w_low, 2 * e + 2)
                if e:
                    pe.wait_ge(scaled_ready, e)
                for s in range(ST):
                    for m in range(MT1):
                        if s == 0 and m % 2 == 0:
                            pe.wait_ge(gl_ready, NQ * e + m // 2 + 1)
                        g, w = slice(m * CAP + s * P, m * CAP + (s + 1) * P), slice(m * D, (m + 1) * D)
                        mm = product(pe, bank(DOWN, s * D, D), (g_h[:, g], g_l[:, g]),
                                     (w_h[:, 2, w], w_l[:, 2, w]), m == 0, m == MT1 - 1)
                mm.then_inc(down_ready, 1)
            pe.wait_ge(yl_ready, E1)
            pe.wait_ge(hot_t_ready, 2 * E1)
            for t in range(NT):
                if t >= 2:
                    pe.wait_ge(added, t - 1)
                n = 0
                for e in range(E1):
                    for s in range(ST):
                        for y in y_parts:
                            mm = pe.matmul(bank(RANKS + t % 2, 0, D), one_hot_t[:, e, s, t * P:(t + 1) * P], y[:, e, s, :],
                                           start=n == 0, stop=n == 2 * ST * E1 - 1)
                            n += 1
                mm.then_inc(back_ready, 1)

        @block.vector
        def _(dve):
            steps = [0]

            def link(ins):
                steps[0] += 1
                ins.then_inc(score_step, 1)
                dve.wait_ge(score_step, steps[0])

            dve.memset(ones[:, :], 1.0).then_inc(preset, 1)
            dve.wait_ge(r_high, 1)
            dve.tensor_tensor(r_l[:, :], r_raw[:, :], r_h[:, :].bitcast(F32), ALU.subtract).then_inc(r_low, 1)
            dve.wait_ge(xh_ready, 1)
            dve.tensor_tensor(x_l[:, :, :], x[:, :, :], x_h[:, :, :].bitcast(F32), ALU.subtract).then_inc(xl_ready, 1)
            dve.wait_ge(logits_ready, 1)
            dve.tensor_tensor(top.logits[:, :, :], bank(LOGITS, 0, NT * E1).rearrange("p (t e) -> p t e", e=E1),
                              mem["bias_g"][:, :].unsqueeze(1).broadcast_to([P, NT, E1]), ALU.add).then_inc(logits_out, 1)
            dve.wait_ge(logits_out, 1)
            top.vector(dve)
            dve.wait_ge(top.done, 1)
            link(dve.scalar_tensor_tensor(out=score[:, :, :], in0=top.chosen[:, :, :], scalar=-1.0,
                                          in1=top.weights[:, :, :], op0=ALU.add, op1=ALU.add))
            link(dve.tensor_copy(s_h[:, :, :], score[:, :, :]))
            dve.tensor_tensor(s_l[:, :, :], score[:, :, :], s_h[:, :, :].bitcast(F32), ALU.subtract).then_inc(parts_ready, 1)
            link(dve.tensor_copy(w_parts[:, :, :, 0], top.weights[:, :, :]))
            dve.tensor_tensor(w_parts[:, :, :, 1], top.weights[:, :, :], w_parts[:, :, :, 0].bitcast(F32), ALU.subtract
                              ).then_inc(parts_ready, 1)
            dve.wait_ge(parts_ready, 1)
            dve.tensor_tensor(score[:, :, :], s_h[:, :, :].bitcast(F32), s_l[:, :, :].bitcast(F32), ALU.add
                              ).then_inc(parts_ready, 1)
            dve.wait_ge(parts_ready, 3)

            def compare(e, a):
                if a == 0:
                    dve.wait_ge(row_out, 2 * e + 2)
                if e:
                    dve.wait_ge(rank_ready, 2 * e)
                own, mine = slice(a * P, (a + 1) * P), score[:, a, e:e + 1]
                n = NT * e + a
                dve.wait_ge(before_ready, n)
                dve.scalar_tensor_tensor(out=ties[:, :], in0=score_row[:, own], scalar=mine, in1=consts[:, C_TRI:C_TRI + P],
                                         op0=ALU.is_equal, op1=ALU.mult).then_inc(tie_step, 1)
                if a:
                    dve.tensor_scalar(before[:, a, 0:a * P], score_row[:, 0:a * P], mine, None, ALU.is_lt)
                if a < NT - 1:
                    dve.tensor_scalar(before[:, a, (a + 1) * P:T], score_row[:, (a + 1) * P:T], mine, None, ALU.is_le)
                dve.wait_ge(tie_step, n + 1)
                dve.scalar_tensor_tensor(out=before[:, a, own], in0=score_row[:, own], scalar=mine, in1=ties[:, :],
                                         op0=ALU.is_lt, op1=ALU.add).then_inc(before_ready, 1)

            def compare_next(e, first, last):
                if e + 1 < E1:
                    for a in range(first, last):
                        compare(e + 1, a)

            def front(e):
                dve.wait_ge(rank_ready, 2 * e + 1)
                dve.tensor_copy(rank[:, :], bank(SMALL, 0, NT)).then_inc(rank_out, 1)
                dve.wait_ge(rank_out, e + 1)
                if e:
                    dve.wait_ge(p_ready, e)
                for t in range(NT):
                    dve.tensor_scalar(one_hot[:, t, :], consts[:, C_IOTA:C_IOTA + CAP], rank[:, t:t + 1], None,
                                      ALU.is_equal).then_inc(hot_ready, 1)
                dve.wait_ge(rank_row_out, 2 * e + 2)
                for s in range(ST):
                    dve.tensor_scalar(one_hot_t[:, e, s, :], rank_row[:, :], consts[:, C_SLOT + s:C_SLOT + s + 1], None,
                                      ALU.is_equal).then_inc(hot_t_ready, 1)
                compare_next(e, 0, C1)
                dve.wait_ge(xgh_ready, e + 1)
                dve.tensor_tensor(xg_l[:, :, :], bank(XG).rearrange("p (k s) -> p k s", k=KD), xg_h[:, :, :].bitcast(F32),
                                  ALU.subtract).then_inc(xgl_ready, 1)
                dve.wait_ge(p_ready, e + 1)
                if e:
                    dve.wait_ge(p_step, e)
                dve.tensor_copy(p_parts[:, :, :], bank(SMALL, 16, 2 * ST).rearrange("p (s l) -> p s l", l=2)).then_inc(p_out, 1)
                dve.wait_ge(p_out, e + 1)
                dve.tensor_reduce(p_slot[:, e % 2, :], p_parts[:, :, :], AX.X, ALU.add).then_inc(p_step, 1)

            for a in range(NT):
                compare(0, a)
            front(0)
            for e in range(E1):
                if e == 0:
                    compare_next(0, C1, NT)
                for q in range(NQ):
                    n = NQ * e + q
                    dve.wait_ge(gh_ready, n + 1)
                    cols = slice(q * HALF, (q + 1) * HALF)
                    dve.tensor_tensor(g_l[:, cols], gelu[:, q % 2, :], g_h[:, cols].bitcast(F32), ALU.subtract
                                      ).then_inc(gl_ready, 1)
                if e + 1 < E1:
                    front(e + 1)
                    compare_next(e + 1, C1, C2)
                dve.wait_ge(down_ready, e + 1)
                dve.wait_ge(p_step, e + 1)
                dve.tensor_tensor(scaled[:, :, :], bank(DOWN).rearrange("p (s d) -> p s d", s=ST),
                                  p_slot[:, e % 2, :].unsqueeze(2).broadcast_to([P, ST, D]), ALU.mult).then_inc(scaled_ready, 1)
                dve.wait_ge(yh_ready, e + 1)
                dve.tensor_tensor(y_parts[1][:, e, :, :], scaled[:, :, :], y_parts[0][:, e, :, :].bitcast(F32), ALU.subtract
                                  ).then_inc(yl_ready, 1)
                if e + 1 < E1:
                    compare_next(e + 1, C2, NT)
            for t in range(NT):
                dve.wait_ge(back_ready, t + 1)
                dve.tensor_tensor(x[:, t, :], bank(RANKS + t % 2, 0, D), x[:, t, :], ALU.add).then_inc(added, 1)
                dve.wait_ge(added, t + 1)
                norm.statistics(dve, t)
            norm.vector(dve)


def store(nc, mem, dram):
    with Stage(nc) as ctx:
        stored = ctx.semaphore("stored")
        block = ctx.enter_context(nc.Block())

        @block.sync
        def _(sp):
            sp.dma_start(dram["out"].rearrange("(t p) d -> p t d", p=P), mem["x"][:, :, :]).then_inc(stored, 16)
            sp.wait_ge(stored, 16)


def program(nc, dram):
    dram = dict(dram)
    for t in "qk":
        dram[f"{t}_parts"] = nc.dram_tensor(f"{t}_parts", (D, 2, T), F32, kind="Internal").ap()
    dram["sums"] = [nc.dram_tensor(name, (D, T), F32, kind="Internal").ap() for name in ("y_high_sums", "y_low_sums", "exp_sums")]
    with ExitStack() as ctx:
        def sb(c, name, shape, dt=F32):
            return c.enter_context(nc.sbuf_tensor(name, shape, dt))

        mem = {
            "ps": ctx.enter_context(nc.psum_tensor("ps", [P, 8 * HALF], F32)),
            "x": sb(ctx, "x", [P, NT, D]),
            "xt_h": sb(ctx, "xt_h", [P, KD, T], F32R),
            "xt_l": sb(ctx, "xt_l", [P, KD, T], F32R),
            "consts": sb(ctx, "consts", [P, C_END]),
            "eps": sb(ctx, "eps", [P, 1]),
            "bias_g": sb(ctx, "bias_g", [P, E1]),
        }
        with ExitStack() as heads:
            mem |= {
                "masks": sb(heads, "masks", [P, C_T8], BF16),
                "bias_qk": sb(heads, "bias_qk", [P, 4]),
                "bias_v": sb(heads, "bias_v", [P, D]),
                "bias_o": sb(heads, "bias_o", [P, D]),
                "wa_h": sb(heads, "wa_h", [P, 10, KD * D], F32R),
                "wa_l": sb(heads, "wa_l", [P, 10, KD * D], F32R),
                "q_stack": sb(heads, "q_stack", [STACK, 4, T], F32R),
                "k_stack": sb(heads, "k_stack", [STACK, 4, T], F32R),
                "zeros": sb(heads, "zeros", [2, T]),
                "v_full": sb(heads, "v_full", [P, 4, NT, 3 * HD]),
                "v_split": sb(heads, "v_split", [P, 4, NT, 3 * HD], F32R),
                "row_max": sb(heads, "row_max", [P, NT, 2]),
                "max_parts": sb(heads, "max_parts", [P, 32], F32R),
            }
            load_and_split(nc, mem, dram)
            for layer in range(2):
                with ExitStack() as out:
                    mem["y_sums"] = sb(out, f"y_sums_{layer}", [P, 3, KD, T])
                    attention(nc, mem, dram, layer)
                    output_projection(nc, mem, layer)
                if layer == 0:
                    mixture_0(nc, mem, dram)
        mixture_1(nc, mem, dram)
        store(nc, mem, dram)


def contraction_first(w):
    k, n = w.shape
    return w.reshape(k // P, P, n).transpose(1, 0, 2).reshape(P, -1)


def shape_constants():
    c = np.zeros((P, C_END), np.float32)
    i = np.arange(P)
    c[:, C_ID:C_ID + P] = np.eye(P)
    c[:, C_CM:C_CM + P] = np.where(i[None, :] > i[:, None], MASKED, 0)
    c[:, C_CMT:C_CMT + P] = np.where(i[:, None] > i[None, :], MASKED, 0)
    for at, e in ((C_T8, E0), (C_T4, E1)):
        c[:, at:at + e * e] = np.tril(np.ones((e, e)), -1).reshape(-1)
    c[:, C_IOTA:C_IOTA + CAP] = np.arange(CAP)
    for s in range(CAP // P):
        c[:, C_SLOT + s] = i + s * P
    c[:, C_TRI:C_TRI + P] = i[:, None] < i[None, :]
    return c


def rope_tables():
    rot = HD // 2
    freq = (1.0 / np.float32(10000.0) ** (np.arange(0, HD, 2, dtype=np.float32) / np.float32(HD))).astype(np.float32)
    ang = (np.arange(T, dtype=np.float32)[:, None] * freq[None, :]).astype(np.float64)
    cos, sin = np.ones((HD, T)), np.zeros((HD, T))
    cos[:rot] = np.cos(ang).T
    sin[:rot] = np.sin(ang).T * np.where(np.arange(rot) < rot // 2, -1, 1)[:, None]
    return np.stack([np.tile(a, (P // HD, 1)) for a in (cos, sin)], 1).astype(np.float32)


def kernel(**inputs):
    import concourse.bacc as _bacc
    from concourse.bass_utils import run_bass_kernel_spmd as _run

    a = {k: np.asarray(v) for k, v in inputs.items()}
    cf = contraction_first
    by_head = lambda w: w.transpose(1, 0, 2).reshape(D, D)
    swap = np.arange(D).reshape(H, HD)
    swap = np.concatenate([swap[:, HD // 4:HD // 2], swap[:, :HD // 4], swap[:, HD // 2:]], 1).reshape(-1)
    x = a["L0_attn_x"].reshape(T, D)
    wq, wk = a["L1_attn_wq"], a["L1_attn_wk"]
    attn = [by_head(a["L0_attn_Wq"]), by_head(a["L0_attn_Wk"]), by_head(a["L0_attn_Wv"]), a["L0_attn_Wo"],
            wq.T, wq[swap].T, wk.T, wk[swap].T, a["L1_attn_wv"].T, a["L1_attn_wo"].T]
    router0 = np.concatenate([a["L0_ffn_w_router"], a["L0_ffn_gate_w"], np.zeros((1, D), np.float32)]).T
    gates = [*a["L0_ffn_wg"], *a["L0_ffn_sw_gate"].reshape(-1, I0, D)]
    ups = [*a["L0_ffn_wu"], *a["L0_ffn_sw_up"].reshape(-1, I0, D)]
    downs = [*a["L0_ffn_wd"], *a["L0_ffn_sw_down"].reshape(D, -1, I0).transpose(1, 0, 2)]
    arrays = {
        "x_t": x.T.reshape(KD, P, T).transpose(1, 0, 2),
        "x_tok": x.reshape(NT, P, D).transpose(1, 0, 2),
        "w_attn": np.stack([cf(w) for w in attn], 1),
        "bias_qk": np.concatenate([a["L0_attn_bq"].reshape(KD, P), a["L0_attn_bk"].reshape(KD, P)]).T,
        "bias_v": a["L0_attn_bv"].reshape(1, D),
        "bias_o": a["L0_attn_bo"].reshape(1, D),
        "bias_g": a["L1_ffn_bg"].reshape(1, E1),
        "w_router0": cf(router0),
        "w_chunks0": np.stack([np.concatenate([cf(g.T), cf(u.T), cf(d.T)], 1) for g, u, d in zip(gates, ups, downs)]),
        "w_router1": cf(a["L1_ffn_Wg"]),
        "w_experts1": np.stack([np.stack([cf(w1), cf(w2)]) for w1, w2 in zip(a["L1_ffn_W1"], a["L1_ffn_W2"])]),
        "consts": shape_constants(),
        "rope": rope_tables(),
    }
    arrays = {k: np.ascontiguousarray(v) for k, v in arrays.items()}
    nc = _bacc.Bacc("TRN2", target_bir_lowering=False, num_devices=1)
    dram = {k: nc.dram_tensor(f"in_{k}", v.shape, F32, kind="ExternalInput").ap() for k, v in arrays.items()}
    dram["out"] = nc.dram_tensor("out", (T, D), F32, kind="ExternalOutput").ap()
    program(nc, dram)
    r = _run(nc, [{f"in_{k}": v for k, v in arrays.items()}], core_ids=[0])
    return r.results[0]["out"].reshape(1, T, D)
```

```python
from contextlib import ExitStack

import numpy as np

import concourse.bass as bass
from concourse import mybir

F32 = mybir.dt.float32
F32R = mybir.dt.float32r
BF16 = mybir.dt.bfloat16
ALU = mybir.AluOpType
ACT = mybir.ActivationFunctionType
AX = mybir.AxisListType

P = 128
T = 1024
D = 256
H = 16
HD = D // H
NT = T // P
KD = D // P
HALF = 512
EPS = 1e-5
MASKED = -3.0e38

E0 = 8
I0 = 128
CH = E0 + 512 // I0
CW = 2 * (D // P) * I0 + D
NR0 = E0 + 2
E1 = 4
H1 = 1024
CAP = T // E1
MT1 = H1 // P

C_ID, C_CM, C_CMT, C_T8, C_T4, C_IOTA, C_SLOT, C_TRI, C_END = 0, 128, 256, 384, 448, 464, 720, 722, 850

LEAD = 7
ROWS = 2 * 2 * HD
STACK = ROWS + 2


class Semaphores(ExitStack):

    def __init__(self, nc):
        super().__init__()
        self.nc, self.numbers = nc, []

    def __call__(self, name):
        sem = self.enter_context(self.nc.semaphore(name))
        self.numbers.append(sem.num)
        return sem

    def clear(self):
        numbers = sorted(self.numbers)
        starts = [n for n in numbers if n - 1 not in numbers]
        ends = [n + 1 for n in numbers if n + 1 not in numbers]
        with self.nc.Block() as block:

            @block.sync
            def _(sp):
                for start, end in zip(starts, ends):
                    sp.sem_clear(range(start, end))


def product(pe, out, lhs, rhs, first, last):
    (lh, ll), (rh, rl) = lhs, rhs
    pe.matmul(out, lh, rl, start=first, stop=False, skip_group_check=True)
    pe.matmul(out, ll, rh, start=False, stop=False, skip_group_check=True)
    return pe.matmul(out, lh, rh, start=False, stop=last, skip_group_check=True)


def load_and_split(nc, mem, dram):
    with ExitStack() as ctx:
        sem = lambda name: mem["semaphore"](name)
        x_raw = ctx.enter_context(nc.sbuf_tensor("x_raw", [P, KD, T], F32))
        w_raw = ctx.enter_context(nc.sbuf_tensor("w_raw", [P, 4, KD * D], F32))
        consts_in, x_in, w_in = sem("consts_in"), [sem("x0_in"), sem("x1_in")], [sem("w0_in"), sem("w1_in")]
        rest_in = sem("rest_in")
        x_high, w_high, low_done, preset = sem("x_high"), sem("w_high"), sem("low_done"), sem("preset")
        block = ctx.enter_context(nc.Block())

        @block.sync
        def _(sp):
            for k in range(KD):
                sp.dma_start(x_raw[:, k, :], dram["x_t"][:, k, :]).then_inc(x_in[k], 16)
            for n in range(2):
                sp.dma_start(w_raw[:, 2 * n:2 * n + 2, :], dram["w_attn"][:, 2 * n:2 * n + 2, :]).then_inc(w_in[n], 16)
            sp.dma_start(mem["consts"][:, :], dram["consts"]).then_inc(consts_in, 16)
            sp.dma_start(mem["bias_qk"][:, :], dram["bias_qk"]).then_inc(rest_in, 16)
            sp.dma_start(mem["bias_v"][:, :], dram["bias_v"].broadcast_to([P, D])).then_inc(rest_in, 16)
            sp.dma_start(mem["bias_o"][:, :], dram["bias_o"].broadcast_to([P, D])).then_inc(rest_in, 16)
            sp.dma_start(mem["bias_g"][:, :], dram["bias_g"].broadcast_to([P, E1])).then_inc(rest_in, 16)
            sp.wait_ge(rest_in, 16 * 4)

        @block.scalar
        def _(act):
            for k in range(KD):
                act.wait_ge(x_in[k], 16)
                act.activation(mem["xt_h"][:, k, :], x_raw[:, k, :], ACT.Copy).then_inc(x_high, 1)
            for n in range(2):
                w = slice(2 * n, 2 * n + 2)
                act.wait_ge(w_in[n], 16)
                act.activation(mem["wa_h"][:, w, :], w_raw[:, w, :], ACT.Copy).then_inc(w_high, 1)

        @block.vector
        def _(dve):
            dve.memset(mem["v_split"][:, :, :, 2 * HD:3 * HD].bitcast(F32), 1.0).then_inc(preset, 1)
            dve.memset(mem["zeros"][:, :], 0.0).then_inc(preset, 1)
            dve.memset(mem["eps"][:, :], EPS).then_inc(preset, 1)
            dve.memset(mem["row_max"][:, :, :], MASKED).then_inc(preset, 1)
            dve.memset(mem["max_parts"][:, :].bitcast(F32), 0.0).then_inc(preset, 1)
            for j in range(4):
                dve.memset(mem["k_stack"][ROWS:STACK, j, :].bitcast(F32), 1.0).then_inc(preset, 1)
            for k in range(KD):
                dve.wait_ge(x_high, k + 1)
                dve.tensor_tensor(mem["xt_l"][:, k, :], x_raw[:, k, :], mem["xt_h"][:, k, :].bitcast(F32),
                                  ALU.subtract).then_inc(low_done, 1)
            for n in range(2):
                w = slice(2 * n, 2 * n + 2)
                dve.wait_ge(w_high, n + 1)
                dve.tensor_tensor(mem["wa_l"][:, w, :], w_raw[:, w, :], mem["wa_h"][:, w, :].bitcast(F32),
                                  ALU.subtract).then_inc(low_done, 1)
            dve.wait_ge(consts_in, 16)
            dve.tensor_copy(mem["masks"][:, :], mem["consts"][:, C_ID:C_T8]).then_inc(low_done, 1)


def attention(nc, mem, dram, layer):
    causal, rope = layer == 0, layer == 1
    ps = mem["ps"]
    qs, ks = mem["q_stack"], mem["k_stack"]
    low_on = ["pool", "dve", "pool", "dve" if causal else "pool"]
    low_on += ["pool"] * 4 if causal else ["dve", "pool", "dve", "pool"]
    on = {e: [kt for kt in range(NT) if low_on[kt] == e] for e in ("pool", "dve")}
    scratch = {"q": dram["q_parts"], "k": dram["k_parts"]}
    units = [(t, m, n) for m in range(KD) for t in "qk" for n in range(2)]
    unit_bank, unit_after = (0, 2, 4, 6, 0, 2, 6, 0), (0, 0, 0, 0, 1, 2, 4, 5)
    w_at = {"q": 4, "qp": 5, "k": 6, "kp": 7, "v": 8} if rope else {"q": 0, "k": 1, "v": 2}

    def pieces(qt):
        end = (qt + 1) * P if causal else T
        return [(a, min(a + HALF, end)) for a in range(0, end, HALF)]

    def piece_number(qt):
        return sum(len(pieces(t)) for t in range(qt))

    PIECES = piece_number(NT)

    with ExitStack() as ctx:
        sem = lambda name: mem["semaphore"](f"{name}_{layer}")
        sb = lambda name, shape, dt=F32: ctx.enter_context(nc.sbuf_tensor(f"{name}_{layer}", shape, dt))
        probs = sb("probs", [P, 4, T])
        p_high, p_low = sb("p_high", [P, 4, T], F32R), sb("p_low", [P, 4, T], F32R)
        halves = lambda n: probs[:, n, :].rearrange("p (u c) -> p u c", u=2)
        flat, turned = halves(0), halves(1)
        parts = p_high[:, :, :].rearrange("p (g l) t -> p g l t", l=2)
        tables = probs[:, 2:4, :]
        v_all = sb("v_all", [P, NT, D])
        max_rows = sb("max_rows", [P, 2, 32])
        negmax = sb("negmax", [P, NT])
        sums = sb("sums", [3 * HD, 2, T])

        unit_ready, unit_out, high_ready, low_ready = sem("unit_ready"), sem("unit_out"), sem("high_ready"), sem("low_ready")
        rope_step = sem("rope_step")
        v_ready, v_out = sem("v_ready"), sem("v_out")
        written = [sem(f"written{m}") for m in range(2 * KD)]
        loaded = [sem(f"loaded{j}") for j in range(4)]
        max_loaded = [sem(f"max_loaded{j}") for j in range(4)]
        scores_ready, scores_free, fin, max_ready = sem("scores_ready"), sem("scores_free"), sem("fin"), sem("max_ready")
        st_ready, exp_done = sem("st_ready"), sem("exp_done")
        pv_ready, sums0_out, sums1_out = sem("pv_ready"), sem("sums0_out"), sem("sums1_out")
        p_high_ready = sem("p_high_ready")
        p_low_ready = {"pool": sem("p_low_pool"), "dve": sem("p_low_dve")}
        stored = [sem("sums_stored0"), sem("sums_stored1")]
        extra_in, recip_ready = sem("extra_in"), sem("sums_inverted")
        y0_loaded, y1_loaded = sem("y0_loaded"), sem("y1_loaded")
        v_step, v_copied, biased = sem("v_step"), sem("v_copied"), sem("x_biased")
        block = ctx.enter_context(nc.Block())

        def bank(b, a=0, n=HALF):
            return ps[:, b * HALF + a:b * HALF + a + n]

        def sums_bank(n, a=0, b=HALF):
            return ps[0:3 * HD, (6 + n) * HALF + a:(6 + n) * HALF + b]

        @block.sync
        def _(sp):
            def write_parts(g):
                t, m, _ = units[2 * g]
                sp.wait_ge(low_ready, 2 * g + 2)
                sp.dma_start(scratch[t][m * P:(m + 1) * P, :, :], parts[:, g % 2, :, :].bitcast(F32)).then_inc(written[g], 16)

            def load_stacks(h, j):
                q = scratch["q"][bass.ds(h * HD, HD), :, :]
                k = scratch["k"][bass.ds(h * HD, HD), :, :].rearrange("d l t -> (d l) t")
                for part in range(2):
                    rows = slice(part * 2 * HD, (part + 1) * 2 * HD)
                    sp.dma_start(qs[rows, j, :].bitcast(F32), q[:, part:part + 1, :].broadcast_to([HD, 2, T])
                                 ).then_inc(loaded[j], 16)
                    sp.dma_start(ks[rows, j, :].bitcast(F32), k).then_inc(loaded[j], 16)
                sp.dma_start(qs[ROWS:STACK, j, :].bitcast(F32), mem["zeros"][0:2, :]).then_inc(loaded[j], 16)

            def load_max(h, j, count):
                sp.wait_ge(max_ready, count)
                for i in range(4):
                    dst = qs[ROWS:STACK, j, :].bitcast(F32).rearrange("l (t i c) -> l t i c", i=4, c=32)[:, :, i, :]
                    sp.dma_start(dst, max_rows[32 * i:32 * i + 2 * NT, j % 2, :]).then_inc(max_loaded[j], 16)

            def store_sums(h, j):
                sp.wait_ge(sums0_out, h + 2)
                sp.wait_ge(sums1_out, h + 2)
                for n in range(3):
                    sp.dma_start(dram["sums"][n][bass.ds(h * HD, HD), :], sums[n * HD:(n + 1) * HD, j % 2, :]
                                 ).then_inc(stored[j % 2], 16)

            def load_sums(a, b, done):
                for parity, st in enumerate(stored):
                    sp.wait_ge(st, 48 * ((b + 1 - parity) // 2) + 48)
                rows = slice(a % 8 * HD, ((b - 1) % 8 + 1) * HD)
                for n in range(3):
                    sp.dma_start(mem["y_sums"][rows, n, a // 8, :], dram["sums"][n][a * HD:b * HD, :]).then_inc(done, 16)

            if rope:
                sp.dma_start(tables, dram["rope"]).then_inc(extra_in, 16)
            else:
                sp.dma_start(mem["x"][:, :, :], dram["x_tok"]).then_inc(extra_in, 16)
            write_parts(0)
            write_parts(1)
            sp.wait_ge(written[0], 16)
            sp.wait_ge(written[1], 16)
            for h in range(4):
                load_stacks(h, h)
            write_parts(2)
            write_parts(3)
            load_max(0, 0, 1)
            load_max(1, 1, 2)
            sp.wait_ge(written[2], 16)
            sp.wait_ge(written[3], 16)
            with sp.Fori(0, H // 4 - 1) as i:
                for j in range(4):
                    load_max(i * 4 + (j + 2), (j + 2) % 4, i * 4 + (j + 3))
                    sp.wait_ge(pv_ready, i * 4 + (j + 1))
                    load_stacks(i * 4 + (j + 4), j)
                    store_sums(i * 4 + j, j)
            load_sums(0, H // 2, y0_loaded)
            for j in range(4):
                if j < 2:
                    load_max(H - 2 + j, j + 2, H - 1 + j)
                store_sums(H - 4 + j, j)
                if j:
                    load_sums((H // 2, H - 2, H - 1)[j - 1], H - 3 + j, y1_loaded)
            sp.wait_ge(extra_in, 16)
            sp.wait_ge(y0_loaded, 3 * 16)
            sp.wait_ge(y1_loaded, 9 * 16)

        @block.tensor
        def _(pe):
            def unit(u):
                t, m, n = units[u]
                if unit_after[u]:
                    pe.wait_ge(unit_out, unit_after[u])
                cols = slice(n * HALF, (n + 1) * HALF)
                for r, name in enumerate([t, t + "p"][:1 + rope]):
                    for k in range(KD):
                        w = slice(k * D + m * P, k * D + (m + 1) * P)
                        mm = product(pe, bank(unit_bank[u] + r),
                                     (mem["wa_h"][:, w_at[name], w], mem["wa_l"][:, w_at[name], w]),
                                     (mem["xt_h"][:, k, cols], mem["xt_l"][:, k, cols]), k == 0, k == KD - 1)
                mm.then_inc(unit_ready, 1)

            def project_v(t):
                if t == 0:
                    pe.wait_ge(unit_out, 3)
                if t >= 2:
                    pe.wait_ge(v_out, t - 1)
                for k in range(KD):
                    toks, w = slice(t * P, (t + 1) * P), slice(k * D, (k + 1) * D)
                    mm = product(pe, bank(4 + t % 2, 0, D), (mem["xt_h"][:, k, toks], mem["xt_l"][:, k, toks]),
                                 (mem["wa_h"][:, w_at["v"], w], mem["wa_l"][:, w_at["v"], w]), k == 0, k == KD - 1)
                mm.then_inc(v_ready, 1)

            def score_tile(h, j, qt, loads, which=(0, 1)):
                if qt == 0 and which[0] == 0:
                    pe.wait_ge(loaded[j], 80 * loads)
                for n, (a, b) in enumerate(pieces(qt)):
                    if n not in which:
                        continue
                    at = piece_number(qt) + n
                    pe.wait_ge(scores_free, h * PIECES + (at + 1))
                    diagonal = causal and b == (qt + 1) * P
                    mm = pe.matmul(bank(4 + at % 2, 0, b - a), qs[0:STACK, j, qt * P:(qt + 1) * P], ks[0:STACK, j, a:b],
                                   start=True, stop=True)
                    if diagonal:
                        mm = pe.matmul(bank(4 + at % 2, b - a - P, P), mem["masks"][:, C_ID:C_ID + P],
                                       mem["masks"][:, C_CM:C_CM + P], start=False, stop=True, skip_group_check=True)
                    mm.then_inc(scores_ready, 1)

            def transposed_scores(j, kt, loads):
                if kt == 0:
                    pe.wait_ge(max_loaded[j], 64 * loads)
                first = kt * P if causal else 0
                base = 2 * (kt % 2) * HALF
                for a, b in ((first, HALF), (max(first, HALF), T)):
                    if a >= b:
                        continue
                    diagonal = causal and a == first
                    mm = pe.matmul(ps[:, base + a:base + b], ks[0:STACK, j, kt * P:(kt + 1) * P], qs[0:STACK, j, a:b],
                                   start=True, stop=True)
                    if diagonal:
                        mm = pe.matmul(ps[:, base + a:base + a + P], mem["masks"][:, C_ID:C_ID + P],
                                       mem["masks"][:, C_CMT:C_CMT + P], start=False, stop=True, skip_group_check=True)
                mm.then_inc(st_ready, 1)

            def times_v(h, j, kt):
                if kt == 0:
                    pe.wait_ge(v_copied, h + 1)
                if kt in on["pool"]:
                    pe.wait_ge(p_low_ready["pool"], h * len(on["pool"]) + (on["pool"].index(kt) + 1))
                v = mem["v_split"][:, j, kt, :]
                first = kt * P if causal else 0
                for n in range(first // HALF, 2):
                    if kt == 0:
                        pe.wait_ge((sums0_out, sums1_out)[n], h + 1)
                    if kt in on["dve"]:
                        pe.wait_ge(p_low_ready["dve"], h * (2 * len(on["dve"])) + (2 * on["dve"].index(kt) + n + 1))
                    start = max(first, n * HALF)
                    for i, p in enumerate((p_high, p_low)):
                        mm = pe.matmul(sums_bank(n, start - n * HALF), v, p[:, kt % 4, start:(n + 1) * HALF],
                                       start=kt == 0 and i == 0, stop=True, skip_group_check=True)
                if kt == NT - 1:
                    mm.then_inc(pv_ready, 1)

            def head(h, j, loads, max_next, ahead, next_head, last_head=True):
                def others(kt, which):
                    if kt < NT - LEAD and next_head:
                        score_tile(h + 1, (j + 1) % 4, kt + LEAD, None, which)
                    elif kt >= NT - LEAD and ahead is not None:
                        score_tile(h + 2, (j + 2) % 4, kt - (NT - LEAD), ahead, which)

                for kt in range(NT):
                    others(kt, (0,))
                    if kt >= 2:
                        times_v(h, j, kt - 2)
                    elif last_head:
                        times_v(h - 1, (j - 1) % 4, kt - 2 + NT)
                    pe.wait_ge(exp_done, h * NT + (kt + 1))
                    if kt < NT - 2:
                        transposed_scores(j, kt + 2, loads)
                    elif next_head:
                        transposed_scores((j + 1) % 4, kt + 2 - NT, max_next)
                    others(kt, (1,))

            for u in range(4):
                unit(u)
            for t in range(NT):
                project_v(t)
            for u in range(4, 8):
                unit(u)
            pe.wait_ge(v_out, NT)
            for qt in range(NT):
                score_tile(0, 0, qt, 1)
            for qt in range(LEAD):
                score_tile(1, 1, qt, 1)
            pe.wait_ge(unit_out, 8)
            transposed_scores(0, 0, 1)
            transposed_scores(0, 1, 1)
            for j in range(4):
                head(j, j, 1, 1 + (j == 3), 1 + (j >= 2), True, j > 0)
            with pe.Fori(1, H // 4 - 1) as i:
                for j in range(4):
                    head(i * 4 + j, j, i + 1, i + (1 + (j == 3)), i + (1 + (j >= 2)), True)
            for j in range(4):
                head(H - 4 + j, j, H // 4, H // 4, H // 4 if j < 2 else None, j < 3)
            times_v(H - 1, 3, NT - 2)
            times_v(H - 1, 3, NT - 1)

        @block.scalar
        def _(act):
            for u, (t, m, n) in enumerate(units):
                g = u // 2
                act.wait_ge(unit_out, u + 1)
                if g >= 2 and n == 0:
                    act.wait_ge(written[g - 2], 16)
                act.activation(parts[:, g % 2, 0, n * HALF:(n + 1) * HALF], flat[:, u % 2, :], ACT.Copy
                               ).then_inc(high_ready, 1)
                if rope and u == 3:
                    for tile in range(NT):
                        act.wait_ge(v_ready, tile + 1)
                        act.activation(v_all[:, tile, :], bank(4 + tile % 2, 0, D), ACT.Copy).then_inc(v_out, 1)

            def exps(h, tiles):
                for kt in tiles:
                    first = kt * P if causal else 0
                    base = 2 * (kt % 2) * HALF
                    act.wait_ge(st_ready, h * NT + (kt + 1))
                    act.activation(probs[:, kt % 4, first:T], ps[:, base + first:base + T], ACT.Exp
                                   ).then_inc(exp_done, 1)
                    act.wait_ge(exp_done, h * NT + (kt + 1))
                    act.activation(p_high[:, kt % 4, first:T], probs[:, kt % 4, first:T], ACT.Copy
                                   ).then_inc(p_high_ready, 1)

            def take_sums(h, j, stores):
                act.wait_ge(pv_ready, h + 1)
                act.wait_ge(stored[j % 2], stores)
                act.activation(sums[:, j % 2, 0:HALF], sums_bank(0), ACT.Copy).then_inc(sums0_out, 1)

            def heads(i, first=False):
                for j in range(4):
                    exps(i * 4 + j, range(2))
                    if j or not first:
                        take_sums(i * 4 + (j - 1), (j - 1) % 4, i * 96 + 48 * ((j - 1) // 2 + 1))
                    exps(i * 4 + j, range(2, NT))

            act.wait_ge(low_ready, 8)
            act.wait_ge(written[2], 16)
            act.wait_ge(written[3], 16)
            heads(0, True)
            with act.Fori(1, H // 4) as i:
                heads(i)
            take_sums(H - 1, 3, 48 * (H // 2))

        @block.gpsimd
        def _(pool):
            def copy_v(h, j):
                full = mem["v_plain"][:, j, :, :]
                high, low = mem["v_split"][:, j, :, 0:HD], mem["v_split"][:, j, :, HD:2 * HD]
                pool.tensor_copy(full, v_all[:, :, bass.ds(h * HD, HD)]).then_inc(v_step, 1)
                pool.tensor_copy(high, v_all[:, :, bass.ds(h * HD, HD)]).then_inc(v_step, 1)
                pool.wait_ge(v_step, h * 2 + 2)
                pool.tensor_tensor(low, full, high.bitcast(F32), ALU.subtract).then_inc(v_copied, 1)

            def lows(h, j, prepare):
                for n, kt in enumerate(on["pool"]):
                    first = kt * P if causal else 0
                    pool.wait_ge(p_high_ready, h * NT + (kt + 1))
                    at = slice(first, T)
                    pool.tensor_tensor(p_low[:, kt % 4, at], probs[:, kt % 4, at], p_high[:, kt % 4, at].bitcast(F32),
                                       ALU.subtract).then_inc(p_low_ready["pool"], 1)
                    if n == len(on["pool"]) - 2 and prepare:
                        pool.wait_ge(pv_ready, h)
                        copy_v(h + 3, (j + 3) % 4)

            def unit_low(u):
                g, n = u // 2, u % 2
                high, low = [parts[:, g % 2, l, n * HALF:(n + 1) * HALF] for l in range(2)]
                pool.wait_ge(high_ready, u + 1)
                pool.tensor_tensor(low, flat[:, u % 2, :], high.bitcast(F32), ALU.subtract).then_inc(low_ready, 1)

            for u in range(4):
                unit_low(u)
            for u in range(4, 8):
                pool.wait_ge(written[u // 2 - 2], 16)
                unit_low(u)
            pool.wait_ge(v_out, NT)
            for h in range(4):
                copy_v(h, h)
            for j in range(4):
                lows(j, j, j > 0)
            with pool.Fori(1, H // 4 - 1) as i:
                for j in range(4):
                    lows(i * 4 + j, j, True)
            for j in range(4):
                lows(H - 4 + j, j, j == 0)
            if layer == 0:
                pool.wait_ge(extra_in, 16)
                for t in range(NT):
                    pool.tensor_tensor(mem["x"][:, t, :], mem["x"][:, t, :], mem["bias_o"][:, :], ALU.add).then_inc(biased, 1)

        @block.vector
        def _(dve):
            def unit_to_flat(u):
                t, m, n = units[u]
                dve.wait_ge(unit_ready, u + 1)
                if u >= 2:
                    dve.wait_ge(low_ready, u - 1)
                src, dst = bank(unit_bank[u]), flat[:, u % 2, :]
                scale = HD ** -0.5 if t == "q" else 1.0
                if not rope:
                    bias = mem["bias_qk"][:, 2 * (t == "k") + m:2 * (t == "k") + m + 1]
                    dve.tensor_scalar(dst, src, bias, scale, ALU.add, ALU.mult).then_inc(unit_out, 1)
                else:
                    cols = slice(n * HALF, (n + 1) * HALF)
                    if u == 0:
                        dve.wait_ge(extra_in, 16)
                    dve.scalar_tensor_tensor(out=dst, in0=src, scalar=scale, in1=tables[:, 0, cols],
                                             op0=ALU.mult, op1=ALU.mult).then_inc(rope_step, 1)
                    dve.scalar_tensor_tensor(out=turned[:, u % 2, :], in0=bank(unit_bank[u] + 1), scalar=scale,
                                             in1=tables[:, 1, cols], op0=ALU.mult, op1=ALU.mult
                                             ).then_inc(rope_step, 1)
                    dve.wait_ge(rope_step, 2 * u + 2)
                    dve.tensor_tensor(dst, dst, turned[:, u % 2, :], ALU.add).then_inc(unit_out, 1)
            def v_to_sbuf(t):
                dve.wait_ge(v_ready, t + 1)
                dve.tensor_tensor(v_all[:, t, :], bank(4 + t % 2, 0, D), mem["bias_v"][:, :], ALU.add).then_inc(v_out, 1)

            def tile_max(h, qt, which=(0, 1)):
                for n, (a, b) in enumerate(pieces(qt)):
                    if n not in which:
                        continue
                    at = piece_number(qt) + n
                    dve.wait_ge(scores_ready, h * PIECES + (at + 1))
                    dve.tensor_reduce(mem["row_max"][:, qt, n:n + 1], bank(4 + at % 2, 0, b - a), AX.X, ALU.max
                                      ).then_inc(scores_free, 1)

            def finish_max(h, j, loads, buf):
                dve.wait_ge(scores_free, h * PIECES + (2 + PIECES))
                dve.tensor_reduce(negmax[:, :], mem["row_max"][:, :, :], AX.X, ALU.max, negate=True).then_inc(fin, 1)
                dve.wait_ge(fin, h * 3 + 1)
                dve.tensor_copy(mem["max_parts"][:, 0:NT], negmax[:, :]).then_inc(fin, 1)
                dve.wait_ge(fin, h * 3 + 2)
                dve.tensor_tensor(mem["max_parts"][:, NT:2 * NT], negmax[:, :], mem["max_parts"][:, 0:NT].bitcast(F32),
                                  ALU.subtract).then_inc(fin, 1)
                dve.wait_ge(fin, h * 3 + 3)
                if loads is not None:
                    dve.wait_ge(max_loaded[buf], loads)
                dve.transpose(max_rows[:, j % 2, :], mem["max_parts"][:, :].bitcast(F32)).then_inc(max_ready, 1)

            def take_sums(h, j, stores):
                dve.wait_ge(pv_ready, h + 1)
                dve.wait_ge(stored[j % 2], stores)
                dve.tensor_copy(sums[:, j % 2, HALF:T], sums_bank(1)).then_inc(sums1_out, 1)

            def head(i, j, first=False, following=2):
                h = i * 4 + j
                for kt in range(NT):
                    if kt == 1 and (j or not first):
                        take_sums(i * 4 + (j - 1), (j - 1) % 4, i * 96 + 48 * ((j - 1) // 2 + 1))
                    for n in range(2):
                        if kt < NT - LEAD and following >= 1:
                            tile_max(i * 4 + (j + 1), kt + LEAD, (n,))
                        elif kt >= NT - LEAD and following >= 2:
                            tile_max(i * 4 + (j + 2), kt - (NT - LEAD), (n,))
                        if kt in on["dve"]:
                            low(h, kt, n)
                    if kt == NT - LEAD - 1 and following >= 1:
                        finish_max(i * 4 + (j + 1), (j + 1) % 4, None if first and j == 0 else i * 64 + 64 * (j > 0), (j - 1) % 4)

            def low(h, kt, n):
                at = slice(max(n * HALF, kt * P if causal else 0), (n + 1) * HALF)
                if n == 0:
                    dve.wait_ge(p_high_ready, h * NT + (kt + 1))
                dve.tensor_tensor(p_low[:, kt % 4, at], probs[:, kt % 4, at], p_high[:, kt % 4, at].bitcast(F32),
                                  ALU.subtract).then_inc(p_low_ready["dve"], 1)

            for c, (done, n) in enumerate(((scores_free, 2), (sums0_out, 1), (sums1_out, 1), *((st, 48) for st in stored))):
                dve.memset(negmax[:, c:c + 1], 0.0).then_inc(done, n)
            for u in range(4):
                unit_to_flat(u)
            if not rope:
                for t in range(NT):
                    v_to_sbuf(t)
            for u in range(4, 8):
                unit_to_flat(u)
            for qt in range(NT):
                tile_max(0, qt)
            finish_max(0, 0, None, 0)
            for qt in range(LEAD):
                tile_max(1, qt)
            for j in range(4):
                head(0, j, True)
            with dve.Fori(1, H // 4 - 1) as i:
                for j in range(4):
                    head(i, j)
            for j in range(4):
                head(H // 4 - 1, j, following=3 - j)
                if j == 2:
                    dve.wait_ge(y0_loaded, 3 * 16)
                    dve.reciprocal(mem["y_sums"][:, 2, 0, :], mem["y_sums"][:, 2, 0, :]).then_inc(recip_ready, 1)
            take_sums(H - 1, 3, 48 * (H // 2))


def norm_statistics(dve, stats, mv, rows, t, step, count):
    dve.bn_stats(stats[:, t % 2, :], rows).then_inc(step, 1)
    dve.wait_ge(step, count + 1)
    dve.bn_aggr(mv[:, t, :], stats[:, t % 2, :]).then_inc(step, 1)
    return count + 2


def output_projection(nc, mem, dram, layer):
    ps, x = mem["ps"], mem["x"]
    y_sums, y_low_sums, exp_sums = [mem["y_sums"][:, n, :, :] for n in range(3)]
    w_o = 3 if layer == 0 else 9
    with ExitStack() as ctx:
        sem = lambda name: mem["semaphore"](f"{name}_{layer}")
        sb = lambda name, shape, dt=F32: ctx.enter_context(nc.sbuf_tensor(f"{name}_{layer}", shape, dt))
        yt_h, yt_l = sb("yt_h", [P, KD, T], F32R), sb("yt_l", [P, KD, T], F32R)
        sums_added, recip_ready = sem("sums_added"), sem("recip_ready")
        y_ready, high_ready, low_ready = sem("y_ready"), sem("y_high"), sem("y_low")
        o_ready, o_out = sem("o_ready"), sem("o_out")
        norm = NormStage(nc, ctx, mem, f"a{layer}")
        mem["first_in"] = [sem("first0_in"), sem("first1_in"), sem("router_in")]
        block = ctx.enter_context(nc.Block())

        @block.sync
        def _(sp):
            sp.wait_ge(low_ready, 4)
            raw, r_raw = (chunks_memory if layer == 0 else experts_memory)(mem)
            for n in range(2):
                first = dram["w_chunks0"][n] if layer == 0 else dram["w_experts1"][0, n]
                sp.dma_start(raw[:, n, :], first).then_inc(mem["first_in"][n], 16)
                if n == 0:
                    sp.dma_start(r_raw, dram[f"w_router{layer}"]).then_inc(mem["first_in"][2], 16)

        def quarter(a, n):
            k, g = n % 2, n // 2
            return a[:, k, g * HALF:(g + 1) * HALF]

        def out_bank(t):
            return ps[:, (2 + t % 2) * HALF:(2 + t % 2) * HALF + D]

        @block.tensor
        def _(pe):
            for t in range(NT):
                if t % 4 == 0:
                    pe.wait_ge(low_ready, 2 + 2 * (t // 4))
                if t >= 2:
                    pe.wait_ge(o_out, t - 1)
                toks = slice(t * P, (t + 1) * P)
                for k in range(KD):
                    w = slice(k * D, (k + 1) * D)
                    mm = product(pe, out_bank(t), (yt_h[:, k, toks], yt_l[:, k, toks]),
                                 (mem["wa_h"][:, w_o, w], mem["wa_l"][:, w_o, w]), k == 0, k == KD - 1)
                mm.then_inc(o_ready, 1)
            norm.tensor(pe)

        @block.scalar
        def _(act):
            for n in range(4):
                act.wait_ge(y_ready, n + 1)
                act.activation(quarter(yt_h, n), quarter(y_sums, n), ACT.Copy).then_inc(high_ready, 1)
            norm.scalar(act)

        @block.gpsimd
        def _(pool):
            for n in range(4):
                pool.tensor_tensor(quarter(y_sums, n), quarter(y_sums, n), quarter(y_low_sums, n), ALU.add).then_inc(sums_added, 1)
            for n in range(4):
                pool.wait_ge(high_ready, n + 1)
                pool.tensor_tensor(quarter(yt_l, n), quarter(y_sums, n), quarter(yt_h, n).bitcast(F32), ALU.subtract
                                   ).then_inc(low_ready, 1)

        @block.vector
        def _(dve):
            for g in range(2):
                dve.reciprocal(quarter(exp_sums, 2 * g + 1), quarter(exp_sums, 2 * g + 1)).then_inc(recip_ready, 1)
                for n in (2 * g, 2 * g + 1):
                    dve.wait_ge(sums_added, n + 1)
                    if n % 2:
                        dve.wait_ge(recip_ready, g + 1)
                    dve.tensor_tensor(quarter(y_sums, n), quarter(y_sums, n), quarter(exp_sums, n), ALU.mult).then_inc(y_ready, 1)
            for t in range(NT):
                dve.wait_ge(o_ready, t + 1)
                dve.tensor_tensor(x[:, t, :], out_bank(t), x[:, t, :], ALU.add).then_inc(o_out, 1)
                dve.wait_ge(o_out, t + 1)
                norm.statistics(dve, t)
            norm.vector(dve)


def borrowed(mem, start, width):
    return mem["y_sums"][:, :, :, :].rearrange("p n k t -> p (n k t)")[:, start:start + width]


def chunks_memory(mem):
    return borrowed(mem, 0, 2 * CW).rearrange("p (b c) -> p b c", b=2), borrowed(mem, 2 * CW, KD * NR0)


def experts_memory(mem):
    return borrowed(mem, 0, 2 * KD * H1).rearrange("p (b c) -> p b c", b=2), borrowed(mem, 2 * KD * H1, KD * E1)


class NormStage:

    def __init__(self, nc, ctx, mem, name, last=False):
        self.mem, self.last, self.count = mem, last, 0
        sb = lambda n, shape: ctx.enter_context(nc.sbuf_tensor(f"{n}_{name}", shape, F32))
        sem = lambda n: mem["semaphore"](f"{n}_{name}")
        self.stats, self.mv = sb("stats", [P, 2, 6]), sb("mv", [P, NT, 2])
        self.std, self.rstd = sb("std", [P, NT]), sb("rstd", [P, NT])
        self.step, self.std_ready, self.rstd_ready = sem("stat_step"), sem("std_ready"), sem("rstd_ready")
        self.normed, self.turned, self.high, self.low = sem("normed"), sem("x_turned"), sem("xt_high"), sem("xt_low")

    def bank(self, n):
        return self.mem["ps"][:, (4 + n) * HALF:(5 + n) * HALF]

    def statistics(self, dve, t):
        self.count = norm_statistics(dve, self.stats, self.mv, self.mem["x"][:, t, :], t, self.step, self.count)

    def scalar(self, act):
        act.wait_ge(self.step, 2 * NT)
        act.activation(self.std[:, :], self.mv[:, :, 1], ACT.Sqrt, bias=self.mem["eps"][:, :]).then_inc(self.std_ready, 1)
        if not self.last:
            for n in range(4):
                k, g = n % 2, n // 2
                act.wait_ge(self.turned, n + 1)
                act.activation(self.mem["xt_h"][:, k, g * HALF:(g + 1) * HALF], self.bank(n), ACT.Copy).then_inc(self.high, 1)

    def tensor(self, pe):
        for n in range(4):
            k, g = n % 2, n // 2
            pe.wait_ge(self.normed, 4 * (g + 1))
            for t in range(4):
                mm = pe.transpose(self.bank(n)[:, t * P:(t + 1) * P], self.mem["x"][:, 4 * g + t, k * P:(k + 1) * P],
                                  self.mem["consts"][:, C_ID:C_ID + P])
            mm.then_inc(self.turned, 1)

    def vector(self, dve):
        x = self.mem["x"]
        dve.wait_ge(self.std_ready, 1)
        dve.reciprocal(self.rstd[:, :], self.std[:, :]).then_inc(self.rstd_ready, 1)
        dve.wait_ge(self.rstd_ready, 1)
        for t in range(NT):
            dve.tensor_scalar(x[:, t, :], x[:, t, :], self.mv[:, t, 0:1], self.rstd[:, t:t + 1],
                              ALU.subtract, ALU.mult).then_inc(self.normed, 1)
        if not self.last:
            for n in range(4):
                k, g = n % 2, n // 2
                dve.wait_ge(self.high, n + 1)
                xh = self.mem["xt_h"][:, k, g * HALF:(g + 1) * HALF]
                dve.tensor_tensor(self.mem["xt_l"][:, k, g * HALF:(g + 1) * HALF], self.bank(n), xh.bitcast(F32),
                                  ALU.subtract).then_inc(self.low, 1)


class Router:

    def __init__(self, nc, ctx, mem, name, columns, turned_bank, out, by_expert):
        self.mem, self.e, self.out, self.by_expert = mem, columns, out, by_expert
        self.rows = [mem["ps"][0:columns, (turned_bank + n) * HALF:(turned_bank + n + 1) * HALF] for n in range(2)]
        sb = lambda n, shape, dt=F32: ctx.enter_context(nc.sbuf_tensor(f"{n}_{name}", shape, dt))
        sem = lambda n: mem["semaphore"](f"{n}_{name}")
        self.high, self.low = sb("r_h", [P, KD * columns], F32R), sb("r_l", [P, KD * columns], F32R)
        self.high_ready, self.low_ready = sem("r_high"), sem("r_low")
        self.product_ready, self.product_out, self.logits_ready = sem("r_product"), sem("r_product_out"), sem("logits_ready")

    def products(self, pe):
        pe.wait_ge(self.low_ready, 1)
        for n in range(2):
            cols = slice(n * HALF, (n + 1) * HALF)
            for k in range(KD):
                r = slice(k * self.e, (k + 1) * self.e)
                mm = product(pe, self.rows[n], (self.high[:, r], self.low[:, r]),
                             (self.mem["xt_h"][:, k, cols], self.mem["xt_l"][:, k, cols]), k == 0, k == KD - 1)
            mm.then_inc(self.product_ready, 1)

    def turn(self, pe):
        for t in range(NT):
            if t % 4 == 0:
                pe.wait_ge(self.product_out, t // 4 + 1)
            mm = pe.transpose(self.out[:, t * self.e:(t + 1) * self.e], self.by_expert[:, t * P:(t + 1) * P],
                              self.mem["consts"][0:self.e, C_ID:C_ID + self.e])
        mm.then_inc(self.logits_ready, 1)

    def vector(self, dve, raw):
        dve.wait_ge(self.high_ready, 1)
        dve.tensor_tensor(self.low[:, :], raw, self.high[:, :].bitcast(F32), ALU.subtract).then_inc(self.low_ready, 1)

    def vector_copy(self, dve):
        for n in range(2):
            dve.wait_ge(self.product_ready, n + 1)
            dve.tensor_copy(self.by_expert[:, n * HALF:(n + 1) * HALF], self.rows[n]).then_inc(self.product_out, 1)


class TopTwo:

    def __init__(self, nc, ctx, mem, name, experts, tri):
        self.mem, self.e, self.tri = mem, experts, tri
        sb = lambda n, shape: ctx.enter_context(nc.sbuf_tensor(f"{n}_{name}", shape, F32))
        sem = lambda n: mem["semaphore"](f"{n}_{name}")
        e = experts
        self.logits = sb("logits", [P, NT, e])
        self.above, self.equal = sb("above", [P, NT, e * e]), sb("equal", [P, NT, e * e])
        self.chosen, self.shifted, self.expd = sb("chosen", [P, NT, e]), sb("shifted", [P, NT, e]), sb("expd", [P, NT, e])
        self.top, self.total, self.inv = sb("top", [P, NT]), sb("total", [P, NT]), sb("inv", [P, NT])
        self.weights = sb("weights", [P, NT, e])
        self.step, self.shift_ready, self.exp_ready, self.done = sem("route_step"), sem("shift_ready"), sem("rexp_ready"), sem("routed")

    def scalar(self, act):
        act.wait_ge(self.shift_ready, 1)
        act.activation(self.expd[:, :, :], self.shifted[:, :, :], ACT.Exp).then_inc(self.exp_ready, 1)

    def vector(self, dve):
        e, step = self.e, self.step
        flat = lambda a: a[:, :, :].rearrange("p t (e j) -> p t e j", j=e)
        mine = self.logits[:, :, :].unsqueeze(3).broadcast_to([P, NT, e, e])
        other = self.logits[:, :, :].unsqueeze(2).broadcast_to([P, NT, e, e])
        tri = self.mem["consts"][:, self.tri:self.tri + e * e].unsqueeze(1).broadcast_to([P, NT, e * e])
        wide = lambda a: a[:, :].unsqueeze(2).broadcast_to([P, NT, e])
        dve.tensor_reduce(self.top[:, :], self.logits[:, :, :], AX.X, ALU.max).then_inc(step, 1)
        dve.tensor_tensor(flat(self.above), other, mine, ALU.is_gt).then_inc(step, 1)
        dve.tensor_tensor(flat(self.equal), other, mine, ALU.is_equal).then_inc(step, 1)
        dve.wait_ge(step, 1)
        dve.tensor_tensor(self.shifted[:, :, :], self.logits[:, :, :], wide(self.top), ALU.subtract).then_inc(self.shift_ready, 1)
        dve.wait_ge(step, 3)
        dve.tensor_tensor(self.equal[:, :, :], self.equal[:, :, :], tri, ALU.mult).then_inc(step, 1)
        dve.wait_ge(step, 4)
        dve.tensor_tensor(self.above[:, :, :], self.above[:, :, :], self.equal[:, :, :], ALU.add).then_inc(step, 1)
        dve.wait_ge(step, 5)
        dve.tensor_reduce(self.chosen[:, :, :], flat(self.above), AX.X, ALU.add).then_inc(step, 1)
        dve.wait_ge(step, 6)
        dve.tensor_scalar(self.chosen[:, :, :], self.chosen[:, :, :], 2.0, None, ALU.is_lt).then_inc(step, 1)
        dve.wait_ge(step, 7)
        dve.wait_ge(self.exp_ready, 1)
        dve.tensor_tensor(self.expd[:, :, :], self.expd[:, :, :], self.chosen[:, :, :], ALU.mult).then_inc(step, 1)
        dve.wait_ge(step, 8)
        dve.tensor_reduce(self.total[:, :], self.expd[:, :, :], AX.X, ALU.add).then_inc(step, 1)
        dve.wait_ge(step, 9)
        dve.reciprocal(self.inv[:, :], self.total[:, :]).then_inc(step, 1)
        dve.wait_ge(step, 10)
        dve.tensor_tensor(self.weights[:, :, :], self.expd[:, :, :], wide(self.inv), ALU.mult).then_inc(self.done, 1)


def mixture_0(nc, mem, dram):
    ps, x, xt = mem["ps"], mem["x"], (mem["xt_h"], mem["xt_l"])
    with ExitStack() as ctx:
        sem = lambda name: mem["semaphore"](f"{name}_m0")
        sb = lambda name, shape, dt=F32: ctx.enter_context(nc.sbuf_tensor(f"{name}_m0", shape, dt))
        raw, r_raw = chunks_memory(mem)
        w_next = borrowed(mem, 2 * CW + KD * NR0, 6 * KD * D).rearrange("p (w c) -> p w c", w=6)
        w_h, w_l = sb("w_chunk_h", [P, 2, CW], F32R), sb("w_chunk_l", [P, 2, CW], F32R)
        gated = sb("gated", [P, 2, HALF])
        hidden = sb("hidden", [P, 2, HALF])
        h_h, h_l = sb("h_h", [P, 2, T], F32R), sb("h_l", [P, 2, T], F32R)
        share = sb("share", [P, NT, CH])
        gate = sb("gate", [P, NT])
        *loaded, r_loaded = mem["first_in"]
        up_high, up_low, dn_high, dn_low = sem("up_high"), sem("up_low"), sem("dn_high"), sem("dn_low")
        UPW, DNW = slice(0, 2 * KD * I0), slice(2 * KD * I0, CW)
        copied, gate_exp, gate_step, shared_ready = sem("copied"), sem("gate_exp"), sem("gate_step"), sem("shared_ready")
        up_ready, silu_ready, hidden_ready, hh_ready, hl_ready = sem("up_ready"), sem("silu_ready"), sem("hidden_ready"), sem("hh_ready"), sem("hl_ready")
        down_ready, added = sem("down_ready"), sem("added")
        next_in, next_high, next_low = sem("next_in"), sem("next_high"), sem("next_low")
        router = Router(nc, ctx, mem, "m0", NR0, 4, ps[:, 6 * HALF:6 * HALF + NT * NR0], sb("by_expert", [NR0, T]))
        top = TopTwo(nc, ctx, mem, "m0", E0, C_T8)
        norm = NormStage(nc, ctx, mem, "m0")
        block = ctx.enter_context(nc.Block())

        G, U = 0, 2

        def bank(b):
            return ps[:, b * HALF:(b + 1) * HALF]

        def down_bank(t):
            return ps[:, (4 + t // 2) * HALF + (t % 2) * D:(4 + t // 2) * HALF + (t % 2 + 1) * D]

        @block.sync
        def _(sp):
            sp.dma_start(w_next[:, :, :], dram["w_attn"][:, 4:10, :]).then_inc(next_in, 16)
            with sp.Fori(0, CH // 2 - 1) as i:
                for b in range(2):
                    sp.wait_ge(dn_low, i * 2 + (b + 1))
                    sp.dma_start(raw[:, b, :], dram["w_chunks0"][bass.ds(i * 2 + (b + 2), 1), :, :]
                                 .rearrange("c p n -> (c p) n")).then_inc(loaded[b], 16)

        @block.gpsimd
        def _(pool):
            def low(c, b, w, high, done):
                pool.wait_ge(high, c + 1)
                pool.tensor_tensor(w_l[:, b, w], raw[:, b, w], w_h[:, b, w].bitcast(F32), ALU.subtract).then_inc(done, 1)

            low(0, 0, UPW, up_high, up_low)
            with pool.Fori(0, CH // 2 - 1) as i:
                for b in range(2):
                    low(i * 2 + (b + 1), 1 - b, UPW, up_high, up_low)
                    low(i * 2 + b, b, DNW, dn_high, dn_low)
            low(CH - 1, 1, UPW, up_high, up_low)
            low(CH - 2, 0, DNW, dn_high, dn_low)
            low(CH - 1, 1, DNW, dn_high, dn_low)
            pool.wait_ge(next_high, 1)
            pool.tensor_tensor(mem["wa_l"][:, 4:10, :], w_next[:, :, :], mem["wa_h"][:, 4:10, :].bitcast(F32), ALU.subtract
                               ).then_inc(next_low, 1)

        @block.tensor
        def _(pe):
            def up(c, b):
                pe.wait_ge(up_low, c + 1)
                for n in range(2):
                    pe.wait_ge(hidden_ready, c * 2 + (n + 1))
                    cols = slice(n * HALF, (n + 1) * HALF)
                    for base, off in ((G, 0), (U, KD * I0)):
                        for k in range(KD):
                            w = slice(off + k * I0, off + (k + 1) * I0)
                            mm = product(pe, bank(base + n), (w_h[:, b, w], w_l[:, b, w]),
                                         (xt[0][:, k, cols], xt[1][:, k, cols]), k == 0, k == KD - 1)
                    mm.then_inc(up_ready, 1)

            def down(c, b):
                pe.wait_ge(hl_ready, c * 2 + 2)
                pe.wait_ge(dn_low, c + 1)
                pe.wait_ge(added, c * NT + NT)
                w = slice(2 * KD * I0, CW)
                for t in range(NT):
                    toks = slice(t * P, (t + 1) * P)
                    mm = product(pe, down_bank(t), (h_h[:, b, toks], h_l[:, b, toks]), (w_h[:, b, w], w_l[:, b, w]),
                                 True, True)
                    mm.then_inc(down_ready, 1)

            router.products(pe)
            up(0, 0)
            router.turn(pe)
            with pe.Fori(0, CH // 2 - 1) as i:
                for b in range(2):
                    up(i * 2 + (b + 1), 1 - b)
                    down(i * 2 + b, b)
            up(CH - 1, 1)
            down(CH - 2, 0)
            down(CH - 1, 1)
            norm.tensor(pe)

        @block.scalar
        def _(act):
            def split_up(c, b, loads):
                act.wait_ge(loaded[b], 16 * loads)
                act.activation(w_h[:, b, UPW], raw[:, b, UPW], ACT.Copy).then_inc(up_high, 1)

            def split_down(c, b):
                act.activation(w_h[:, b, DNW], raw[:, b, DNW], ACT.Copy).then_inc(dn_high, 1)

            def silu(c, b):
                for n in range(2):
                    act.wait_ge(up_ready, c * 2 + (n + 1))
                    act.wait_ge(hidden_ready, c * 2 + (n + 1))
                    act.activation(gated[:, n, :], bank(G + n), ACT.Silu).then_inc(silu_ready, 1)
                    act.wait_ge(hidden_ready, c * 2 + (n + 3))
                    act.activation(h_h[:, b, n * HALF:(n + 1) * HALF], hidden[:, n, :], ACT.Copy).then_inc(hh_ready, 1)

            act.wait_ge(r_loaded, 16)
            act.activation(router.high[:, :], r_raw[:, :], ACT.Copy).then_inc(router.high_ready, 1)
            split_up(0, 0, 1)
            split_down(0, 0)
            split_up(1, 1, 1)
            silu(0, 0)
            top.scalar(act)
            act.wait_ge(copied, 2)
            act.activation(gate[:, :], gate[:, :], ACT.Exp, scale=-1.0).then_inc(gate_exp, 1)
            act.wait_ge(up_ready, 2)
            split_up(2, 0, 2)
            split_down(1, 1)
            silu(1, 1)
            with act.Fori(1, CH // 2 - 1) as i:
                for b in range(2):
                    act.wait_ge(up_ready, i * 4 + 2 * b)
                    split_up(i * 2 + (b + 1), 1 - b, i + (1 + b))
                    act.wait_ge(down_ready, i * (2 * NT) + (b - 1) * NT)
                    split_down(i * 2 + b, b)
                    silu(i * 2 + b, b)
            act.wait_ge(up_ready, 2 * CH - 4)
            split_up(CH - 1, 1, CH // 2)
            act.wait_ge(down_ready, (CH - 3) * NT)
            split_down(CH - 2, 0)
            silu(CH - 2, 0)
            act.wait_ge(down_ready, (CH - 2) * NT)
            split_down(CH - 1, 1)
            silu(CH - 1, 1)
            act.wait_ge(next_in, 16)
            act.activation(mem["wa_h"][:, 4:10, :], w_next[:, :, :], ACT.Copy).then_inc(next_high, 1)
            norm.scalar(act)

        @block.vector
        def _(dve):
            def multiply(c, b):
                for n in range(2):
                    dve.wait_ge(silu_ready, c * 2 + (n + 1))
                    dve.tensor_tensor(hidden[:, n, :], gated[:, n, :], bank(U + n), ALU.mult).then_inc(hidden_ready, 1)
                    dve.wait_ge(hh_ready, c * 2 + (n + 1))
                    cols = slice(n * HALF, (n + 1) * HALF)
                    dve.tensor_tensor(h_l[:, b, cols], hidden[:, n, :], h_h[:, b, cols].bitcast(F32), ALU.subtract
                                      ).then_inc(hl_ready, 1)

            def add_up(c, b):
                for t in range(NT):
                    dve.wait_ge(down_ready, c * NT + (t // 2 * 2 + 2))
                    dve.wait_ge(added, c * NT + (t + 1))
                    dve.scalar_tensor_tensor(out=x[:, t, :], in0=down_bank(t), scalar=share[:, t, bass.ds(c, 1)],
                                             in1=x[:, t, :], op0=ALU.mult, op1=ALU.add).then_inc(added, 1)

            router.vector(dve, r_raw[:, :])
            dve.memset(hidden[:, 0, 0:1], 0.0).then_inc(hidden_ready, 2)
            dve.memset(hidden[:, 1, 0:1], 0.0).then_inc(copied, 1)
            router.vector_copy(dve)
            dve.wait_ge(hidden_ready, 2)
            multiply(0, 0)
            dve.wait_ge(router.logits_ready, 1)
            logits = router.out.rearrange("p (t e) -> p t e", e=NR0)
            dve.tensor_copy(gate[:, :], logits[:, :, E0]).then_inc(copied, 1)
            dve.tensor_copy(top.logits[:, :, :], logits[:, :, 0:E0]).then_inc(copied, 1)
            dve.wait_ge(copied, 3)
            dve.memset(share[:, :, :], 0.0).then_inc(added, NT)
            top.vector(dve)
            dve.wait_ge(gate_exp, 1)
            dve.tensor_scalar(gate[:, :], gate[:, :], 1.0, None, ALU.add).then_inc(gate_step, 1)
            dve.wait_ge(gate_step, 1)
            dve.reciprocal(gate[:, :], gate[:, :]).then_inc(gate_step, 1)
            dve.wait_ge(gate_step, 2)
            dve.wait_ge(added, NT)
            dve.wait_ge(top.done, 1)
            dve.tensor_copy(share[:, :, 0:E0], top.weights[:, :, :]).then_inc(shared_ready, 1)
            dve.tensor_copy(share[:, :, E0:CH], gate[:, :].unsqueeze(2).broadcast_to([P, NT, CH - E0])).then_inc(shared_ready, 1)
            dve.wait_ge(shared_ready, 2)
            with dve.Fori(0, CH // 2 - 1) as i:
                for b in range(2):
                    multiply(i * 2 + (b + 1), 1 - b)
                    add_up(i * 2 + b, b)
            multiply(CH - 1, 1)
            add_up(CH - 2, 0)
            add_up(CH - 1, 1)
            dve.wait_ge(added, NT * (CH + 1))
            for t in range(NT):
                norm.statistics(dve, t)
            norm.vector(dve)


def mixture_1(nc, mem, dram):
    ps, x, consts = mem["ps"], mem["x"], mem["consts"]
    xt = (mem["xt_h"], mem["xt_l"])
    ST = CAP // P
    C1, C2 = 4, 6
    with ExitStack() as ctx:
        sem = lambda name: mem["semaphore"](f"{name}_m1")
        sb = lambda name, shape, dt=F32: ctx.enter_context(nc.sbuf_tensor(f"{name}_m1", shape, dt))
        raw, r_raw = experts_memory(mem)
        w_h, w_l = sb("w_h", [P, 3, KD * H1], F32R), sb("w_l", [P, 3, KD * H1], F32R)
        x_h, x_l = sb("x_h", [P, NT, D], F32R), sb("x_l", [P, NT, D], F32R)
        score = sb("score", [P, NT, E1])
        s_h, s_l = sb("s_h", [P, NT, E1], F32R), sb("s_l", [P, NT, E1], F32R)
        w_parts = sb("w_parts", [P, NT, E1, 2], F32R)
        ident = sb("ident", [P, P], F32R)
        score_row = sb("score_row", [P, T])
        ties = sb("ties", [P, P])
        before = sb("before", [P, NT, T], BF16)
        ones = sb("ones", [P, P], BF16)
        rank = sb("rank", [P, NT])
        rank_row = sb("rank_row", [P, T])
        one_hot = sb("one_hot", [P, NT, CAP], F32R)
        one_hot_t = sb("one_hot_t", [P, E1, ST, T], F32R)
        xg_h, xg_l = sb("xg_h", [P, KD, CAP], F32R), sb("xg_l", [P, KD, CAP], F32R)
        gelu = borrowed(mem, 2 * KD * H1 + KD * E1, 4 * CAP).rearrange("p (b c) -> p b c", b=2)
        g_h, g_l = sb("g_h", [P, MT1 * CAP], F32R), sb("g_l", [P, MT1 * CAP], F32R)
        p_parts, p_slot = sb("p_parts", [P, ST, 2]), sb("p_slot", [P, 2, ST])
        scaled = sb("scaled", [P, ST, D])
        y_parts = [mem[n][:, :, :].rearrange("p k (a s d) -> p (k a) s d", s=ST, d=D) for n in ("xt_h", "xt_l")]

        w1_in, w2_in, r_in = mem["first_in"]
        xh_ready, xl_ready = sem("xh_ready"), sem("xl_ready")
        preset, logits_out = sem("preset"), sem("logits_out")
        score_step, parts_ready = sem("score_step"), sem("parts_ready")
        row_ready, row_out, tie_step, before_ready = sem("row_ready"), sem("row_out"), sem("tie_step"), sem("before_ready")
        rank_ready, rank_out, rank_row_out = sem("rank_ready"), sem("rank_out"), sem("rank_row_out")
        hot_ready, hot_t_ready = sem("hot_ready"), sem("hot_t_ready")
        gathered, xgh_ready, xgl_ready = sem("gathered"), sem("xgh_ready"), sem("xgl_ready")
        p_ready, p_out, p_step = sem("p_ready"), sem("p_out"), sem("p_step")
        w_high, w_low = sem("w_high"), sem("w_low")
        up_ready, gelu_ready, gh_ready, gl_ready = sem("up_ready"), sem("gelu_ready"), sem("gh_ready"), sem("gl_ready")
        down_ready, scaled_ready, yh_ready, yl_ready = sem("down_ready"), sem("scaled_ready"), sem("yh_ready"), sem("yl_ready")
        back_ready, added, stored = sem("back_ready"), sem("added"), sem("stored")
        router = Router(nc, ctx, mem, "m1", E1, 2, ps[:, 0:NT * E1], score_row[0:E1, :])
        top = TopTwo(nc, ctx, mem, "m1", E1, C_T4)
        norm = NormStage(nc, ctx, mem, "m1", last=True)
        block = ctx.enter_context(nc.Block())

        def bank(b, a=0, n=HALF):
            return ps[:, b * HALF + a:b * HALF + a + n]

        LOGITS, ROW, DOWN, RANKS, XG, SMALL, UP = 0, 0, 1, 2, 4, 5, 6
        NQ = MT1 // 2

        @block.sync
        def _(sp):
            for e in range(1, E1):
                for n, done in ((0, w1_in), (1, w2_in)):
                    sp.wait_ge(w_low, 2 * (e - 1) + n + 1)
                    sp.dma_start(raw[:, n, :], dram["w_experts1"][e, n]).then_inc(done, 16)
            out = dram["out"].rearrange("(t p) d -> p t d", p=P)
            for t in range(0, NT, 2):
                sp.wait_ge(norm.normed, t + 2)
                sp.dma_start(out[:, t:t + 2, :], x[:, t:t + 2, :]).then_inc(stored, 16)
            sp.wait_ge(stored, 16 * (NT // 2))

        @block.gpsimd
        def _(pool):
            for e in range(E1):
                for n in range(2):
                    pool.wait_ge(w_high, 2 * e + n + 1)
                    at = 2 if n else e % 2
                    pool.tensor_tensor(w_l[:, at, :], raw[:, n, :], w_h[:, at, :].bitcast(F32), ALU.subtract
                                       ).then_inc(w_low, 1)

        @block.scalar
        def _(act):
            def split_weights(e, n):
                act.wait_ge((w1_in, w2_in)[n], 16 * (e + 1))
                act.activation(w_h[:, 2 if n else e % 2, :], raw[:, n, :], ACT.Copy).then_inc(w_high, 1)

            def copy_row(e):
                for n in range(2):
                    act.wait_ge(row_ready, 2 * e + n + 1)
                    act.wait_ge(before_ready, NT * e)
                    act.activation(score_row[:, n * HALF:(n + 1) * HALF], bank(ROW), ACT.Copy).then_inc(row_out, 1)

            act.wait_ge(r_in, 16)
            act.activation(router.high[:, :], r_raw[:, :], ACT.Copy).then_inc(router.high_ready, 1)
            act.activation(x_h[:, :, :], x[:, :, :], ACT.Copy).then_inc(xh_ready, 1)
            act.activation(ident[:, :], consts[:, C_ID:C_ID + P], ACT.Copy).then_inc(preset, 1)
            top.scalar(act)
            copy_row(0)
            split_weights(0, 0)
            split_weights(0, 1)

            def front(e):
                for n in range(2):
                    act.wait_ge(rank_ready, 2 * e + 2)
                    if e:
                        act.wait_ge(hot_t_ready, 2 * e)
                    act.activation(rank_row[:, n * HALF:(n + 1) * HALF], bank(RANKS + n), ACT.Copy).then_inc(rank_row_out, 1)
                if e + 1 < E1:
                    copy_row(e + 1)
                act.wait_ge(gathered, e + 1)
                act.activation(xg_h[:, :, :], bank(XG).rearrange("p (k s) -> p k s", k=KD), ACT.Copy).then_inc(xgh_ready, 1)

            front(0)
            for e in range(E1):
                for q in range(NQ):
                    n = NQ * e + q
                    act.wait_ge(up_ready, n + 1)
                    if n >= 2:
                        act.wait_ge(gl_ready, n - 1)
                    act.activation(gelu[:, q % 2, :], bank(UP + q % 2), ACT.Gelu).then_inc(gelu_ready, 1)
                    act.wait_ge(gelu_ready, n + 1)
                    if e:
                        act.wait_ge(down_ready, e)
                    act.activation(g_h[:, q * HALF:(q + 1) * HALF], gelu[:, q % 2, :], ACT.Copy).then_inc(gh_ready, 1)
                if e + 1 < E1:
                    split_weights(e + 1, 0)
                    front(e + 1)
                act.wait_ge(scaled_ready, e + 1)
                act.activation(y_parts[0][:, e, :, :], scaled[:, :, :], ACT.Copy).then_inc(yh_ready, 1)
                if e + 1 < E1:
                    split_weights(e + 1, 1)
            norm.scalar(act)

        @block.tensor
        def _(pe):
            router.products(pe)
            router.turn(pe)

            def row(e):
                for n in range(2):
                    if e or n:
                        pe.wait_ge(row_out, 2 * e + n)
                    for t in range(4 * n, 4 * n + 4):
                        for part, s in enumerate((s_h, s_l)):
                            mm = pe.matmul(bank(ROW, (t % 4) * P, P), s[:, t, e:e + 1].broadcast_to([P, P]), ident[:, :],
                                           start=part == 0, stop=part == 1, skip_group_check=True)
                    mm.then_inc(row_ready, 1)

            pe.wait_ge(parts_ready, 3)
            pe.wait_ge(preset, 2)
            def front(e):
                for a in range(NT):
                    pe.wait_ge(before_ready, NT * e + a + 1)
                    if a == 0 and e:
                        pe.wait_ge(rank_row_out, 2 * e)
                        pe.wait_ge(p_out, e)
                    for t in range(NT):
                        mm = pe.matmul(bank(SMALL, t, 1), before[:, a, t * P:(t + 1) * P], ones[:, 0:1],
                                       start=(a == 0 and t == 0), stop=a == NT - 1, skip_group_check=True)
                    if a == NT - 1:
                        mm.then_inc(rank_ready, 1)
                    for n in range(2):
                        mm = pe.matmul(bank(RANKS + n), ones[:, :], before[:, a, n * HALF:(n + 1) * HALF],
                                       start=a == 0, stop=a == NT - 1)
                mm.then_inc(rank_ready, 1)
                if e + 1 < E1:
                    row(e + 1)
                if e:
                    pe.wait_ge(xgl_ready, e)
                for k in range(KD):
                    for t in range(NT):
                        if k == 0:
                            pe.wait_ge(hot_ready, NT * e + t + 1)
                        for part, xp in enumerate((x_h, x_l)):
                            mm = pe.matmul(bank(XG, k * CAP, CAP), xp[:, t, k * P:(k + 1) * P], one_hot[:, t, :],
                                           start=(t == 0 and part == 0), stop=(t == NT - 1 and part == 1),
                                           skip_group_check=True)
                mm.then_inc(gathered, 1)
                for s in range(ST):
                    for t in range(NT):
                        mm = pe.matmul(bank(SMALL, 16 + 2 * s, 2), one_hot[:, t, s * P:(s + 1) * P],
                                       w_parts[:, t, e, :], start=t == 0, stop=t == NT - 1, skip_group_check=True)
                mm.then_inc(p_ready, 1)

            row(0)
            front(0)
            for e in range(E1):
                pe.wait_ge(xgl_ready, e + 1)
                pe.wait_ge(w_low, 2 * e + 1)
                for q in range(NQ):
                    n = NQ * e + q
                    if n >= 2:
                        pe.wait_ge(gelu_ready, n - 1)
                    for half in range(2):
                        for k in range(KD):
                            w = slice(k * H1 + (2 * q + half) * P, k * H1 + (2 * q + half + 1) * P)
                            mm = product(pe, bank(UP + q % 2, half * CAP, CAP), (w_h[:, e % 2, w], w_l[:, e % 2, w]),
                                         (xg_h[:, k, :], xg_l[:, k, :]), k == 0, k == KD - 1)
                    mm.then_inc(up_ready, 1)
                if e + 1 < E1:
                    front(e + 1)
                pe.wait_ge(w_low, 2 * e + 2)
                if e:
                    pe.wait_ge(scaled_ready, e)
                for s in range(ST):
                    for m in range(MT1):
                        if s == 0 and m % 2 == 0:
                            pe.wait_ge(gl_ready, NQ * e + m // 2 + 1)
                        g, w = slice(m * CAP + s * P, m * CAP + (s + 1) * P), slice(m * D, (m + 1) * D)
                        mm = product(pe, bank(DOWN, s * D, D), (g_h[:, g], g_l[:, g]),
                                     (w_h[:, 2, w], w_l[:, 2, w]), m == 0, m == MT1 - 1)
                mm.then_inc(down_ready, 1)
            pe.wait_ge(yl_ready, E1)
            pe.wait_ge(hot_t_ready, 2 * E1)
            for t in range(NT):
                if t >= 2:
                    pe.wait_ge(added, t - 1)
                n = 0
                for e in range(E1):
                    for s in range(ST):
                        for y in y_parts:
                            mm = pe.matmul(bank(RANKS + t % 2, 0, D), one_hot_t[:, e, s, t * P:(t + 1) * P], y[:, e, s, :],
                                           start=n == 0, stop=n == 2 * ST * E1 - 1)
                            n += 1
                mm.then_inc(back_ready, 1)

        @block.vector
        def _(dve):
            steps = [0]

            def link(ins):
                steps[0] += 1
                ins.then_inc(score_step, 1)
                dve.wait_ge(score_step, steps[0])

            dve.memset(ones[:, :], 1.0).then_inc(preset, 1)
            router.vector(dve, r_raw[:, :])
            router.vector_copy(dve)
            dve.wait_ge(router.logits_ready, 1)
            dve.tensor_tensor(top.logits[:, :, :], bank(LOGITS, 0, NT * E1).rearrange("p (t e) -> p t e", e=E1),
                              mem["bias_g"][:, :].unsqueeze(1).broadcast_to([P, NT, E1]), ALU.add).then_inc(logits_out, 1)
            dve.wait_ge(logits_out, 1)
            top.vector(dve)
            dve.wait_ge(top.done, 1)
            link(dve.scalar_tensor_tensor(out=score[:, :, :], in0=top.chosen[:, :, :], scalar=-1.0,
                                          in1=top.weights[:, :, :], op0=ALU.add, op1=ALU.add))
            link(dve.tensor_copy(s_h[:, :, :], score[:, :, :]))
            dve.tensor_tensor(s_l[:, :, :], score[:, :, :], s_h[:, :, :].bitcast(F32), ALU.subtract).then_inc(parts_ready, 1)
            link(dve.tensor_copy(w_parts[:, :, :, 0], top.weights[:, :, :]))
            dve.tensor_tensor(w_parts[:, :, :, 1], top.weights[:, :, :], w_parts[:, :, :, 0].bitcast(F32), ALU.subtract
                              ).then_inc(parts_ready, 1)
            dve.wait_ge(parts_ready, 1)
            dve.tensor_tensor(score[:, :, :], s_h[:, :, :].bitcast(F32), s_l[:, :, :].bitcast(F32), ALU.add
                              ).then_inc(parts_ready, 1)
            dve.wait_ge(parts_ready, 3)

            def compare(e, a):
                if a == 0:
                    dve.wait_ge(row_out, 2 * e + 2)
                if e:
                    dve.wait_ge(rank_ready, 2 * e)
                own, mine = slice(a * P, (a + 1) * P), score[:, a, e:e + 1]
                n = NT * e + a
                dve.wait_ge(before_ready, n)
                dve.scalar_tensor_tensor(out=ties[:, :], in0=score_row[:, own], scalar=mine, in1=consts[:, C_TRI:C_TRI + P],
                                         op0=ALU.is_equal, op1=ALU.mult).then_inc(tie_step, 1)
                if a:
                    dve.tensor_scalar(before[:, a, 0:a * P], score_row[:, 0:a * P], mine, None, ALU.is_lt)
                if a < NT - 1:
                    dve.tensor_scalar(before[:, a, (a + 1) * P:T], score_row[:, (a + 1) * P:T], mine, None, ALU.is_le)
                dve.wait_ge(tie_step, n + 1)
                dve.scalar_tensor_tensor(out=before[:, a, own], in0=score_row[:, own], scalar=mine, in1=ties[:, :],
                                         op0=ALU.is_lt, op1=ALU.add).then_inc(before_ready, 1)

            def compare_next(e, first, last):
                if e + 1 < E1:
                    for a in range(first, last):
                        compare(e + 1, a)

            def front(e):
                dve.wait_ge(rank_ready, 2 * e + 1)
                dve.tensor_copy(rank[:, :], bank(SMALL, 0, NT)).then_inc(rank_out, 1)
                dve.wait_ge(rank_out, e + 1)
                if e:
                    dve.wait_ge(p_ready, e)
                for t in range(NT):
                    dve.tensor_scalar(one_hot[:, t, :], consts[:, C_IOTA:C_IOTA + CAP], rank[:, t:t + 1], None,
                                      ALU.is_equal).then_inc(hot_ready, 1)
                dve.wait_ge(rank_row_out, 2 * e + 2)
                for s in range(ST):
                    dve.tensor_scalar(one_hot_t[:, e, s, :], rank_row[:, :], consts[:, C_SLOT + s:C_SLOT + s + 1], None,
                                      ALU.is_equal).then_inc(hot_t_ready, 1)
                compare_next(e, 0, C1)
                dve.wait_ge(xgh_ready, e + 1)
                dve.tensor_tensor(xg_l[:, :, :], bank(XG).rearrange("p (k s) -> p k s", k=KD), xg_h[:, :, :].bitcast(F32),
                                  ALU.subtract).then_inc(xgl_ready, 1)
                dve.wait_ge(p_ready, e + 1)
                if e:
                    dve.wait_ge(p_step, e)
                dve.tensor_copy(p_parts[:, :, :], bank(SMALL, 16, 2 * ST).rearrange("p (s l) -> p s l", l=2)).then_inc(p_out, 1)
                dve.wait_ge(p_out, e + 1)
                dve.tensor_reduce(p_slot[:, e % 2, :], p_parts[:, :, :], AX.X, ALU.add).then_inc(p_step, 1)

            dve.wait_ge(xh_ready, 1)
            dve.tensor_tensor(x_l[:, :, :], x[:, :, :], x_h[:, :, :].bitcast(F32), ALU.subtract).then_inc(xl_ready, 1)
            for a in range(NT):
                compare(0, a)
            front(0)
            for e in range(E1):
                if e == 0:
                    compare_next(0, C1, NT)
                for q in range(NQ):
                    n = NQ * e + q
                    dve.wait_ge(gh_ready, n + 1)
                    cols = slice(q * HALF, (q + 1) * HALF)
                    dve.tensor_tensor(g_l[:, cols], gelu[:, q % 2, :], g_h[:, cols].bitcast(F32), ALU.subtract
                                      ).then_inc(gl_ready, 1)
                if e + 1 < E1:
                    front(e + 1)
                    compare_next(e + 1, C1, C2)
                dve.wait_ge(down_ready, e + 1)
                dve.wait_ge(p_step, e + 1)
                dve.tensor_tensor(scaled[:, :, :], bank(DOWN).rearrange("p (s d) -> p s d", s=ST),
                                  p_slot[:, e % 2, :].unsqueeze(2).broadcast_to([P, ST, D]), ALU.mult).then_inc(scaled_ready, 1)
                dve.wait_ge(yh_ready, e + 1)
                dve.tensor_tensor(y_parts[1][:, e, :, :], scaled[:, :, :], y_parts[0][:, e, :, :].bitcast(F32), ALU.subtract
                                  ).then_inc(yl_ready, 1)
                if e + 1 < E1:
                    compare_next(e + 1, C2, NT)
            for t in range(NT):
                dve.wait_ge(back_ready, t + 1)
                dve.tensor_tensor(x[:, t, :], bank(RANKS + t % 2, 0, D), x[:, t, :], ALU.add).then_inc(added, 1)
                dve.wait_ge(added, t + 1)
                norm.statistics(dve, t)
            norm.vector(dve)


def program(nc, dram):
    dram = dict(dram)
    for t in "qk":
        dram[f"{t}_parts"] = nc.dram_tensor(f"{t}_parts", (D, 2, T), F32, kind="Internal").ap()
    dram["sums"] = [nc.dram_tensor(name, (D, T), F32, kind="Internal").ap() for name in ("y_high_sums", "y_low_sums", "exp_sums")]
    with ExitStack() as ctx:
        def sb(c, name, shape, dt=F32):
            return c.enter_context(nc.sbuf_tensor(name, shape, dt))

        mem = {
            "ps": ctx.enter_context(nc.psum_tensor("ps", [P, 8 * HALF], F32)),
            "x": sb(ctx, "x", [P, NT, D]),
            "xt_h": sb(ctx, "xt_h", [P, KD, T], F32R),
            "xt_l": sb(ctx, "xt_l", [P, KD, T], F32R),
            "y_sums": sb(ctx, "y_sums", [P, 3, KD, T]),
            "consts": sb(ctx, "consts", [P, C_END]),
            "eps": sb(ctx, "eps", [P, 1]),
            "bias_g": sb(ctx, "bias_g", [P, E1]),
        }
        with ExitStack() as heads:
            mem |= {
                "masks": sb(heads, "masks", [P, C_T8], BF16),
                "bias_qk": sb(heads, "bias_qk", [P, 4]),
                "bias_v": sb(heads, "bias_v", [P, D]),
                "bias_o": sb(heads, "bias_o", [P, D]),
                "wa_h": sb(heads, "wa_h", [P, 10, KD * D], F32R),
                "wa_l": sb(heads, "wa_l", [P, 10, KD * D], F32R),
                "q_stack": sb(heads, "q_stack", [STACK, 4, T], F32R),
                "k_stack": sb(heads, "k_stack", [STACK, 4, T], F32R),
                "zeros": sb(heads, "zeros", [2, T]),
                "v_plain": sb(heads, "v_plain", [P, 4, NT, HD]),
                "v_split": sb(heads, "v_split", [P, 4, NT, 3 * HD], F32R),
                "row_max": sb(heads, "row_max", [P, NT, 2]),
                "max_parts": sb(heads, "max_parts", [P, 32], F32R),
            }
            with Semaphores(nc) as mem["semaphore"]:
                load_and_split(nc, mem, dram)
                attention(nc, mem, dram, 0)
                output_projection(nc, mem, dram, 0)
                mixture_0(nc, mem, dram)
                mem["semaphore"].clear()
            last = ctx.enter_context(Semaphores(nc))
            mem["semaphore"] = last
            attention(nc, mem, dram, 1)
            output_projection(nc, mem, dram, 1)
        mixture_1(nc, mem, dram)


def contraction_first(w):
    k, n = w.shape
    return w.reshape(k // P, P, n).transpose(1, 0, 2).reshape(P, -1)


def shape_constants():
    c = np.zeros((P, C_END), np.float32)
    i = np.arange(P)
    c[:, C_ID:C_ID + P] = np.eye(P)
    c[:, C_CM:C_CM + P] = np.where(i[None, :] > i[:, None], MASKED, 0)
    c[:, C_CMT:C_CMT + P] = np.where(i[:, None] > i[None, :], MASKED, 0)
    for at, e in ((C_T8, E0), (C_T4, E1)):
        c[:, at:at + e * e] = np.tril(np.ones((e, e)), -1).reshape(-1)
    c[:, C_IOTA:C_IOTA + CAP] = np.arange(CAP)
    for s in range(CAP // P):
        c[:, C_SLOT + s] = i + s * P
    c[:, C_TRI:C_TRI + P] = i[:, None] < i[None, :]
    return c


def rope_tables():
    rot = HD // 2
    freq = (1.0 / np.float32(10000.0) ** (np.arange(0, HD, 2, dtype=np.float32) / np.float32(HD))).astype(np.float32)
    ang = (np.arange(T, dtype=np.float32)[:, None] * freq[None, :]).astype(np.float64)
    cos, sin = np.ones((HD, T)), np.zeros((HD, T))
    cos[:rot] = np.cos(ang).T
    sin[:rot] = np.sin(ang).T * np.where(np.arange(rot) < rot // 2, -1, 1)[:, None]
    return np.stack([np.tile(a, (P // HD, 1)) for a in (cos, sin)], 1).astype(np.float32)


def kernel(**inputs):
    import concourse.bacc as _bacc
    from concourse.bass_utils import run_bass_kernel_spmd as _run

    a = {k: np.asarray(v) for k, v in inputs.items()}
    cf = contraction_first
    by_head = lambda w: w.transpose(1, 0, 2).reshape(D, D)
    swap = np.arange(D).reshape(H, HD)
    swap = np.concatenate([swap[:, HD // 4:HD // 2], swap[:, :HD // 4], swap[:, HD // 2:]], 1).reshape(-1)
    x = a["L0_attn_x"].reshape(T, D)
    wq, wk = a["L1_attn_wq"], a["L1_attn_wk"]
    attn = [by_head(a["L0_attn_Wq"]), by_head(a["L0_attn_Wk"]), by_head(a["L0_attn_Wv"]), a["L0_attn_Wo"],
            wq.T, wq[swap].T, wk.T, wk[swap].T, a["L1_attn_wv"].T, a["L1_attn_wo"].T]
    router0 = np.concatenate([a["L0_ffn_w_router"], a["L0_ffn_gate_w"], np.zeros((1, D), np.float32)]).T
    gates = [*a["L0_ffn_wg"], *a["L0_ffn_sw_gate"].reshape(-1, I0, D)]
    ups = [*a["L0_ffn_wu"], *a["L0_ffn_sw_up"].reshape(-1, I0, D)]
    downs = [*a["L0_ffn_wd"], *a["L0_ffn_sw_down"].reshape(D, -1, I0).transpose(1, 0, 2)]
    arrays = {
        "x_t": x.T.reshape(KD, P, T).transpose(1, 0, 2),
        "x_tok": x.reshape(NT, P, D).transpose(1, 0, 2),
        "w_attn": np.stack([cf(w) for w in attn], 1),
        "bias_qk": np.concatenate([a["L0_attn_bq"].reshape(KD, P), a["L0_attn_bk"].reshape(KD, P)]).T,
        "bias_v": a["L0_attn_bv"].reshape(1, D),
        "bias_o": a["L0_attn_bo"].reshape(1, D),
        "bias_g": a["L1_ffn_bg"].reshape(1, E1),
        "w_router0": cf(router0),
        "w_chunks0": np.stack([np.concatenate([cf(g.T), cf(u.T), cf(d.T)], 1) for g, u, d in zip(gates, ups, downs)]),
        "w_router1": cf(a["L1_ffn_Wg"]),
        "w_experts1": np.stack([np.stack([cf(w1), cf(w2)]) for w1, w2 in zip(a["L1_ffn_W1"], a["L1_ffn_W2"])]),
        "consts": shape_constants(),
        "rope": rope_tables(),
    }
    arrays = {k: np.ascontiguousarray(v) for k, v in arrays.items()}
    nc = _bacc.Bacc("TRN2", target_bir_lowering=False, num_devices=1)
    dram = {k: nc.dram_tensor(f"in_{k}", v.shape, F32, kind="ExternalInput").ap() for k, v in arrays.items()}
    dram["out"] = nc.dram_tensor("out", (T, D), F32, kind="ExternalOutput").ap()
    program(nc, dram)
    r = _run(nc, [{f"in_{k}": v for k, v in arrays.items()}], core_ids=[0])
    return r.results[0]["out"].reshape(1, T, D)
```
